# Optimizing a Trainium2 kernel written in Bass

```python
import numpy as np
import jax
import jax.numpy as jnp

def _softmax(x, axis=-1):
    return jax.nn.softmax(x, axis=axis)

def _gelu(x):
    return jax.nn.gelu(x, approximate=True)

def _silu(x):
    return jax.nn.silu(x)

def _sigmoid(x):
    return jax.nn.sigmoid(x)

def _layernorm(x, axis=-1, eps=1e-05):
    m = jnp.mean(x, axis=axis, keepdims=True)
    v = jnp.var(x, axis=axis, keepdims=True)
    return (x - m) / jnp.sqrt(v + eps)

def _scatter_add(tgt, idx, src, axis=0):
    return tgt.at[idx].add(src)

def _segment_sum(src, seg, n):
    return jax.ops.segment_sum(src, seg, n)
kernel_name = 'mk_sandwich_d2_jaxref_r8_7757eb'

def setup_inputs(seed: int=0):
    np.random.seed(seed)
    _w = jnp.asarray

    def _L0_attn_setup():
        import jax, jax.numpy as jnp
        import numpy as np
        B, S, D = (1, 256, 512)
        H = 32
        Q_RANK, KV_RANK = (192, 64)
        NOPE, ROPE, VD = (128, 64, 128)
        QD = NOPE + ROPE
        EPS = 1e-06
        THETA = 10000.0

        def _rmsnorm(x, w):
            return x * jax.lax.rsqrt(jnp.mean(x * x, axis=-1, keepdims=True) + EPS) * w

        def _rotate_half(x):
            h = x.shape[-1] // 2
            return jnp.concatenate([-x[..., h:], x[..., :h]], axis=-1)

        def _apply_rope(x, cos, sin):
            xp = jnp.concatenate([x[..., 0::2], x[..., 1::2]], axis=-1)
            return xp * cos + _rotate_half(xp) * sin

        def _mla_forward(hidden_states, Wq_a, q_a_ln_w, Wq_b, Wkv_a, kv_a_ln_w, Wkv_b, Wo):
            b, s, _ = hidden_states.shape
            q = _rmsnorm(hidden_states @ Wq_a, q_a_ln_w) @ Wq_b
            q = q.reshape(b, s, H, QD).transpose(0, 2, 1, 3)
            q_nope, q_pe = (q[..., :NOPE], q[..., NOPE:])
            ckv = hidden_states @ Wkv_a
            compressed, k_pe = (ckv[..., :KV_RANK], ckv[..., KV_RANK:])
            kv = _rmsnorm(compressed, kv_a_ln_w) @ Wkv_b
            kv = kv.reshape(b, s, H, NOPE + VD).transpose(0, 2, 1, 3)
            k_nope, v = (kv[..., :NOPE], kv[..., NOPE:])
            k_pe = k_pe[:, None, :, :]
            inv_freq = 1.0 / THETA ** (jnp.arange(0, ROPE, 2, dtype=jnp.float32) / ROPE)
            freqs = jnp.outer(jnp.arange(s, dtype=jnp.float32), inv_freq)
            emb = jnp.concatenate([freqs, freqs], axis=-1)
            cos = jnp.cos(emb)[None, None].astype(hidden_states.dtype)
            sin = jnp.sin(emb)[None, None].astype(hidden_states.dtype)
            q_pe = _apply_rope(q_pe, cos, sin)
            k_pe = _apply_rope(k_pe, cos, sin)
            qf = jnp.concatenate([q_nope, q_pe], axis=-1)
            kf = jnp.concatenate([k_nope, jnp.broadcast_to(k_pe, (b, H, s, ROPE))], axis=-1)
            scale = QD ** (-0.5)
            scores = jnp.einsum('bhqd,bhkd->bhqk', qf, kf) * scale
            causal = jnp.tril(jnp.ones((s, s), dtype=bool))
            scores = jnp.where(causal, scores, jnp.finfo(scores.dtype).min)
            probs = jax.nn.softmax(scores, axis=-1)
            o = jnp.einsum('bhqk,bhkd->bhqd', probs, v)
            o = o.transpose(0, 2, 1, 3).reshape(b, s, H * VD)
            return o @ Wo
        key = jax.random.key(seed)
        ks = jax.random.split(key, 8)
        std = 0.02
        return {'hidden_states': jax.random.normal(ks[0], (B, S, D), jnp.float32), 'Wq_a': jax.random.normal(ks[1], (D, Q_RANK), jnp.float32) * std, 'q_a_ln_w': jnp.ones((Q_RANK,), jnp.float32), 'Wq_b': jax.random.normal(ks[2], (Q_RANK, H * QD), jnp.float32) * std, 'Wkv_a': jax.random.normal(ks[3], (D, KV_RANK + ROPE), jnp.float32) * std, 'kv_a_ln_w': jnp.ones((KV_RANK,), jnp.float32), 'Wkv_b': jax.random.normal(ks[4], (KV_RANK, H * (NOPE + VD)), jnp.float32) * std, 'Wo': jax.random.normal(ks[5], (H * VD, D), jnp.float32) * std}
    _L0_attn_in = _L0_attn_setup()

    def _L0_ffn_setup():
        import jax, jax.numpy as jnp
        import numpy as np
        B, S, H, I, R = (4, 32, 512, 1792, 4)

        def _anemll_linear(x, w, su, sv):
            w_eff = w * (su @ sv)
            return jnp.einsum('bsh,oh->bso', x, w_eff)
        key = jax.random.key(seed)
        ks = jax.random.split(key, 10)
        sd = 0.02
        return {'x': jax.random.normal(ks[0], (B, S, H), dtype=jnp.float32), 'gate_w': jax.random.normal(ks[1], (I, H), dtype=jnp.float32) * sd, 'gate_su': jax.random.normal(ks[2], (I, R), dtype=jnp.float32) * 0.5, 'gate_sv': jax.random.normal(ks[3], (R, H), dtype=jnp.float32) * 0.5, 'up_w': jax.random.normal(ks[4], (I, H), dtype=jnp.float32) * sd, 'up_su': jax.random.normal(ks[5], (I, R), dtype=jnp.float32) * 0.5, 'up_sv': jax.random.normal(ks[6], (R, H), dtype=jnp.float32) * 0.5, 'down_w': jax.random.normal(ks[7], (H, I), dtype=jnp.float32) * sd, 'down_su': jax.random.normal(ks[8], (H, R), dtype=jnp.float32) * 0.5, 'down_sv': jax.random.normal(ks[9], (R, I), dtype=jnp.float32) * 0.5}
    _L0_ffn_in = _L0_ffn_setup()

    def _L1_attn_setup():
        import jax, jax.numpy as jnp
        import numpy as np
        HEADS = 32
        key = jax.random.key(seed)
        ks = jax.random.split(key, 5)
        H = 512
        B, S = (2, 256)
        w_scale = 1.0 / np.sqrt(H)
        return {'x': jax.random.normal(ks[0], (B, S, H), dtype=jnp.float32), 'attn_qkvw': jax.random.normal(ks[1], (H, 3 * H), dtype=jnp.float32) * w_scale, 'attn_qkvb': jax.random.normal(ks[2], (3 * H,), dtype=jnp.float32) * 0.02, 'attn_ow': jax.random.normal(ks[3], (H, H), dtype=jnp.float32) * w_scale, 'attn_ob': jax.random.normal(ks[4], (H,), dtype=jnp.float32) * 0.02}
    _L1_attn_in = _L1_attn_setup()

    def _L1_ffn_setup():
        import jax, jax.numpy as jnp
        import numpy as np
        GROUP_SIZE = 32

        def dequantize(qweight, scales, zeros, dtype):
            out_f, in_f = qweight.shape
            w = qweight.astype(dtype).reshape(-1, GROUP_SIZE)
            w = (w - zeros) * scales
            return w.reshape(out_f, in_f)
        key = jax.random.key(seed)
        k1, k2, k3, k4, k5 = jax.random.split(key, 5)
        B, S, IN, OUT = (4, 256, 512, 512)
        n_groups = OUT * IN // GROUP_SIZE
        x = jax.random.normal(k1, (B, S, IN), dtype=jnp.float32)
        qweight = jax.random.randint(k2, (OUT, IN), 0, 32, dtype=jnp.int32)
        scales = jax.random.uniform(k3, (n_groups, 1), dtype=jnp.float32) * 0.01 + 0.0001
        zeros = jax.random.randint(k4, (n_groups, 1), 0, 32).astype(jnp.float32)
        bias = jax.random.normal(k5, (OUT,), dtype=jnp.float32) * 0.02
        return {'x': x, 'qweight': qweight, 'scales': scales, 'zeros': zeros, 'bias': bias}
    _L1_ffn_in = _L1_ffn_setup()
    _d = {'L0_attn_hidden_states': _L0_attn_in['hidden_states'], 'L0_attn_Wq_a': _L0_attn_in['Wq_a'], 'L0_attn_q_a_ln_w': _L0_attn_in['q_a_ln_w'], 'L0_attn_Wq_b': _L0_attn_in['Wq_b'], 'L0_attn_Wkv_a': _L0_attn_in['Wkv_a'], 'L0_attn_kv_a_ln_w': _L0_attn_in['kv_a_ln_w'], 'L0_attn_Wkv_b': _L0_attn_in['Wkv_b'], 'L0_attn_Wo': _L0_attn_in['Wo'], 'L0_ffn_gate_w': _L0_ffn_in['gate_w'], 'L0_ffn_gate_su': _L0_ffn_in['gate_su'], 'L0_ffn_gate_sv': _L0_ffn_in['gate_sv'], 'L0_ffn_up_w': _L0_ffn_in['up_w'], 'L0_ffn_up_su': _L0_ffn_in['up_su'], 'L0_ffn_up_sv': _L0_ffn_in['up_sv'], 'L0_ffn_down_w': _L0_ffn_in['down_w'], 'L0_ffn_down_su': _L0_ffn_in['down_su'], 'L0_ffn_down_sv': _L0_ffn_in['down_sv'], 'L1_attn_attn_qkvw': _L1_attn_in['attn_qkvw'], 'L1_attn_attn_qkvb': _L1_attn_in['attn_qkvb'], 'L1_attn_attn_ow': _L1_attn_in['attn_ow'], 'L1_attn_attn_ob': _L1_attn_in['attn_ob'], 'L1_ffn_qweight': _L1_ffn_in['qweight'], 'L1_ffn_scales': _L1_ffn_in['scales'], 'L1_ffn_zeros': _L1_ffn_in['zeros'], 'L1_ffn_bias': _L1_ffn_in['bias']}
    _x0 = _d['L0_attn_hidden_states']
    _d['L0_attn_hidden_states'] = jax.random.normal(jax.random.fold_in(jax.random.key(seed), 1), (1, 1024, 512), dtype=_x0.dtype)
    del _x0
    return _d

def reference(L0_attn_hidden_states, L0_attn_Wq_a, L0_attn_q_a_ln_w, L0_attn_Wq_b, L0_attn_Wkv_a, L0_attn_kv_a_ln_w, L0_attn_Wkv_b, L0_attn_Wo, L0_ffn_gate_w, L0_ffn_gate_su, L0_ffn_gate_sv, L0_ffn_up_w, L0_ffn_up_su, L0_ffn_up_sv, L0_ffn_down_w, L0_ffn_down_su, L0_ffn_down_sv, L1_attn_attn_qkvw, L1_attn_attn_qkvb, L1_attn_attn_ow, L1_attn_attn_ob, L1_ffn_qweight, L1_ffn_scales, L1_ffn_zeros, L1_ffn_bias):

    def _L0_attn_ref(hidden_states, Wq_a, q_a_ln_w, Wq_b, Wkv_a, kv_a_ln_w, Wkv_b, Wo):
        import jax, jax.numpy as jnp
        import numpy as np
        B, S, D = (1, 256, 512)
        H = 32
        Q_RANK, KV_RANK = (192, 64)
        NOPE, ROPE, VD = (128, 64, 128)
        QD = NOPE + ROPE
        EPS = 1e-06
        THETA = 10000.0

        def _rmsnorm(x, w):
            return x * jax.lax.rsqrt(jnp.mean(x * x, axis=-1, keepdims=True) + EPS) * w

        def _rotate_half(x):
            h = x.shape[-1] // 2
            return jnp.concatenate([-x[..., h:], x[..., :h]], axis=-1)

        def _apply_rope(x, cos, sin):
            xp = jnp.concatenate([x[..., 0::2], x[..., 1::2]], axis=-1)
            return xp * cos + _rotate_half(xp) * sin

        def _mla_forward(hidden_states, Wq_a, q_a_ln_w, Wq_b, Wkv_a, kv_a_ln_w, Wkv_b, Wo):
            b, s, _ = hidden_states.shape
            q = _rmsnorm(hidden_states @ Wq_a, q_a_ln_w) @ Wq_b
            q = q.reshape(b, s, H, QD).transpose(0, 2, 1, 3)
            q_nope, q_pe = (q[..., :NOPE], q[..., NOPE:])
            ckv = hidden_states @ Wkv_a
            compressed, k_pe = (ckv[..., :KV_RANK], ckv[..., KV_RANK:])
            kv = _rmsnorm(compressed, kv_a_ln_w) @ Wkv_b
            kv = kv.reshape(b, s, H, NOPE + VD).transpose(0, 2, 1, 3)
            k_nope, v = (kv[..., :NOPE], kv[..., NOPE:])
            k_pe = k_pe[:, None, :, :]
            inv_freq = 1.0 / THETA ** (jnp.arange(0, ROPE, 2, dtype=jnp.float32) / ROPE)
            freqs = jnp.outer(jnp.arange(s, dtype=jnp.float32), inv_freq)
            emb = jnp.concatenate([freqs, freqs], axis=-1)
            cos = jnp.cos(emb)[None, None].astype(hidden_states.dtype)
            sin = jnp.sin(emb)[None, None].astype(hidden_states.dtype)
            q_pe = _apply_rope(q_pe, cos, sin)
            k_pe = _apply_rope(k_pe, cos, sin)
            qf = jnp.concatenate([q_nope, q_pe], axis=-1)
            kf = jnp.concatenate([k_nope, jnp.broadcast_to(k_pe, (b, H, s, ROPE))], axis=-1)
            scale = QD ** (-0.5)
            scores = jnp.einsum('bhqd,bhkd->bhqk', qf, kf) * scale
            causal = jnp.tril(jnp.ones((s, s), dtype=bool))
            scores = jnp.where(causal, scores, jnp.finfo(scores.dtype).min)
            probs = jax.nn.softmax(scores, axis=-1)
            o = jnp.einsum('bhqk,bhkd->bhqd', probs, v)
            o = o.transpose(0, 2, 1, 3).reshape(b, s, H * VD)
            return o @ Wo
        return _mla_forward(hidden_states, Wq_a, q_a_ln_w, Wq_b, Wkv_a, kv_a_ln_w, Wkv_b, Wo)

    def _L0_ffn_ref(x, gate_w, gate_su, gate_sv, up_w, up_su, up_sv, down_w, down_su, down_sv):
        import jax, jax.numpy as jnp
        import numpy as np
        B, S, H, I, R = (4, 32, 512, 1792, 4)

        def _anemll_linear(x, w, su, sv):
            w_eff = w * (su @ sv)
            return jnp.einsum('bsh,oh->bso', x, w_eff)
        a = _anemll_linear(x, gate_w, gate_su, gate_sv)
        b = _anemll_linear(x, up_w, up_su, up_sv)
        d = jax.nn.silu(a) * b
        return _anemll_linear(d, down_w, down_su, down_sv)

    def _L1_attn_ref(x, attn_qkvw, attn_qkvb, attn_ow, attn_ob):
        import jax, jax.numpy as jnp
        import numpy as np
        HEADS = 32
        B, S, H = x.shape
        hd = H // HEADS
        scale = 1.0 / np.sqrt(hd)
        qkv = x @ attn_qkvw + attn_qkvb
        qkv = qkv.reshape(B, S, 3, HEADS, hd)
        q = jnp.transpose(qkv[:, :, 0], (0, 2, 1, 3))
        k = jnp.transpose(qkv[:, :, 1], (0, 2, 1, 3))
        v = jnp.transpose(qkv[:, :, 2], (0, 2, 1, 3))
        scores = jnp.einsum('bhqd,bhkd->bhqk', q, k) * scale
        probs = jax.nn.softmax(scores, axis=-1)
        ctx = jnp.einsum('bhqk,bhkd->bhqd', probs, v)
        ctx = jnp.transpose(ctx, (0, 2, 1, 3)).reshape(B, S, H)
        return ctx @ attn_ow + attn_ob

    def _L1_ffn_ref(x, qweight, scales, zeros, bias):
        import jax, jax.numpy as jnp
        import numpy as np
        GROUP_SIZE = 32

        def dequantize(qweight, scales, zeros, dtype):
            out_f, in_f = qweight.shape
            w = qweight.astype(dtype).reshape(-1, GROUP_SIZE)
            w = (w - zeros) * scales
            return w.reshape(out_f, in_f)
        w = dequantize(qweight, scales, zeros, x.dtype)
        return jnp.einsum('bsi,oi->bso', x, w) + bias
    x = L0_attn_hidden_states
    x = x + _layernorm(_L0_attn_ref(_layernorm(x, axis=-1), L0_attn_Wq_a, L0_attn_q_a_ln_w, L0_attn_Wq_b, L0_attn_Wkv_a, L0_attn_kv_a_ln_w, L0_attn_Wkv_b, L0_attn_Wo), axis=-1)
    x = x + _layernorm(_L0_ffn_ref(_layernorm(x, axis=-1), L0_ffn_gate_w, L0_ffn_gate_su, L0_ffn_gate_sv, L0_ffn_up_w, L0_ffn_up_su, L0_ffn_up_sv, L0_ffn_down_w, L0_ffn_down_su, L0_ffn_down_sv), axis=-1)
    x = x + _layernorm(_L1_attn_ref(_layernorm(x, axis=-1), L1_attn_attn_qkvw, L1_attn_attn_qkvb, L1_attn_attn_ow, L1_attn_attn_ob), axis=-1)
    x = x + _layernorm(_L1_ffn_ref(_layernorm(x, axis=-1), L1_ffn_qweight, L1_ffn_scales, L1_ffn_zeros, L1_ffn_bias), axis=-1)
    return x

_drawn_inputs = setup_inputs


def setup_inputs(seed=0):
    import zlib

    import numpy as np

    out = dict(_drawn_inputs(seed))
    spreads = {'L0_attn_q_a_ln_w': (1.0, 0.6), 'L0_attn_kv_a_ln_w': (1.0, 0.2)}
    factors = {'L1_ffn_bias': 8.0}
    for name, (base, spread) in spreads.items():
        noise = np.random.default_rng([zlib.crc32(name.encode()), seed]).standard_normal(out[name].shape)
        drawn = base * np.exp(spread * noise) if base else spread * noise
        out[name] = jnp.asarray(drawn.astype(out[name].dtype))
    for name, factor in factors.items():
        out[name] = (out[name] * factor).astype(out[name].dtype)
    return out
```

```python
import concourse.bass as bass
from concourse import mybir
from contextlib import ExitStack

F32 = mybir.dt.float32
F32R = mybir.dt.float32r
BF16 = mybir.dt.bfloat16
I32 = mybir.dt.int32
ALU = mybir.AluOpType
ACT = mybir.ActivationFunctionType
AX = mybir.AxisListType

P = 128
S = 1024
D = 512
NT = S // P
ND = D // P
BANK = 512
NHALF = S // BANK
LN_EPS = 1e-5

H = 32
QR, CR = 192, 64
NOPE, ROPE, VD = 128, 64, 128
PAIRS = H // 2
RMS_EPS = 1e-6
MLA_SCALE = float((NOPE + ROPE) ** -0.5)
PACK = 2 * (QR + CR + CR + D)

INNER = 1792
NI = INNER // P
RANK = 4

HD = 16
GROUPS = H // 4
MHA_SCALE = float(HD ** -0.5)

QGROUP = 32


def wait(engine, semaphore, value):
    if isinstance(value, int) and value <= 0:
        return
    engine.wait_ge(semaphore, value)


def causal_units():
    units = []
    for half in range(NHALF):
        for j in range((half + 1) * BANK // P):
            q0 = max(P * j, BANK * half)
            units.append((half, j, q0, BANK * (half + 1) - q0))
    return units


UNITS = causal_units()
NU = len(UNITS)
NU_HALF = [sum(u[0] <= h for u in UNITS) for h in range(NHALF)]


def norm_block(nc, name, x, hT, ident, project=None, y_out=None, first_waits=None, x_loads=None, out_dram=None):
    with ExitStack() as ctx:
        sem = lambda n: ctx.enter_context(nc.semaphore(f"{name}_{n}"))
        sb = lambda n, s, d=F32: ctx.enter_context(nc.sbuf_tensor(f"{name}_{n}", s, d))
        y_ready, y_used = sem("y_ready"), sem("y_used")
        var_ready, std_ready = sem("var_ready"), sem("std_ready")
        h_ready, ht_ready, ht_used = sem("h_ready"), sem("ht_ready"), sem("ht_used")
        dve_done, x_out, eps_set = sem("dve_done"), sem("x_out"), sem("eps_set")
        x_ready = sem("x_ready")
        py = [ctx.enter_context(nc.psum_tensor(f"{name}_py{i}", [P, D], F32)) for i in range(2)]
        pt = [ctx.enter_context(nc.psum_tensor(f"{name}_pt{i}", [P, ND, P], F32)) for i in range(2)]
        stats, mv = sb("stats", [P, 2, 6]), sb("mv", [P, 2, 2])
        std, rstd = sb("std", [P, 2]), sb("rstd", [P, 2])
        eps = sb("eps", [P, 1])
        yn, hn = sb("yn", [P, D]), sb("hn", [P, 2, D])
        block = ctx.enter_context(nc.Block())
        norms = (project is not None) + (hT is not None)

        @block.tensor
        def _(pe):
            def transposes(t):
                pe.wait_ge(h_ready, t + 1)
                wait(pe, ht_used, t - 1)
                for k in range(ND):
                    last = nc.tensor.transpose(pt[t % 2][:, k, :], hn[:, t % 2, k * P:(k + 1) * P], ident[:])
                last.then_inc(ht_ready, 1)

            for t in range(NT):
                if project is not None:
                    wait(pe, y_used, t - 1)
                    project(pe, t, py[t % 2]).then_inc(y_ready, 1)
                if hT is not None and t:
                    transposes(t - 1)
            if hT is not None:
                transposes(NT - 1)

        @block.scalar
        def _(act):
            act.wait_ge(eps_set, 1)
            n = 0
            for t in range(NT):
                for _ in range(norms):
                    act.wait_ge(var_ready, n + 1)
                    nc.scalar.activation(std[:, n % 2:n % 2 + 1], mv[:, n % 2, 1:2], ACT.Sqrt,
                                         bias=eps[:, 0:1]).then_inc(std_ready, 1)
                    n += 1
                if hT is not None:
                    act.wait_ge(ht_ready, t + 1)
                    nc.scalar.copy(hT[:, :, t * P:(t + 1) * P], pt[t % 2][:]).then_inc(ht_used, 1)

        @block.vector
        def _(dve):
            done = [0]

            def then(instruction):
                done[0] += 1
                instruction.then_inc(dve_done, 1)
                dve.wait_ge(dve_done, done[0])

            n = 0

            def moments(src):
                then(nc.vector.bn_stats(stats[:, n % 2, :], src))
                nc.vector.bn_aggr(mv[:, n % 2, :], stats[:, n % 2, :]).then_inc(var_ready, 1)
                dve.wait_ge(std_ready, n + 1)
                then(nc.vector.reciprocal(rstd[:, n % 2:n % 2 + 1], std[:, n % 2:n % 2 + 1]))

            nc.vector.memset(eps[:], LN_EPS).then_inc(eps_set, 1)
            for t in range(NT):
                if project is not None:
                    dve.wait_ge(y_ready, t + 1)
                    moments(py[t % 2][:])
                    done[0] += 1
                    nc.vector.tensor_scalar(yn[:], py[t % 2][:], mv[:, n % 2, 0:1], rstd[:, n % 2:n % 2 + 1],
                                            ALU.subtract, ALU.mult).then_inc(y_used, 1)
                    done[0] -= 1
                    dve.wait_ge(y_used, t + 1)
                    n += 1
                    nc.vector.tensor_tensor(x[:, t, :], x[:, t, :], yn[:], ALU.add).then_inc(x_ready, 1)
                    dve.wait_ge(x_ready, t + 1)
                elif x_loads is not None:
                    dve.wait_ge(x_loads[t], 16)
                if hT is not None:
                    moments(x[:, t, :])
                    wait(dve, ht_ready, t - 1)
                    nc.vector.tensor_scalar(hn[:, t % 2, :], x[:, t, :], mv[:, n % 2, 0:1], rstd[:, n % 2:n % 2 + 1],
                                            ALU.subtract, ALU.mult).then_inc(h_ready, 1)
                    n += 1

        if out_dram is not None:
            @block.sync
            def _(sp):
                for t in range(NT):
                    sp.wait_ge(x_ready, t + 1)
                    sp.dma_start(out_dram[t * P:(t + 1) * P, :], x[:, t, :]).then_inc(x_out, 16)
                sp.wait_ge(x_out, 16 * NT)


def mla_inputs(nc, io, x, hT, ident, m):
    with ExitStack() as ctx:
        sem = lambda n: ctx.enter_context(nc.semaphore(f"mi_{n}"))
        sb = lambda n, s, d=F32: ctx.enter_context(nc.sbuf_tensor(f"mi_{n}", s, d))
        w_a = sb("w_a", [P, ND, QR + CR + ROPE])
        w_pe1, w_pe2 = sb("w_pe1", [P, H * ROPE]), sb("w_pe2", [QR - P, H * ROPE])
        cos, sin = sb("cos", [P, NT, ROPE]), sb("sin", [P, NT, ROPE])
        squares = sb("squares", [P, QR])
        ssq, std, rstd = sb("ssq", [P, 2, 2]), sb("std", [P, 2, 2]), sb("rstd", [P, 2, 2])
        eps = sb("eps", [P, 1])
        qn = sb("qn", [P, 2, QR])
        ck = sb("ck", [P, 2, 3 * CR])
        rope_k = sb("rope_k", [P, 2, ROPE])
        rope_a, rope_b = sb("rope_a", [P, 2, BANK]), sb("rope_b", [P, 2, BANK])
        q_pe = sb("q_pe", [P, 4, BANK])
        kt32 = sb("kt32", [P, 2, S])
        down = [ctx.enter_context(nc.psum_tensor(f"mi_down{i}", [P, BANK], F32)) for i in range(2)]
        turned = [ctx.enter_context(nc.psum_tensor(f"mi_turned{i}", [P, 4, P], F32)) for i in range(2)]
        pq = [ctx.enter_context(nc.psum_tensor(f"mi_pq{i}", [P, BANK], F32)) for i in range(2)]
        loads, consts = sem("loads"), sem("consts")
        down_ready = sem("down_ready")
        ssq_ready, std_ready = sem("ssq_ready"), sem("std_ready")
        tok_ready, turned_ready, turned_used = sem("tok_ready"), sem("turned_ready"), sem("turned_used")
        dve_done, kt_hi = sem("dve_done"), sem("kt_hi")
        pq_ready, pq_used, rot_ready, rot_used = sem("pq_ready"), sem("pq_used"), sem("rot_ready"), sem("rot_used")
        pe_ready, pt_ready, pt_used = sem("pe_ready"), sem("pt_ready"), sem("pt_used")
        block = ctx.enter_context(nc.Block())
        n_loads = 8
        NCH = H * ROPE // BANK
        HPC = BANK // ROPE

        @block.sync
        def _(sp):
            for dst, src in ((w_a[:], io["w_a"]), (cos[:], io["cos"]), (sin[:], io["sin"]),
                             (m["qw1"][:], io["qw1"]), (m["qw2"][:], io["qw2"]),
                             (w_pe1[:], io["w_pe"][0:P, :]), (w_pe2[:], io["w_pe"][P:QR, :]),
                             (m["kw"][:], io["kw"])):
                sp.dma_start(dst, src).then_inc(loads, 16)

        @block.tensor
        def _(pe):
            pe.wait_ge(loads, 16 * n_loads)
            pe.wait_ge(consts, 2)

            def project(t):
                wait(pe, tok_ready, t - 1)
                for k in range(ND):
                    last = nc.tensor.matmul(down[t % 2][:, 0:QR + CR + ROPE], hT[:, k, t * P:(t + 1) * P],
                                            w_a[:, k, :], start=k == 0, stop=k == ND - 1)
                last.then_inc(down_ready, 1)

            def turn(t):
                pe.wait_ge(tok_ready, t + 1)
                wait(pe, turned_used, t - 1)
                nc.tensor.transpose(turned[t % 2][:, 0, :], qn[:, t % 2, 0:P], ident[:])
                nc.tensor.transpose(turned[t % 2][0:QR - P, 1, :], qn[:, t % 2, P:QR], ident[:])
                nc.tensor.transpose(turned[t % 2][:, 2, :], ck[:, t % 2, 0:P], ident[:])
                nc.tensor.transpose(turned[t % 2][:, 3, :], ck[:, t % 2, CR:CR + P], ident[:]).then_inc(turned_ready, 1)

            project(0)
            for t in range(NT):
                if t + 1 < NT:
                    project(t + 1)
                turn(t)

            def rotary(n):
                t, c = divmod(n, NCH)
                pe.wait_ge(turned_used, t + 1)
                wait(pe, pq_used, n - 1)
                nc.tensor.matmul(pq[n % 2][:], m["qnT1"][:, t * P:(t + 1) * P], w_pe1[:, c * BANK:(c + 1) * BANK],
                                 start=True, stop=False)
                nc.tensor.matmul(pq[n % 2][:], m["qnT2"][:, t * P:(t + 1) * P], w_pe2[:, c * BANK:(c + 1) * BANK],
                                 start=False, stop=True).then_inc(pq_ready, 1)

            def turn_pe(n):
                t, c = divmod(n, NCH)
                pe.wait_ge(pe_ready, n + 1)
                wait(pe, pt_used, n - 1)
                for a in range(4):
                    last = nc.tensor.transpose(turned[n % 2][:, a, :], q_pe[:, n % 4, a * P:(a + 1) * P], ident[:])
                last.then_inc(pt_ready, 1)

            pe.wait_ge(turned_used, NT)
            for n in range(NT * NCH):
                rotary(n)
                if n >= 2:
                    turn_pe(n - 2)
            turn_pe(NT * NCH - 2)
            turn_pe(NT * NCH - 1)

        @block.scalar
        def _(act):
            act.wait_ge(loads, 16 * n_loads)
            act.wait_ge(consts, 2)

            def norms(t):
                act.wait_ge(down_ready, t + 1)
                nc.scalar.activation(squares[:], down[t % 2][:, 0:QR], ACT.Square,
                                     accum_out=ssq[:, t % 2, 0:1]).then_inc(ssq_ready, 1)
                act.wait_ge(ssq_ready, 2 * t + 1)
                nc.scalar.activation(squares[:, 0:CR], down[t % 2][:, QR:QR + CR], ACT.Square,
                                     accum_out=ssq[:, t % 2, 1:2]).then_inc(ssq_ready, 1)
                act.wait_ge(ssq_ready, 2 * t + 2)
                nc.scalar.activation(std[:, t % 2, 0:1], ssq[:, t % 2, 0:1], ACT.Sqrt, scale=1.0 / QR,
                                     bias=eps[:, 0:1])
                nc.scalar.activation(std[:, t % 2, 1:2], ssq[:, t % 2, 1:2], ACT.Sqrt, scale=1.0 / CR,
                                     bias=eps[:, 0:1]).then_inc(std_ready, 1)

            norms(0)
            for t in range(NT):
                if t + 1 < NT:
                    norms(t + 1)
                act.wait_ge(turned_ready, t + 1)
                tt = slice(t * P, (t + 1) * P)
                nc.scalar.mul(m["qnT1"][:, tt], turned[t % 2][:, 0, :], m["qw1"][:, 0:1])
                nc.scalar.mul(m["qnT2"][:, tt], turned[t % 2][0:QR - P, 1, :], m["qw2"][:, 0:1])
                nc.scalar.mul(kt32[:, 0, tt], turned[t % 2][:, 2, :], m["kw"][:, 0:1])
                nc.scalar.mul(kt32[:, 1, tt], turned[t % 2][:, 3, :], m["kw"][:, 1:2]).then_inc(turned_used, 1)
            act.wait_ge(turned_used, NT)
            for e in range(2):
                nc.scalar.copy(m["kt_hi"][e][:], kt32[:, e, :]).then_inc(kt_hi, 1)
            for n in range(NT * NCH):
                t, c = divmod(n, NCH)
                act.wait_ge(pt_ready, n + 1)
                nc.scalar.copy(m["peT"][:, 4 * c:4 * c + 4, t * P:(t + 1) * P], turned[n % 2][:]).then_inc(pt_used, 1)

        @block.vector
        def _(dve):
            done = [0]

            def then(instruction):
                done[0] += 1
                instruction.then_inc(dve_done, 1)
                dve.wait_ge(dve_done, done[0])

            nc.vector.memset(eps[:], RMS_EPS).then_inc(consts, 1)
            nc.vector.memset(m["c1"][:, :, CR:2 * CR], 1.0).then_inc(consts, 1)
            dve.wait_ge(loads, 16 * n_loads)

            def rotate(dst_a, dst_b, src, heads, t):
                pairs = lambda ap: ap.rearrange("p (h i two) -> p h i two", h=heads, two=2)
                table = lambda tab: tab[:, t, :].unsqueeze(1).to_broadcast([P, heads, ROPE])
                s4 = lambda tab: table(tab).rearrange("p h (i two) -> p h i two", two=2)
                nc.vector.tensor_tensor(dst_a.rearrange("p (h r) -> p h r", h=heads), src.rearrange("p (h r) -> p h r", h=heads),
                                        table(cos), ALU.mult)
                nc.vector.tensor_tensor(pairs(dst_b)[:, :, :, 0], pairs(src)[:, :, :, 1], s4(sin)[:, :, :, 0], ALU.mult)
                return nc.vector.tensor_tensor(pairs(dst_b)[:, :, :, 1], pairs(src)[:, :, :, 0], s4(sin)[:, :, :, 1],
                                               ALU.mult)

            for t in range(NT):
                dve.wait_ge(std_ready, t + 1)
                wait(dve, turned_ready, t - 1)
                then(nc.vector.reciprocal(rstd[:, t % 2, :], std[:, t % 2, :]))
                then(rotate(rope_k[:, 0, :], rope_k[:, 1, :], down[t % 2][:, QR + CR:QR + CR + ROPE], 1, t))
                nc.vector.tensor_tensor(ck[:, t % 2, CR:2 * CR], rope_k[:, 0, :], rope_k[:, 1, :], ALU.add)
                latent = down[t % 2][:, QR:QR + CR].unsqueeze(1).to_broadcast([P, 2, CR])
                outer = lambda ap: ap.rearrange("p (a c) -> p a c", c=CR)[:, 0:3:2, :]
                nc.vector.tensor_scalar(outer(ck[:, t % 2, :]), latent, rstd[:, t % 2, 1:2], None, ALU.mult)
                nc.vector.tensor_scalar(outer(m["c1"][:, t, :]), latent, rstd[:, t % 2, 1:2], None, ALU.mult)
                nc.vector.tensor_scalar(qn[:, t % 2, :], down[t % 2][:, 0:QR], rstd[:, t % 2, 0:1], None,
                                        ALU.mult).then_inc(tok_ready, 1)
            for e in range(2):
                dve.wait_ge(kt_hi, e + 1)
                nc.vector.tensor_tensor(m["kt_lo"][e][:], kt32[:, e, :], m["kt_hi"][e][:].bitcast(F32), ALU.subtract)
            for n in range(NT * NCH):
                t, c = divmod(n, NCH)
                dve.wait_ge(pq_ready, n + 1)
                wait(dve, pe_ready, n - 1)
                rotate(rope_a[:, n % 2, :], rope_b[:, n % 2, :], pq[n % 2][:], HPC, t).then_inc(pq_used, 1)

        @block.gpsimd
        def _(pool):
            for n in range(NT * NCH):
                t, c = divmod(n, NCH)
                pool.wait_ge(pq_used, n + 1)
                wait(pool, pt_ready, n - 3)
                dst = q_pe[:, n % 4, :].rearrange("p (a two r) -> p a two r", two=2, r=ROPE)
                view = lambda ap: ap.rearrange("p (a two r) -> p a two r", two=2, r=ROPE)
                a, b = view(rope_a[:, n % 2, :]), view(rope_b[:, n % 2, :])
                nc.gpsimd.tensor_tensor(dst[:, :, 0, :], a[:, :, 1, :], b[:, :, 1, :], ALU.add)
                nc.gpsimd.tensor_tensor(dst[:, :, 1, :], a[:, :, 0, :], b[:, :, 0, :], ALU.add).then_inc(pe_ready, 1)


def mla_heads(nc, io, ident_bf, ident, m):
    with ExitStack() as ctx:
        sem = lambda n: ctx.enter_context(nc.semaphore(f"mh_{n}"))
        sb = lambda n, s, d=F32: ctx.enter_context(nc.sbuf_tensor(f"mh_{n}", s, d))
        w = sb("w", [P, PACK])
        w_q = w[:, 0:2 * QR].rearrange("p (e r) -> p e r", e=2)
        w_k = w[:, 2 * QR:2 * QR + 2 * CR].rearrange("p (e c) -> p e c", e=2)
        w_v = w[:, 2 * QR + 2 * CR:2 * QR + 4 * CR].rearrange("p (e c) -> p e c", e=2)
        w_o = w[:, 2 * QR + 4 * CR:PACK].rearrange("p (e n) -> p e n", e=2)
        absorbed1, absorbed2 = sb("absorbed1", [P, 2 * CR]), sb("absorbed2", [QR - P, 2 * CR])
        q32 = [sb(f"q32_{e}", [P, S]) for e in range(2)]
        q_hi = [sb(f"q_hi{e}", [P, S], F32R) for e in range(2)]
        q_lo = [sb(f"q_lo{e}", [P, S], F32R) for e in range(2)]
        shift = [sb(f"shift{e}", [P, S], F32R) for e in range(2)]
        minus_one = sb("minus_one", [P, P], F32R)
        minus_f = sb("minus_f", [P, P])
        row_max = sb("row_max", [P, 2, NT])
        probs = sb("probs", [P, 3, BANK])
        mixed = sb("mixed", [P, 2, S])
        mask_qk, mask_kq = sb("mask_qk", [P, P], BF16), sb("mask_kq", [P, P], BF16)
        mask_f = sb("mask_f", [P, 2, P])
        max_ps = [ctx.enter_context(nc.psum_tensor(f"mh_max{i}", [P, S], F32)) for i in range(2)]
        score_ps = [ctx.enter_context(nc.psum_tensor(f"mh_score{i}", [P, BANK], F32)) for i in range(2)]
        mix_ps = ctx.enter_context(nc.psum_tensor("mh_mix", [P, BANK], F32))
        prep_ps = ctx.enter_context(nc.psum_tensor("mh_prep", [P, BANK], F32))
        consts, masks_in = sem("consts"), sem("masks_in")
        w_in, pe_in = sem("w_in"), [sem(f"pe_in{e}") for e in range(2)]
        prep_ready, prep_used = sem("prep_ready"), sem("prep_used")
        hi_ready, lo_ready = sem("hi_ready"), sem("lo_ready")
        max_ready, max_taken, shift_ready = sem("max_ready"), sem("max_taken"), sem("shift_ready")
        scores_ready, probs_ready, probs_used = sem("scores_ready"), sem("probs_ready"), sem("probs_used")
        mixed_ready = sem("mixed_ready")
        mixed_out = [sem(f"mixed_out{e}") for e in range(2)]
        block = ctx.enter_context(nc.Block())

        def looped(engine, body, first=1, end=PAIRS - 1):
            for i in range(first):
                body(i)
            with engine.Fori(first, end) as i:
                body(i)
            for i in range(end, PAIRS):
                body(i)

        is_last = lambda i: isinstance(i, int) and i == PAIRS - 1

        def split_rows(e):
            return (slice(0, CR), slice(CR, P)) if e == 0 else (slice(CR, P), slice(0, CR))

        @block.sync
        def _(sp):
            sp.dma_start(mask_f[:], io["masks"]).then_inc(masks_in, 16)

            def load_weights(i):
                wait(sp, prep_ready, 4 * i - 2)
                sp.dma_start(w[:], io["w_pairs"][bass.ds(i * P, P), :]).then_inc(w_in, 16)

            def load_rotary(i, e):
                wait(sp, lo_ready, 2 * i + e - 1)
                rows = split_rows(e)[1]
                sp.dma_start(q32[e][rows, :], m["peT"][rows, i, :]).then_inc(pe_in[e], 16)

            def step(i, more_weights):
                if not is_last(i):
                    load_rotary(i + 1, 0)
                    load_rotary(i + 1, 1)
                if more_weights:
                    load_weights(i + 2)

            load_weights(0)
            load_rotary(0, 0)
            load_rotary(0, 1)
            load_weights(1)
            step(0, True)
            with sp.Fori(1, PAIRS - 2) as i:
                step(i, True)
            step(PAIRS - 2, False)

        @block.gpsimd
        def _(pool):
            def make_shift(i, e, part):
                wait(pool, max_taken, 8 * (2 * i + e) + 4 * (part + 1))
                tiles = slice(4 * part, 4 * part + 4)
                nc.gpsimd.tensor_tensor(shift[e][:].rearrange("p (t k) -> p t k", k=P)[:, tiles, :],
                                        ident[:].unsqueeze(1).to_broadcast([P, 4, P]),
                                        row_max[:, e, tiles].unsqueeze(2).to_broadcast([P, 4, P]), ALU.mult
                                        ).then_inc(shift_ready, 1)

            def store(i, e):
                wait(pool, mixed_ready, 2 * (2 * i + e) + 2)
                rows, other = split_rows(e)
                pool.dma_start(m["peT"][rows, i, :], mixed[rows, e, :]).then_inc(mixed_out[e], 16)
                pool.dma_start(m["sums_dram"][bass.ds(2 * i + e, 1), :], mixed[other.start:other.start + 1, e, :]
                               ).then_inc(mixed_out[e], 16)

            def slot(i, e):
                nxt = (i, 1) if e == 0 else (i + 1, 0)
                if not (is_last(i) and e == 1):
                    make_shift(*nxt, 0)
                    make_shift(*nxt, 1)
                store(i, e)

            make_shift(0, 0, 0)
            make_shift(0, 0, 1)

            def body(i):
                slot(i, 0)
                slot(i, 1)
            looped(pool, body)
            pool.wait_ge(mixed_out[0], 32 * PAIRS)
            pool.wait_ge(mixed_out[1], 32 * PAIRS)

        @block.tensor
        def _(pe):
            def prep_absorb(i):
                wait(pe, w_in, 16 * (i + 1))
                wait(pe, prep_used, 4 * i)
                for e in range(2):
                    nc.tensor.matmul(prep_ps[:, e * CR:(e + 1) * CR], w_q[:, e, 0:P], w_k[:, e, :], start=True, stop=True)
                    last = nc.tensor.matmul(prep_ps[0:QR - P, P + e * CR:P + (e + 1) * CR], w_q[:, e, P:QR], w_k[:, e, :],
                                            start=True, stop=True)
                last.then_inc(prep_ready, 1)

            def prep_output(i):
                wait(pe, prep_used, 4 * i + 1)
                for e in range(2):
                    last = nc.tensor.matmul(prep_ps[e * CR:(e + 1) * CR, :], w_v[:, e, :], w_o[:, e, :], start=True, stop=True)
                last.then_inc(prep_ready, 1)

            def prep_queries(i, half):
                wait(pe, prep_used, 4 * i + 2 + half)
                h = slice(half * BANK, (half + 1) * BANK)
                nc.tensor.matmul(prep_ps[:], absorbed1[:], m["qnT1"][:, h], start=True, stop=False)
                nc.tensor.matmul(prep_ps[:], absorbed2[:], m["qnT2"][:, h], start=False, stop=True).then_inc(prep_ready, 1)

            def maximum(i, e, t):
                n = 8 * (2 * i + e) + t
                if t == 0:
                    wait(pe, hi_ready, 2 * i + e + 1)
                wait(pe, max_taken, n - 1)
                out, q = max_ps[t % 2], q_hi[e][:, t * P:(t + 1) * P]
                for c in range(t * P // BANK + 1):
                    k0, k1 = c * BANK, min((c + 1) * BANK, (t + 1) * P)
                    diagonal = k1 == (t + 1) * P
                    last = nc.tensor.matmul(out[:, k0:k1], q, m["kt_hi"][e][:, k0:k1], start=True, stop=not diagonal)
                    if diagonal:
                        last = nc.tensor.matmul(out[:, k1 - P:k1], ident_bf[:], mask_qk[:], start=False, stop=True)
                last.then_inc(max_ready, 1)

            def scores(i, e, u):
                half, j, q0, width = UNITS[u]
                n = NU * (2 * i + e) + u
                if u == 0:
                    wait(pe, lo_ready, 2 * i + e + 1)
                if j == 0:
                    wait(pe, shift_ready, 2 * (2 * i + e) + half + 1)
                wait(pe, probs_ready, n - 1)
                out, q, k = score_ps[u % 2][:, 0:width], slice(q0, q0 + width), slice(j * P, (j + 1) * P)
                diagonal = q0 == j * P
                nc.tensor.matmul(out, minus_one[:], shift[e][:, q], start=True, stop=False)
                nc.tensor.matmul(out, m["kt_hi"][e][:, k], q_hi[e][:, q], start=False, stop=False)
                nc.tensor.matmul(out, m["kt_hi"][e][:, k], q_lo[e][:, q], start=False, stop=False)
                last = nc.tensor.matmul(out, m["kt_lo"][e][:, k], q_hi[e][:, q], start=False, stop=not diagonal)
                if diagonal:
                    last = nc.tensor.matmul(out[:, 0:P], ident_bf[:], mask_kq[:], start=False, stop=True)
                last.then_inc(scores_ready, 1)

            def mix(i, e, u):
                half, j, q0, width = UNITS[u]
                if j == 0:
                    wait(pe, mixed_ready, 2 * (2 * i + e) + half)
                wait(pe, probs_ready, NU * (2 * i + e) + u + 1)
                o = q0 - half * BANK
                nc.tensor.matmul(mix_ps[:, o:o + width], m["c1"][:, j, e * CR:e * CR + P], probs[:, u % 3, 0:width],
                                 start=j == 0, stop=u + 1 == NU_HALF[half]).then_inc(probs_used, 1)

            def slot(i, e):
                nxt = (i, 1) if e == 0 else (i + 1, 0)
                for u in range(NU):
                    scores(i, e, u)
                    if u:
                        mix(i, e, u - 1)
                    if 2 <= u < 2 + NT and not (is_last(i) and e == 1):
                        maximum(*nxt, u - 2)
                    if e == 0 and not is_last(i):
                        if u == 1:
                            prep_absorb(i + 1)
                        if u == 4:
                            prep_output(i + 1)
                        if u == 7:
                            prep_queries(i + 1, 0)
                        if u == 9:
                            prep_queries(i + 1, 1)
                mix(i, e, NU - 1)

            pe.wait_ge(consts, 4)
            prep_absorb(0)
            prep_output(0)
            prep_queries(0, 0)
            prep_queries(0, 1)
            for t in range(NT):
                maximum(0, 0, t)

            def body(i):
                slot(i, 0)
                slot(i, 1)
            looped(pe, body)

        @block.scalar
        def _(act):
            def take_absorbed(i):
                wait(act, prep_ready, 4 * i + 1)
                nc.scalar.copy(absorbed1[:], prep_ps[:, 0:P])
                nc.scalar.copy(absorbed2[:], prep_ps[0:QR - P, P:2 * P]).then_inc(prep_used, 1)

            def take_output(i):
                wait(act, prep_ready, 4 * i + 2)
                nc.scalar.mul(m["w_out"][:, bass.ds(i, 1), :].rearrange("p a n -> p (a n)"), prep_ps[:], m["kw2"][:, 0:1]
                              ).then_inc(prep_used, 1)

            def take_queries(i, half):
                wait(act, prep_ready, 4 * i + 3 + half)
                if half == 0:
                    wait(act, lo_ready, 2 * i)
                h = slice(half * BANK, (half + 1) * BANK)
                for e in range(2):
                    rows = split_rows(e)[0]
                    last = nc.scalar.copy(q32[e][rows, h], prep_ps[rows, :])
                last.then_inc(prep_used, 1)

            def upper(i, e):
                wait(act, scores_ready, NU * (2 * i + e - 1))
                if e == 0:
                    wait(act, prep_used, 4 * i + 4)
                wait(act, pe_in[e], 16 * (i + 1))
                nc.scalar.copy(q_hi[e][:], q32[e][:]).then_inc(hi_ready, 1)

            def exp(i, e, u):
                n = NU * (2 * i + e) + u
                wait(act, scores_ready, n + 1)
                wait(act, probs_used, n - 2)
                width = UNITS[u][3]
                nc.scalar.activation(probs[:, u % 3, 0:width], score_ps[u % 2][:, 0:width], ACT.Exp,
                                     scale=MLA_SCALE).then_inc(probs_ready, 1)

            def slot(i, e):
                nxt = (i, 1) if e == 0 else (i + 1, 0)
                if not (is_last(i) and e == 1):
                    upper(*nxt)
                for u in range(NU):
                    exp(i, e, u)
                    if e == 0 and not is_last(i):
                        if u == 2:
                            take_absorbed(i + 1)
                        if u == 5:
                            take_output(i + 1)
                        if u == 8:
                            take_queries(i + 1, 0)
                        if u == 10:
                            take_queries(i + 1, 1)

            take_absorbed(0)
            take_output(0)
            take_queries(0, 0)
            take_queries(0, 1)
            upper(0, 0)

            def body(i):
                slot(i, 0)
                slot(i, 1)
            looped(act, body)

        @block.vector
        def _(dve):
            nc.vector.memset(minus_f[:], -1.0).then_inc(consts, 1)
            dve.wait_ge(consts, 1)
            nc.vector.tensor_copy(minus_one[:], minus_f[:]).then_inc(consts, 1)
            dve.wait_ge(masks_in, 16)
            nc.vector.tensor_copy(mask_qk[:], mask_f[:, 0, :]).then_inc(consts, 1)
            nc.vector.tensor_copy(mask_kq[:], mask_f[:, 1, :]).then_inc(consts, 1)

            def lower(i, e):
                wait(dve, hi_ready, 2 * i + e + 1)
                nc.vector.tensor_tensor(q_lo[e][:], q32[e][:], q_hi[e][:].bitcast(F32), ALU.subtract).then_inc(lo_ready, 1)

            def take_max(i, e, t):
                n = 8 * (2 * i + e) + t
                wait(dve, max_ready, n + 1)
                if t == 0:
                    wait(dve, shift_ready, 2 * (2 * i + e) - 2)
                nc.vector.reduce_max(row_max[:, e, t:t + 1], max_ps[t % 2][:, 0:(t + 1) * P], AX.X).then_inc(max_taken, 1)

            def take_mixed(i, e, half):
                wait(dve, probs_used, NU * (2 * i + e) + NU_HALF[half])
                if half == 0:
                    wait(dve, mixed_out[e], 32 * i)
                nc.vector.tensor_copy(mixed[:, e, half * BANK:(half + 1) * BANK], mix_ps[:]).then_inc(mixed_ready, 1)

            def slot(i, e):
                nxt = (i, 1) if e == 0 else (i + 1, 0)
                more = not (is_last(i) and e == 1)
                if more:
                    lower(*nxt)
                for t in range(NT):
                    if t == 2:
                        take_mixed(i, e, 0)
                    if more:
                        take_max(*nxt, t)
                take_mixed(i, e, 1)

            lower(0, 0)
            for t in range(NT):
                take_max(0, 0, t)

            def body(i):
                slot(i, 0)
                slot(i, 1)
            looped(dve, body)


def normalise(nc, name, out, sums_src, sums_dram_waits, select, n, io_select):
    with ExitStack() as ctx:
        sem = lambda s: ctx.enter_context(nc.semaphore(f"{name}_{s}"))
        sums = ctx.enter_context(nc.sbuf_tensor(f"{name}_sums", [H, S], F32))
        inverse = ctx.enter_context(nc.sbuf_tensor(f"{name}_inverse", [H, S], F32))
        spread = ctx.enter_context(nc.sbuf_tensor(f"{name}_spread", [H, n, P], F32))
        ps = [ctx.enter_context(nc.psum_tensor(f"{name}_ps{i}", [P, BANK], F32)) for i in range(4)]
        loads, inverse_ready, spread_ready, used = sem("loads"), sem("inverse_ready"), sem("spread_ready"), sem("used")
        block = ctx.enter_context(nc.Block())
        n_loads = len(sums_src(sums)) + 1

        @block.sync
        def _(sp):
            sp.dma_start(spread[:], io_select).then_inc(loads, 16)
            for dst, src in sums_src(sums):
                sp.dma_start(dst, src).then_inc(loads, 16)

        @block.tensor
        def _(pe):
            pe.wait_ge(inverse_ready, 1)
            for i in range(n):
                for half in range(NHALF):
                    k = NHALF * i + half
                    wait(pe, used, k - 3)
                    nc.tensor.matmul(ps[k % 4][:], spread[:, i, :], inverse[:, half * BANK:(half + 1) * BANK],
                                     start=True, stop=True).then_inc(spread_ready, 1)

        @block.vector
        def _(dve):
            dve.wait_ge(loads, 16 * n_loads)
            nc.vector.reciprocal(inverse[:], sums[:]).then_inc(inverse_ready, 1)
            for i in range(n):
                for half in range(NHALF):
                    k = NHALF * i + half
                    o = out[:, i, half * BANK:(half + 1) * BANK]
                    dve.wait_ge(spread_ready, k + 1)
                    nc.vector.tensor_tensor(o, o, ps[k % 4][:], ALU.mult).then_inc(used, 1)


def ffn_inner(nc, io, hT, d, w_down):
    with ExitStack() as ctx:
        sem = lambda s: ctx.enter_context(nc.semaphore(f"ff_{s}"))
        sb = lambda n, s, dt=F32: ctx.enter_context(nc.sbuf_tensor(f"ff_{n}", s, dt))
        w = [sb("w_gate", [P, ND, INNER]), sb("w_up", [P, ND, INNER])]
        su, sv = [sb(f"su{i}", [RANK, INNER]) for i in range(2)], [sb(f"sv{i}", [RANK, D]) for i in range(2)]
        su_d, sv_d = sb("su_d", [RANK, D]), sb("sv_d", [RANK, INNER])
        gated = sb("gated", [P, 2, BANK])
        CH = INNER // 4
        scale_ps = [ctx.enter_context(nc.psum_tensor(f"ff_scale{i}", [P, BANK], F32)) for i in range(2)]
        gate_ps = [ctx.enter_context(nc.psum_tensor(f"ff_gate{i}", [P, BANK], F32)) for i in range(2)]
        up_ps = [ctx.enter_context(nc.psum_tensor(f"ff_up{i}", [P, BANK], F32)) for i in range(2)]
        loads, w_loads = sem("loads"), [sem(f"w_load{i}") for i in range(2 * ND)]
        down_loads = sem("down_loads")
        scale_ready, scale_used = sem("scale_ready"), sem("scale_used")
        gate_ready, up_ready, gated_ready, d_ready = sem("gate_ready"), sem("up_ready"), sem("gated_ready"), sem("d_ready")
        block = ctx.enter_context(nc.Block())
        jobs = [(sv[i][:, k * P:(k + 1) * P], su[i][:, c * CH:(c + 1) * CH], w[i][:, k, c * CH:(c + 1) * CH],
                 w_loads[i * ND + k]) for i in range(2) for k in range(ND) for c in range(4)]
        jobs += [(sv_d[:, k * P:(k + 1) * P], su_d[:], w_down[:, k, :], down_loads) for k in range(NI)]
        N_UP = 2 * ND * 4

        @block.sync
        def _(sp):
            small = ((su[0], "gate_su"), (sv[0], "gate_sv"), (su[1], "up_su"), (sv[1], "up_sv"),
                     (su_d, "down_su"), (sv_d, "down_sv"))
            for dst, src in small:
                sp.dma_start(dst[:], io[src]).then_inc(loads, 16)
            for i, src in enumerate(("gate_w", "up_w")):
                for k in range(ND):
                    sp.dma_start(w[i][:, k, :], io[src][k * P:(k + 1) * P, :]).then_inc(w_loads[i * ND + k], 16)
            sp.dma_start(w_down[:], io["down_w"].rearrange("(k p) o -> p k o", p=P)).then_inc(down_loads, 16)

        @block.tensor
        def _(pe):
            pe.wait_ge(loads, 16 * 6)

            def scales(n):
                left, right, target, _ = jobs[n]
                wait(pe, scale_used, n - 1)
                nc.tensor.matmul(scale_ps[n % 2][:, 0:right.shape[1]], left, right, start=True, stop=True
                                 ).then_inc(scale_ready, 1)

            for n in range(N_UP):
                scales(n)
            pe.wait_ge(scale_used, N_UP)
            for n in range(NI * NHALF):
                it, half = divmod(n, NHALF)
                h = slice(half * BANK, (half + 1) * BANK)
                wait(pe, d_ready, n - 1)
                for i, (out, ready) in enumerate(((gate_ps, gate_ready), (up_ps, up_ready))):
                    for k in range(ND):
                        last = nc.tensor.matmul(out[n % 2][:], w[i][:, k, it * P:(it + 1) * P], hT[:, k, h],
                                                start=k == 0, stop=k == ND - 1)
                    last.then_inc(ready, 1)
                if n < NI:
                    scales(N_UP + n)

        @block.scalar
        def _(act):
            for n in range(NI * NHALF):
                act.wait_ge(gate_ready, n + 1)
                wait(act, d_ready, n - 1)
                nc.scalar.activation(gated[:, n % 2, :], gate_ps[n % 2][:], ACT.Silu).then_inc(gated_ready, 1)

        @block.vector
        def _(dve):
            def scale(n):
                _, right, target, load = jobs[n]
                dve.wait_ge(load, 16)
                dve.wait_ge(scale_ready, n + 1)
                nc.vector.tensor_tensor(target, target, scale_ps[n % 2][:, 0:right.shape[1]], ALU.mult
                                        ).then_inc(scale_used, 1)

            for n in range(N_UP):
                scale(n)
            for n in range(NI * NHALF):
                it, half = divmod(n, NHALF)
                dve.wait_ge(gated_ready, n + 1)
                dve.wait_ge(up_ready, n + 1)
                nc.vector.tensor_tensor(d[:, it, half * BANK:(half + 1) * BANK], gated[:, n % 2, :], up_ps[n % 2][:],
                                        ALU.mult).then_inc(d_ready, 1)
                if n < NI:
                    scale(N_UP + n)


def mha_inputs(nc, io, hT, scratch):
    with ExitStack() as ctx:
        sem = lambda s: ctx.enter_context(nc.semaphore(f"ai_{s}"))
        sb = lambda n, s, dt=F32: ctx.enter_context(nc.sbuf_tensor(f"ai_{n}", s, dt))
        w, bias_qk, bias_v = sb("w", [P, ND, 3 * D]), sb("bias_qk", [P, 2 * ND]), sb("bias_v", [P, D])
        full = sb("full", [P, 3, BANK])
        hi, lo = sb("hi", [P, 3, BANK], F32R), sb("lo", [P, 3, BANK], F32R)
        values = [sb(f"values{i}", [P, H, 2 * HD]) for i in range(2)]
        ps = [ctx.enter_context(nc.psum_tensor(f"ai_ps{i}", [P, BANK], F32)) for i in range(4)]
        loads, ones_set, ready, full_ready, hi_ready, lo_ready = (sem(s) for s in (
            "loads", "ones_set", "ready", "full_ready", "hi_ready", "lo_ready"))
        part_out, v_ready, v_out = [sem(f"part_out{i}") for i in range(3)], sem("v_ready"), [sem(f"v_out{i}") for i in range(2)]
        block = ctx.enter_context(nc.Block())
        NQK = 2 * ND * NHALF

        @block.sync
        def _(sp):
            for dst, src in ((w[:], io["qkv_w"]), (bias_qk[:], io["bias_qk"]), (bias_v[:], io["bias_v"])):
                sp.dma_start(dst, src).then_inc(loads, 16)
            for n in range(NQK):
                blk, half = divmod(n, NHALF)
                for part, buf, done in ((0, hi, hi_ready), (1, lo, lo_ready)):
                    sp.wait_ge(done, n + 1)
                    sp.dma_start(scratch["qk"][part, blk * P:(blk + 1) * P, half * BANK:(half + 1) * BANK],
                                 buf[:, n % 3, :].bitcast(F32)
                                 ).then_inc(part_out[n % 3], 16)
            for t in range(NT):
                sp.wait_ge(v_ready, t + 1)
                sp.dma_start(scratch["v"][t * P:(t + 1) * P, :], values[t % 2][:].rearrange("p h r -> p (h r)")
                             ).then_inc(v_out[t % 2], 16)
            for i in range(3):
                sp.wait_ge(part_out[i], 32 * len(range(i, NQK, 3)))
            for i in range(2):
                sp.wait_ge(v_out[i], 16 * NT // 2)

        @block.tensor
        def _(pe):
            pe.wait_ge(loads, 48)
            for n in range(NQK + NT):
                wait(pe, lo_ready, min(n - 3, NQK))
                wait(pe, v_ready, n - 3 - NQK)
                for k in range(ND):
                    if n < NQK:
                        blk, half = divmod(n, NHALF)
                        last = nc.tensor.matmul(ps[n % 4][:], w[:, k, blk * P:(blk + 1) * P],
                                                hT[:, k, half * BANK:(half + 1) * BANK], start=k == 0, stop=k == ND - 1)
                    else:
                        t = n - NQK
                        last = nc.tensor.matmul(ps[n % 4][:], hT[:, k, t * P:(t + 1) * P], w[:, k, 2 * D:3 * D],
                                                start=k == 0, stop=k == ND - 1)
                last.then_inc(ready, 1)

        @block.scalar
        def _(act):
            act.wait_ge(loads, 48)
            for n in range(NQK):
                blk = n // NHALF
                act.wait_ge(ready, n + 1)
                wait(act, lo_ready, n - 2)
                nc.scalar.activation(full[:, n % 3, :], ps[n % 4][:], ACT.Identity, bias=bias_qk[:, blk:blk + 1]
                                     ).then_inc(full_ready, 1)

        @block.vector
        def _(dve):
            for v in values:
                nc.vector.memset(v[:, :, HD:2 * HD], 1.0).then_inc(ones_set, 1)
            for n in range(NQK):
                dve.wait_ge(full_ready, n + 1)
                if n >= 3:
                    dve.wait_ge(part_out[n % 3], 32 * (n // 3))
                nc.vector.tensor_copy(hi[:, n % 3, :], full[:, n % 3, :]).then_inc(hi_ready, 1)
                dve.wait_ge(hi_ready, n + 1)
                nc.vector.tensor_tensor(lo[:, n % 3, :], full[:, n % 3, :], hi[:, n % 3, :].bitcast(F32), ALU.subtract
                                        ).then_inc(lo_ready, 1)
            dve.wait_ge(loads, 48)
            for t in range(NT):
                dve.wait_ge(ready, NQK + t + 1)
                if t >= 2:
                    dve.wait_ge(v_out[t % 2], 16 * (t // 2))
                nc.vector.tensor_tensor(values[t % 2][:, :, 0:HD], ps[(NQK + t) % 4][:].rearrange("p (h r) -> p h r", h=H),
                                        bias_v[:].rearrange("p (h r) -> p h r", h=H), ALU.add).then_inc(v_ready, 1)


def mha_heads(nc, io, ident, scratch, out):
    with ExitStack() as ctx:
        sem = lambda s: ctx.enter_context(nc.semaphore(f"ah_{s}"))
        sb = lambda n, s, dt=F32: ctx.enter_context(nc.sbuf_tensor(f"ah_{n}", s, dt))
        MAX_ROW = 3 * HD
        q_stack = [sb(f"q_stack{i}", [P, 4, S], F32R) for i in range(2)]
        k_stack = [sb(f"k_stack{i}", [P, 4, S], F32R) for i in range(2)]
        v = [sb(f"v{i}", [P, NT, 4 * 2 * HD]) for i in range(2)]
        zero_one = sb("zero_one", [1, 2, 4 * S], F32R)
        half_max, row_max = sb("half_max", [P, 4, NT, 2]), sb("row_max", [P, 4 * NT])
        minus_max = sb("minus_max", [4 * NT, P], F32R)
        probs = sb("probs", [P, 4, 2 * BANK])
        max_ps = [ctx.enter_context(nc.psum_tensor(f"ah_max{i}", [P, BANK], F32)) for i in range(2)]
        score_ps = [ctx.enter_context(nc.psum_tensor(f"ah_score{i}", [P, 2, BANK], F32)) for i in range(2)]
        mix_ps = ctx.enter_context(nc.psum_tensor("ah_mix", [P, BANK], F32))
        turn_ps = ctx.enter_context(nc.psum_tensor("ah_turn", [P, BANK], F32))
        cleared, rows_set = sem("cleared"), sem("rows_set")
        stacks_in = [sem(f"stacks_in{i}") for i in range(2)]
        v_in = [sem(f"v_in{i}") for i in range(2)]
        max_ready, max_taken, row_max_ready, turned, minus_ready, max_row_in = (sem(s) for s in (
            "max_ready", "max_taken", "row_max_ready", "turned", "minus_ready", "max_row_in"))
        scores_ready, probs_ready, mixed, out_taken = (sem(s) for s in ("scores_ready", "probs_ready", "mixed", "out_taken"))
        dve_done = sem("dve_done")
        block = ctx.enter_context(nc.Block())
        NUNIT = NHALF * NT
        NMAX = 4 * NT * 2
        qk_rows = scratch["qk"].rearrange("part (kind h d) s -> part kind d h s", kind=2, d=HD)
        v_rows = scratch["v"].rearrange("(t p) n -> p t n", p=P)

        def looped(engine, body):
            body(0)
            with engine.Fori(1, GROUPS // 2 - 1) as r:
                body(r)
            body(GROUPS // 2 - 1)

        more = lambda r, a: not (isinstance(r, int) and r == GROUPS // 2 - 1 and a == 1)

        @block.sync
        def _(sp):
            def load(r, a):
                g = 2 * r + a
                wait(sp, mixed, NUNIT * (g - 1))
                heads = bass.ds(4 * g, 4)
                for kind, stack, parts in ((0, q_stack[a], (0, 0, 1)), (1, k_stack[a], (0, 1, 0))):
                    for n, part in enumerate(parts):
                        sp.dma_start(stack[n * HD:(n + 1) * HD, :, :].bitcast(F32), qk_rows[part, kind, :, heads, :]).then_inc(stacks_in[a], 16)
                sp.dma_start(q_stack[a][MAX_ROW:MAX_ROW + 1, :, :].bitcast(F32), zero_f32r[0]).then_inc(stacks_in[a], 16)
                sp.dma_start(v[a][:], v_rows[:, :, bass.ds(4 * g * 2 * HD, 4 * 2 * HD)]).then_inc(v_in[a], 16)

            def put_max(r, a):
                g = 2 * r + a
                wait(sp, minus_ready, g + 1)
                sp.dma_start(q_stack[a][MAX_ROW:MAX_ROW + 1, :, :].rearrange("p h (t q) -> p (h t) q", q=P).bitcast(F32),
                             minus_max[:].bitcast(F32)).then_inc(max_row_in, 16)

            sp.wait_ge(cleared, 6)
            zero_f32r = [zero_one[:, i, :].rearrange("p (h s) -> p h s", h=4).bitcast(F32) for i in range(2)]
            for a in range(2):
                sp.dma_start(k_stack[a][MAX_ROW:MAX_ROW + 1, :, :].bitcast(F32), zero_f32r[1]).then_inc(rows_set, 16)
            load(0, 0)
            load(0, 1)
            put_max(0, 0)

            def body(r):
                for a in range(2):
                    if more(r, a):
                        put_max(*((r, 1) if a == 0 else (r + 1, 0)))
                    if not (isinstance(r, int) and r == GROUPS // 2 - 1):
                        load(r + 1, a)
            looped(sp, body)

        @block.tensor
        def _(pe):
            def maximum(r, a, n):
                g = 2 * r + a
                t, head, half = n // 8, n // 2 % 4, n % 2
                if n == 0:
                    wait(pe, stacks_in[a], 16 * 7 * (r + 1))
                wait(pe, max_taken, NMAX * g + n - 1)
                nc.tensor.matmul(max_ps[n % 2][:], q_stack[a][:, head, t * P:(t + 1) * P],
                                 k_stack[a][:, head, half * BANK:(half + 1) * BANK], start=True, stop=True
                                 ).then_inc(max_ready, 1)

            def turn_max(r, a):
                g = 2 * r + a
                wait(pe, row_max_ready, g + 1)
                wait(pe, minus_ready, g)
                nc.tensor.transpose(turn_ps[0:4 * NT, 0:P], row_max[:], ident[:]).then_inc(turned, 1)

            def scores(r, a, u, pair):
                g = 2 * r + a
                half, j = divmod(u, NT)
                if u == 0 and pair == 0:
                    wait(pe, max_row_in, 16 * (g + 1))
                wait(pe, probs_ready, 2 * (NUNIT * g + u) + pair - 1)
                for e in range(2):
                    head = 2 * pair + e
                    last = nc.tensor.matmul(score_ps[pair][:, e, :], k_stack[a][:, head, j * P:(j + 1) * P],
                                            q_stack[a][:, head, half * BANK:(half + 1) * BANK], start=True, stop=True)
                last.then_inc(scores_ready, 1)

            def mix(r, a, u):
                g = 2 * r + a
                half, j = divmod(u, NT)
                if u == 0:
                    wait(pe, v_in[a], 16 * (r + 1))
                if j == 0:
                    wait(pe, out_taken, NHALF * g + half)
                wait(pe, probs_ready, 2 * (NUNIT * g + u + 1))
                for head in range(4):
                    rows = slice(32 * head, 32 * head + 32)
                    last = nc.tensor.matmul(mix_ps[rows, :], v[a][:, j, rows],
                                            probs[:, 2 * (u % 2) + head // 2, (head % 2) * BANK:(head % 2 + 1) * BANK],
                                            start=j == 0, stop=j == NT - 1)
                last.then_inc(mixed, 1)

            def slot(r, a):
                nxt = (r, 1) if a == 0 else (r + 1, 0)
                n = 0
                for u in range(NUNIT):
                    scores(r, a, u, 0)
                    scores(r, a, u, 1)
                    if more(r, a) and u:
                        for _ in range(min(5, NMAX - n)):
                            maximum(*nxt, n)
                            n += 1
                    if u:
                        mix(r, a, u - 1)
                    if u == 14 and more(r, a):
                        turn_max(*nxt)
                mix(r, a, NUNIT - 1)

            pe.wait_ge(rows_set, 32)
            for n in range(NMAX):
                maximum(0, 0, n)
            turn_max(0, 0)

            def body(r):
                slot(r, 0)
                slot(r, 1)
            looped(pe, body)

        @block.scalar
        def _(act):
            def take_turned(r, a):
                g = 2 * r + a
                wait(act, turned, g + 1)
                wait(act, max_row_in, 16 * g)
                nc.scalar.mul(minus_max[:], turn_ps[0:4 * NT, 0:P], -1.0).then_inc(minus_ready, 1)

            def take_out(r, a, half):
                g = 2 * r + a
                wait(act, mixed, NUNIT * g + NT * (half + 1))
                nc.scalar.copy(out[:, bass.ds(g, 1), half * BANK:(half + 1) * BANK].rearrange("p a n -> p (a n)"), mix_ps[:]
                               ).then_inc(out_taken, 1)

            def exp(r, a, u, pair):
                g = 2 * r + a
                wait(act, scores_ready, 2 * (NUNIT * g + u) + pair + 1)
                wait(act, mixed, NUNIT * g + u - 1)
                nc.scalar.activation(probs[:, 2 * (u % 2) + pair, :], score_ps[pair][:].rearrange("p e n -> p (e n)"),
                                     ACT.Exp, scale=MHA_SCALE).then_inc(probs_ready, 1)

            def slot(r, a):
                for u in range(NUNIT):
                    exp(r, a, u, 0)
                    exp(r, a, u, 1)
                    if u == NT:
                        take_out(r, a, 0)
                    if u == 14 and more(r, a):
                        take_turned(*((r, 1) if a == 0 else (r + 1, 0)))
                take_out(r, a, 1)

            take_turned(0, 0)

            def body(r):
                slot(r, 0)
                slot(r, 1)
            looped(act, body)

        @block.vector
        def _(dve):
            for stack in (*q_stack, *k_stack):
                nc.vector.memset(stack[:].bitcast(F32), 0.0).then_inc(cleared, 1)
            for i, value in enumerate((0.0, 1.0)):
                nc.vector.memset(zero_one[:, i, :].bitcast(F32), value).then_inc(cleared, 1)

            def take_max(r, a, n):
                g = 2 * r + a
                t, head, half = n // 8, n // 2 % 4, n % 2
                wait(dve, max_ready, NMAX * g + n + 1)
                nc.vector.reduce_max(half_max[:, head, t, half:half + 1], max_ps[n % 2][:], AX.X).then_inc(max_taken, 1)

            def join_max(r, a):
                g = 2 * r + a
                wait(dve, turned, g)
                wait(dve, max_taken, NMAX * (g + 1))
                flat = half_max[:].rearrange("p h t two -> p (h t) two")
                nc.vector.tensor_tensor(row_max[:], flat[:, :, 0], flat[:, :, 1], ALU.max).then_inc(row_max_ready, 1)

            def group(r, a):
                for n in range(NMAX):
                    take_max(r, a, n)
                join_max(r, a)

            group(0, 0)

            def body(r):
                group(r, 1)
                if more(r, 1):
                    group(r + 1, 0)
            looped(dve, body)


def dequantise(nc, io, w):
    with ExitStack() as ctx:
        sem = lambda s: ctx.enter_context(nc.semaphore(f"dq_{s}"))
        sb = lambda n, s, dt=F32: ctx.enter_context(nc.sbuf_tensor(f"dq_{n}", s, dt))
        q, zeros, scales = sb("q", [P, ND, D], I32), sb("zeros", [P, ND, D]), sb("scales", [P, ND, D])
        loads, done = sem("loads"), sem("done")
        block = ctx.enter_context(nc.Block())
        per_tile = P // QGROUP

        @block.sync
        def _(sp):
            sp.dma_start(q[:], io["qweight"].rearrange("(k p) o -> p k o", p=P)).then_inc(loads, 16)
            for dst, src in ((zeros, io["zeros"]), (scales, io["scales"])):
                grouped = src.rearrange("(k g) o -> g k o", g=per_tile)
                for g in range(per_tile):
                    sp.dma_start(dst[g * QGROUP:(g + 1) * QGROUP, :, :],
                                 grouped[g:g + 1, :, :].to_broadcast([QGROUP, ND, D])).then_inc(loads, 16)

        @block.vector
        def _(dve):
            dve.wait_ge(loads, 16 * (1 + 2 * per_tile))
            nc.vector.tensor_copy(w[:], q[:]).then_inc(done, 1)
            dve.wait_ge(done, 1)
            nc.vector.tensor_tensor(w[:], w[:], zeros[:], ALU.subtract).then_inc(done, 1)
            dve.wait_ge(done, 2)
            nc.vector.tensor_tensor(w[:], w[:], scales[:], ALU.mult).then_inc(done, 1)


def load_all(nc, name, pairs):
    with ExitStack() as ctx:
        loads = ctx.enter_context(nc.semaphore(f"{name}_loads"))
        block = ctx.enter_context(nc.Block())

        @block.sync
        def _(sp):
            for dst, src in pairs:
                sp.dma_start(dst, src).then_inc(loads, 16)
            sp.wait_ge(loads, 16 * len(pairs))


def two_layers(nc, io, out_dram, upto=4):
    with ExitStack() as ctx:
        sb = lambda n, s, dt=F32: ctx.enter_context(nc.sbuf_tensor(n, s, dt))
        x, ident, ident_bf = sb("x", [P, NT, D]), sb("ident", [P, P]), sb("ident_bf", [P, P], BF16)
        sums_dram = nc.dram_tensor("sums_scratch", (H, S), F32, kind="Internal").ap()
        scratch = {"qk": nc.dram_tensor("qk_scratch", (2, 2 * D, S), F32, kind="Internal").ap(),
                   "v": nc.dram_tensor("v_scratch", (S, H * 2 * HD), F32, kind="Internal").ap()}
        load_all(nc, "in", [(ident[:], io["ident"]), (x[:], io["x"].rearrange("(t p) d -> p t d", p=P))])

        with ExitStack() as layer:
            sb = lambda n, s, dt=F32: layer.enter_context(nc.sbuf_tensor(n, s, dt))
            peT = sb("peT", [P, PAIRS, S])
            w_out = sb("w_out", [P, PAIRS, D])
            with ExitStack() as part:
                sb = lambda n, s, dt=F32: part.enter_context(nc.sbuf_tensor(n, s, dt))
                m = {"peT": peT, "w_out": w_out, "sums_dram": sums_dram,
                     "qnT1": sb("qnT1", [P, S]), "qnT2": sb("qnT2", [QR - P, S]),
                     "kt_hi": [sb(f"kt_hi{e}", [P, S], F32R) for e in range(2)],
                     "kt_lo": [sb(f"kt_lo{e}", [P, S], F32R) for e in range(2)],
                     "c1": sb("c1", [P, NT, 3 * CR]), "qw1": sb("qw1", [P, 1]), "qw2": sb("qw2", [QR - P, 1]),
                     "kw": sb("kw", [P, 2]), "kw2": sb("kw2", [P, 1])}
                load_all(nc, "kw2", [(m["kw2"][:], io["kw2"])])
                hT = w_out[:, 0:ND * S // D, :].rearrange("p a n -> p (a n)").rearrange("p (k s) -> p k s", k=ND)
                norm_block(nc, "n0", x, hT, ident)
                mla_inputs(nc, io, x, hT, ident, m)
                with nc.semaphore("ident_bf_set") as done, nc.Block() as block:
                    @block.vector
                    def _(dve):
                        nc.vector.tensor_copy(ident_bf[:], ident[:]).then_inc(done, 1)
                        dve.wait_ge(done, 1)
                mla_heads(nc, io, ident_bf, ident, m)
            normalise(nc, "mn", peT, lambda sums: [(sums[:], sums_dram)], None, io["spread_mla"], PAIRS, io["spread_mla"])

            def project(pe, t, out):
                for i in range(PAIRS):
                    last = nc.tensor.matmul(out[:], peT[:, i, t * P:(t + 1) * P], w_out[:, i, :], start=i == 0,
                                            stop=i == PAIRS - 1)
                return last
            if upto == 1:
                norm_block(nc, "n1", x, None, ident, project=project, out_dram=out_dram)
                return
            hT1 = sb("hT1", [P, ND, S]) if False else layer.enter_context(nc.sbuf_tensor("hT1", [P, ND, S], F32))
            norm_block(nc, "n1", x, hT1, ident, project=project)
            hT_home = nc.dram_tensor("hT_scratch", (P, ND * S), F32, kind="Internal").ap()
            load_all(nc, "hT_away", [(hT_home, hT1[:].rearrange("p k s -> p (k s)"))])

        with ExitStack() as layer:
            sb = lambda n, s, dt=F32: layer.enter_context(nc.sbuf_tensor(n, s, dt))
            hT, d, w_down = sb("hT2", [P, ND, S]), sb("d", [P, NI, S]), sb("w_down", [P, NI, D])
            load_all(nc, "hT_back", [(hT[:].rearrange("p k s -> p (k s)"), hT_home)])
            ffn_inner(nc, io, hT, d, w_down)

            def project(pe, t, out):
                for i in range(NI):
                    last = nc.tensor.matmul(out[:], d[:, i, t * P:(t + 1) * P], w_down[:, i, :], start=i == 0,
                                            stop=i == NI - 1)
                return last
            if upto == 2:
                norm_block(nc, "n2", x, None, ident, project=project, out_dram=out_dram)
                return
            norm_block(nc, "n2", x, hT, ident, project=project)
            mha_inputs(nc, io, hT, scratch)

        with ExitStack() as layer:
            sb = lambda n, s, dt=F32: layer.enter_context(nc.sbuf_tensor(n, s, dt))
            mixed, w_out = sb("mha_mixed", [P, GROUPS, S]), sb("w_out_mha", [P, GROUPS, D])
            load_all(nc, "wo", [(w_out[:], io["o_w"])])
            mha_heads(nc, io, ident, scratch, mixed)
            normalise(nc, "an", mixed, lambda sums: [
                (sums[g * GROUPS:(g + 1) * GROUPS, :], mixed[32 * g + HD:32 * g + HD + 1, :, :]) for g in range(4)],
                None, io["spread_mha"], GROUPS, io["spread_mha"])

            def project(pe, t, out):
                for i in range(GROUPS):
                    last = nc.tensor.matmul(out[:], mixed[:, i, t * P:(t + 1) * P], w_out[:, i, :], start=i == 0,
                                            stop=i == GROUPS - 1)
                return last
            if upto == 3:
                norm_block(nc, "n3", x, None, ident, project=project, out_dram=out_dram)
                return
            hT, w, bias, ones = sb("hT3", [P, ND, S]), sb("w_lin", [P, ND, D]), sb("bias_lin", [1, D]), sb("ones_lin", [1, P])
            norm_block(nc, "n3", x, hT, ident, project=project)
            dequantise(nc, io, w)
            load_all(nc, "bias", [(bias[:], io["lin_bias"]), (ones[:], io["ones"])])

            def project(pe, t, out):
                for k in range(ND):
                    nc.tensor.matmul(out[:], hT[:, k, t * P:(t + 1) * P], w[:, k, :], start=k == 0, stop=False)
                return nc.tensor.matmul(out[:], ones[:], bias[:], start=False, stop=True)
            norm_block(nc, "n4", x, None, ident, project=project, out_dram=out_dram)


def layouts(i):
    import numpy as np
    c = np.ascontiguousarray
    a = {k: np.asarray(v) for k, v in i.items()}
    wq = a["L0_attn_Wq_b"].reshape(QR, H, NOPE + ROPE)
    wkv = a["L0_attn_Wkv_b"].reshape(CR, H, NOPE + VD)
    wo = a["L0_attn_Wo"].reshape(H, VD, D)
    by_pair = lambda m: m.reshape(PAIRS, 2, P, -1).transpose(0, 2, 1, 3).reshape(PAIRS, P, -1)
    packed = [by_pair(m) for m in (wq[:, :, :NOPE].transpose(1, 2, 0), wkv[:, :, :NOPE].transpose(1, 2, 0),
                                   wkv[:, :, NOPE:].transpose(1, 2, 0), wo)]
    qw, kw = a["L0_attn_q_a_ln_w"], a["L0_attn_kv_a_ln_w"]
    one = np.ones((CR,), np.float32)
    w_a = np.concatenate([a["L0_attn_Wq_a"], a["L0_attn_Wkv_a"]], 1)
    angle_f = np.float32(1.0) / np.float32(10000.0) ** (np.arange(0, ROPE, 2, dtype=np.float32) / np.float32(ROPE))
    angle = np.outer(np.arange(S, dtype=np.float32), angle_f.astype(np.float32)).astype(np.float32)
    cos = np.repeat(np.cos(angle), 2, 1).astype(np.float32)
    sin = np.repeat(np.sin(angle), 2, 1).astype(np.float32) * np.tile(np.array([-1, 1], np.float32), ROPE // 2)
    by_tile = lambda m: c(m.reshape(-1, P, m.shape[1]).transpose(1, 0, 2))
    below = np.arange(P)[:, None] < np.arange(P)[None, :]
    mask = np.where(below, np.float32(-1e30), np.float32(0))
    rows = np.arange(P)
    spread_mla = np.zeros((H, PAIRS, P), np.float32)
    for n in range(PAIRS):
        spread_mla[2 * n + rows // CR, n, rows] = 1
    spread_mha = np.zeros((H, GROUPS, P), np.float32)
    for n in range(GROUPS):
        spread_mha[(rows // 32) * GROUPS + n, n, rows] = 1
    o_w = np.zeros((4, 32, GROUPS, D), np.float32)
    o_w[:, :HD] = a["L1_attn_attn_ow"].reshape(GROUPS, 4, HD, D).transpose(1, 2, 0, 3)
    o_w[0, HD, 0] = a["L1_attn_attn_ob"]
    qkv_b = a["L1_attn_attn_qkvb"]
    return {
        "x": c(a["L0_attn_hidden_states"].reshape(S, D)), "ident": np.eye(P, dtype=np.float32),
        "w_a": by_tile(w_a), "cos": by_tile(cos), "sin": by_tile(sin),
        "qw1": c(qw[:P, None]), "qw2": c(qw[P:, None]), "kw2": c(np.concatenate([kw, kw])[:, None]),
        "kw": c(np.stack([np.concatenate([kw, one]), np.concatenate([one, kw])], 1)),
        "w_pe": c(wq[:, :, NOPE:].reshape(QR, H * ROPE)),
        "w_pairs": c(np.concatenate(packed, 2).reshape(PAIRS * P, PACK)),
        "masks": c(np.stack([mask, mask.T], 1)), "spread_mla": spread_mla, "spread_mha": spread_mha,
        "gate_w": c(a["L0_ffn_gate_w"].T), "up_w": c(a["L0_ffn_up_w"].T), "down_w": c(a["L0_ffn_down_w"].T),
        "gate_su": c(a["L0_ffn_gate_su"].T), "up_su": c(a["L0_ffn_up_su"].T), "down_su": c(a["L0_ffn_down_su"].T),
        "gate_sv": c(a["L0_ffn_gate_sv"]), "up_sv": c(a["L0_ffn_up_sv"]), "down_sv": c(a["L0_ffn_down_sv"]),
        "qkv_w": by_tile(a["L1_attn_attn_qkvw"]), "bias_qk": c(qkv_b[:2 * D].reshape(2 * ND, P).T),
        "bias_v": c(np.broadcast_to(qkv_b[None, 2 * D:], (P, D))), "o_w": c(o_w.reshape(P, GROUPS, D)),
        "qweight": c(a["L1_ffn_qweight"].T),
        "zeros": c(a["L1_ffn_zeros"].reshape(D, -1).T), "scales": c(a["L1_ffn_scales"].reshape(D, -1).T),
        "lin_bias": c(a["L1_ffn_bias"][None, :]), "ones": np.ones((1, P), np.float32),
    }


def kernel(**inputs):
    import concourse.bacc as bacc
    import numpy as np
    from concourse.bass_utils import run_bass_kernel_spmd

    nc = bacc.Bacc("TRN2", target_bir_lowering=False, num_devices=1)
    arrays = {f"in_{k}": v for k, v in layouts(inputs).items()}
    io = {k[3:]: nc.dram_tensor(k, v.shape, mybir.dt.from_np(v.dtype), kind="ExternalInput").ap() for k, v in arrays.items()}
    out = nc.dram_tensor("out", (S, D), F32, kind="ExternalOutput").ap()
    two_layers(nc, io, out)
    r = run_bass_kernel_spmd(nc, [arrays], core_ids=[0])
    return r.results[0]["out"].reshape(1, S, D)
```

```python
import concourse.bass as bass
from concourse import mybir
from contextlib import ExitStack

F32 = mybir.dt.float32
F32R = mybir.dt.float32r
BF16 = mybir.dt.bfloat16
I32 = mybir.dt.int32
ALU = mybir.AluOpType
ACT = mybir.ActivationFunctionType
AX = mybir.AxisListType

P = 128
S = 1024
D = 512
NT = S // P
ND = D // P
BANK = 512
NHALF = S // BANK
LN_EPS = 1e-5

H = 32
QR, CR = 192, 64
NOPE, ROPE, VD = 128, 64, 128
PAIRS = H // 2
RMS_EPS = 1e-6
MLA_SCALE = float((NOPE + ROPE) ** -0.5)
PACK = 2 * (QR + CR + CR + D)

INNER = 1792
NI = INNER // P
RANK = 4
RIGHT = 2 * INNER + D
SIDES = RIGHT + 2 * D + INNER

HD = 16
GROUPS = H // 4
MHA_SCALE = float(HD ** -0.5)

QGROUP = 32


def wait(engine, semaphore, value):
    if isinstance(value, int) and value <= 0:
        return
    engine.wait_ge(semaphore, value)


def norm_block(nc, name, x, hT, ident, project=None, out_dram=None, x_dram=None, scalar_work=None, vector_work=None,
               projected=None):
    with ExitStack() as ctx:
        sem = lambda n: ctx.enter_context(nc.semaphore(f"{name}_{n}"))
        sb = lambda n, s, d=F32: ctx.enter_context(nc.sbuf_tensor(f"{name}_{n}", s, d))
        var_ready, std_ready, dve_done = sem("var_ready"), sem("std_ready"), sem("dve_done")
        if project is not None:
            y_ready, y_used, x_ready = projected or sem("y_ready"), sem("y_used"), sem("x_ready")
        if hT is not None:
            h_ready, ht_ready, ht_used = sem("h_ready"), sem("ht_ready"), sem("ht_used")
            parts = isinstance(hT, tuple)
            hT_hi_ready = sem("hT_hi_ready") if parts else None
        if out_dram is not None:
            x_out = sem("x_out")
        if x_dram is not None:
            x_tiles = ((0, NT),) if project is not None else ((0, 1), (1, 4), (4, NT))
            x_in = [sem(f"x_in{n}") for n in range(len(x_tiles))]
        py = [ctx.enter_context(nc.psum_tensor(f"{name}_py{i}", [P, D], F32)) for i in range(2)]
        pt = [ctx.enter_context(nc.psum_tensor(f"{name}_pt{i}", [P, ND, P], F32)) for i in range(2)]
        stats, mv = sb("stats", [P, 2, 6]), sb("mv", [P, 2, 2])
        std, rstd = sb("std", [P, 2]), sb("rstd", [P, 2])
        eps = sb("eps", [P, 1])
        yn, hn = sb("yn", [P, D]), sb("hn", [P, 2, D])
        block = ctx.enter_context(nc.Block())
        norms = (project is not None) + (hT is not None)

        if x_dram is not None:
            @block.sync
            def _(sp):
                for n, (first, end) in enumerate(x_tiles):
                    sp.dma_start(x[:, first:end, :], x_dram[first * P:end * P, :].rearrange("(t p) d -> p t d", p=P)
                                 ).then_inc(x_in[n], 16)

        @block.tensor
        def _(pe):
            def transposes(t):
                pe.wait_ge(h_ready, t + 1)
                wait(pe, ht_used, t - 1)
                for k in range(ND):
                    last = nc.tensor.transpose(pt[t % 2][:, k, :], hn[:, t % 2, k * P:(k + 1) * P], ident[:])
                last.then_inc(ht_ready, 1)

            for t in range(NT):
                if project is not None:
                    wait(pe, y_used, t - 1)
                    project(pe, t, py[t % 2]).then_inc(y_ready, 1)
                if hT is not None and t:
                    transposes(t - 1)
            if hT is not None:
                transposes(NT - 1)

        @block.scalar
        def _(act):
            n = 0
            if scalar_work is not None:
                scalar_work(act, 0)
                scalar_work(act, 1)
            for t in range(NT):
                for _ in range(norms):
                    act.wait_ge(var_ready, n + 1)
                    nc.scalar.activation(std[:, n % 2:n % 2 + 1], mv[:, n % 2, 1:2], ACT.Sqrt,
                                         bias=eps[:, 0:1]).then_inc(std_ready, 1)
                    n += 1
                if scalar_work is not None and t + 2 < NT:
                    scalar_work(act, t + 2)
                if hT is not None:
                    act.wait_ge(ht_ready, t + 1)
                    nc.scalar.copy((hT[0] if parts else hT)[:, :, t * P:(t + 1) * P], pt[t % 2][:]
                                   ).then_inc(hT_hi_ready if parts else ht_used, 1)

        @block.vector
        def _(dve):
            done = [0]

            def then(instruction):
                done[0] += 1
                instruction.then_inc(dve_done, 1)
                dve.wait_ge(dve_done, done[0])

            n = 0

            def moments(src):
                then(nc.vector.bn_stats(stats[:, n % 2, :], src))
                nc.vector.bn_aggr(mv[:, n % 2, :], stats[:, n % 2, :]).then_inc(var_ready, 1)
                dve.wait_ge(std_ready, n + 1)
                then(nc.vector.reciprocal(rstd[:, n % 2:n % 2 + 1], std[:, n % 2:n % 2 + 1]))

            def lower(t):
                dve.wait_ge(hT_hi_ready, t + 1)
                tokens = slice(t * P, (t + 1) * P)
                nc.vector.tensor_tensor(hT[1][:, :, tokens], pt[t % 2][:], hT[0][:, :, tokens].bitcast(F32), ALU.subtract
                                        ).then_inc(ht_used, 1)

            nc.vector.memset(eps[:], LN_EPS)
            if vector_work is not None:
                vector_work(dve, 0)
                vector_work(dve, 1)
            for t in range(NT):
                if x_dram is not None:
                    dve.wait_ge(x_in[sum(t >= end for _, end in x_tiles)], 16)
                if project is not None:
                    dve.wait_ge(y_ready, t + 1)
                    moments(py[t % 2][:])
                    done[0] += 1
                    nc.vector.tensor_scalar(yn[:], py[t % 2][:], mv[:, n % 2, 0:1], rstd[:, n % 2:n % 2 + 1],
                                            ALU.subtract, ALU.mult).then_inc(y_used, 1)
                    done[0] -= 1
                    dve.wait_ge(y_used, t + 1)
                    n += 1
                    nc.vector.tensor_tensor(x[:, t, :], x[:, t, :], yn[:], ALU.add).then_inc(x_ready, 1)
                    dve.wait_ge(x_ready, t + 1)
                if hT is not None:
                    moments(x[:, t, :])
                    wait(dve, ht_ready, t - 1)
                    nc.vector.tensor_scalar(hn[:, t % 2, :], x[:, t, :], mv[:, n % 2, 0:1], rstd[:, n % 2:n % 2 + 1],
                                            ALU.subtract, ALU.mult).then_inc(h_ready, 1)
                    n += 1
                if vector_work is not None and t + 2 < NT:
                    vector_work(dve, t + 2)
                if hT is not None and parts and t:
                    lower(t - 1)
            if hT is not None and parts:
                lower(NT - 1)

        if out_dram is not None:
            @block.sync
            def _(sp):
                for t in range(NT):
                    sp.wait_ge(x_ready, t + 1)
                    sp.dma_start(out_dram[t * P:(t + 1) * P, :], x[:, t, :]).then_inc(x_out, 16)
                sp.wait_ge(x_out, 16 * NT)


def mla_inputs(nc, io, hT, ident, m):
    with ExitStack() as ctx:
        sem = lambda n: ctx.enter_context(nc.semaphore(f"mi_{n}"))
        sb = lambda n, s, d=F32: ctx.enter_context(nc.sbuf_tensor(f"mi_{n}", s, d))
        w_a = sb("w_a", [P, ND, QR + CR + ROPE])
        w_pe1, w_pe2 = sb("w_pe1", [P, H * ROPE]), sb("w_pe2", [QR - P, H * ROPE])
        cos, sin = sb("cos", [P, NT, ROPE]), sb("sin", [P, NT, ROPE])
        squares = sb("squares", [P, QR])
        ssq, std, rstd = sb("ssq", [P, 2, 2]), sb("std", [P, 2, 2]), sb("rstd", [P, 2, 2])
        eps = sb("eps", [P, 1])
        qn = sb("qn", [P, 2, QR])
        ck = sb("ck", [P, 2, 3 * CR])
        rope_k = sb("rope_k", [P, 2, ROPE])
        rope_a, rope_b = sb("rope_a", [P, 2, BANK]), sb("rope_b", [P, 2, BANK])
        q_pe = sb("q_pe", [P, 4, BANK])
        kt32 = sb("kt32", [P, 2, S])
        down = [ctx.enter_context(nc.psum_tensor(f"mi_down{i}", [P, BANK], F32)) for i in range(2)]
        turned = [ctx.enter_context(nc.psum_tensor(f"mi_turned{i}", [P, 4, P], F32)) for i in range(2)]
        pq = [ctx.enter_context(nc.psum_tensor(f"mi_pq{i}", [P, BANK], F32)) for i in range(2)]
        loads, consts = sem("loads"), sem("consts")
        down_ready = sem("down_ready")
        ssq_ready, std_ready = sem("ssq_ready"), sem("std_ready")
        tok_ready, turned_ready, turned_used = sem("tok_ready"), sem("turned_ready"), sem("turned_used")
        dve_done, kt_hi = sem("dve_done"), sem("kt_hi")
        pq_ready, pq_used, rot_ready, rot_used = sem("pq_ready"), sem("pq_used"), sem("rot_ready"), sem("rot_used")
        pe_ready, pt_ready, pt_used = sem("pe_ready"), sem("pt_ready"), sem("pt_used")
        block = ctx.enter_context(nc.Block())
        n_loads = 8
        NCH = H * ROPE // BANK
        HPC = BANK // ROPE

        @block.sync
        def _(sp):
            for dst, src in ((w_a[:], io["w_a"]), (cos[:], io["cos"]), (sin[:], io["sin"]),
                             (m["qw1"][:], io["qw1"]), (m["qw2"][:], io["qw2"]),
                             (w_pe1[:], io["w_pe"][0:P, :]), (w_pe2[:], io["w_pe"][P:QR, :]),
                             (m["kw"][:], io["kw"])):
                sp.dma_start(dst, src).then_inc(loads, 16)

        @block.tensor
        def _(pe):
            pe.wait_ge(loads, 16 * n_loads)

            def project(t):
                wait(pe, tok_ready, t - 1)
                for k in range(ND):
                    last = nc.tensor.matmul(down[t % 2][:, 0:QR + CR + ROPE], hT[:, k, t * P:(t + 1) * P],
                                            w_a[:, k, :], start=k == 0, stop=k == ND - 1)
                last.then_inc(down_ready, 1)

            def turn(t):
                pe.wait_ge(tok_ready, t + 1)
                wait(pe, turned_used, t - 1)
                nc.tensor.transpose(turned[t % 2][:, 0, :], qn[:, t % 2, 0:P], ident[:])
                nc.tensor.transpose(turned[t % 2][0:QR - P, 1, :], qn[:, t % 2, P:QR], ident[:])
                nc.tensor.transpose(turned[t % 2][:, 2, :], ck[:, t % 2, 0:P], ident[:])
                nc.tensor.transpose(turned[t % 2][:, 3, :], ck[:, t % 2, CR:CR + P], ident[:]).then_inc(turned_ready, 1)

            project(0)
            for t in range(NT):
                if t + 1 < NT:
                    project(t + 1)
                turn(t)

            def rotary(n):
                t, c = divmod(n, NCH)
                pe.wait_ge(turned_used, t + 1)
                wait(pe, pq_used, n - 1)
                nc.tensor.matmul(pq[n % 2][:], m["qnT1"][:, t * P:(t + 1) * P], w_pe1[:, c * BANK:(c + 1) * BANK],
                                 start=True, stop=False)
                nc.tensor.matmul(pq[n % 2][:], m["qnT2"][:, t * P:(t + 1) * P], w_pe2[:, c * BANK:(c + 1) * BANK],
                                 start=False, stop=True).then_inc(pq_ready, 1)

            def turn_pe(n):
                t, c = divmod(n, NCH)
                pe.wait_ge(pe_ready, n + 1)
                wait(pe, pt_used, n - 1)
                for a in range(4):
                    last = nc.tensor.transpose(turned[n % 2][:, a, :], q_pe[:, n % 4, a * P:(a + 1) * P], ident[:])
                last.then_inc(pt_ready, 1)

            pe.wait_ge(turned_used, NT)
            for n in range(NT * NCH):
                rotary(n)
                if n >= 2:
                    turn_pe(n - 2)
            turn_pe(NT * NCH - 2)
            turn_pe(NT * NCH - 1)

        @block.scalar
        def _(act):
            act.wait_ge(loads, 16 * n_loads)
            act.wait_ge(consts, 1)

            def norms(t):
                act.wait_ge(down_ready, t + 1)
                nc.scalar.activation(squares[:], down[t % 2][:, 0:QR], ACT.Square,
                                     accum_out=ssq[:, t % 2, 0:1]).then_inc(ssq_ready, 1)
                act.wait_ge(ssq_ready, 2 * t + 1)
                nc.scalar.activation(squares[:, 0:CR], down[t % 2][:, QR:QR + CR], ACT.Square,
                                     accum_out=ssq[:, t % 2, 1:2]).then_inc(ssq_ready, 1)
                act.wait_ge(ssq_ready, 2 * t + 2)
                nc.scalar.activation(std[:, t % 2, 0:1], ssq[:, t % 2, 0:1], ACT.Sqrt, scale=1.0 / QR,
                                     bias=eps[:, 0:1])
                nc.scalar.activation(std[:, t % 2, 1:2], ssq[:, t % 2, 1:2], ACT.Sqrt, scale=1.0 / CR,
                                     bias=eps[:, 0:1]).then_inc(std_ready, 1)

            norms(0)
            for t in range(NT):
                if t + 1 < NT:
                    norms(t + 1)
                act.wait_ge(turned_ready, t + 1)
                tt = slice(t * P, (t + 1) * P)
                nc.scalar.mul(m["qnT1"][:, tt], turned[t % 2][:, 0, :], m["qw1"][:, 0:1])
                nc.scalar.mul(m["qnT2"][:, tt], turned[t % 2][0:QR - P, 1, :], m["qw2"][:, 0:1])
                nc.scalar.mul(kt32[:, 0, tt], turned[t % 2][:, 2, :], m["kw"][:, 0:1])
                nc.scalar.mul(kt32[:, 1, tt], turned[t % 2][:, 3, :], m["kw"][:, 1:2]).then_inc(turned_used, 1)
            act.wait_ge(turned_used, NT)
            for e in range(2):
                nc.scalar.copy(m["kt_hi"][e][:], kt32[:, e, :]).then_inc(kt_hi, 1)
            for n in range(NT * NCH):
                t, c = divmod(n, NCH)
                act.wait_ge(pt_ready, n + 1)
                nc.scalar.copy(m["peT"][:, 4 * c:4 * c + 4, t * P:(t + 1) * P], turned[n % 2][:]).then_inc(pt_used, 1)

        @block.vector
        def _(dve):
            done = [0]

            def then(instruction):
                done[0] += 1
                instruction.then_inc(dve_done, 1)
                dve.wait_ge(dve_done, done[0])

            nc.vector.memset(eps[:], RMS_EPS).then_inc(consts, 1)
            dve.wait_ge(loads, 16 * n_loads)

            def rotate(dst_a, dst_b, src, heads, t):
                pairs = lambda ap: ap.rearrange("p (h i two) -> p h i two", h=heads, two=2)
                table = lambda tab: tab[:, t, :].unsqueeze(1).to_broadcast([P, heads, ROPE])
                s4 = lambda tab: table(tab).rearrange("p h (i two) -> p h i two", two=2)
                nc.vector.tensor_tensor(dst_a.rearrange("p (h r) -> p h r", h=heads), src.rearrange("p (h r) -> p h r", h=heads),
                                        table(cos), ALU.mult)
                nc.vector.tensor_tensor(pairs(dst_b)[:, :, :, 0], pairs(src)[:, :, :, 1], s4(sin)[:, :, :, 0], ALU.mult)
                return nc.vector.tensor_tensor(pairs(dst_b)[:, :, :, 1], pairs(src)[:, :, :, 0], s4(sin)[:, :, :, 1],
                                               ALU.mult)

            for t in range(NT):
                dve.wait_ge(std_ready, t + 1)
                wait(dve, turned_ready, t - 1)
                then(nc.vector.reciprocal(rstd[:, t % 2, :], std[:, t % 2, :]))
                then(rotate(rope_k[:, 0, :], rope_k[:, 1, :], down[t % 2][:, QR + CR:QR + CR + ROPE], 1, t))
                nc.vector.tensor_tensor(ck[:, t % 2, CR:2 * CR], rope_k[:, 0, :], rope_k[:, 1, :], ALU.add)
                latent = down[t % 2][:, QR:QR + CR].unsqueeze(1).to_broadcast([P, 2, CR])
                outer = lambda ap: ap.rearrange("p (a c) -> p a c", c=CR)[:, 0:3:2, :]
                nc.vector.tensor_scalar(outer(ck[:, t % 2, :]), latent, rstd[:, t % 2, 1:2], None, ALU.mult)
                then(nc.vector.tensor_scalar(qn[:, t % 2, :], down[t % 2][:, 0:QR], rstd[:, t % 2, 0:1], MLA_SCALE,
                                             ALU.mult, ALU.mult))
                then(nc.vector.tensor_copy(m["values"][:, t, 0:CR], ck[:, t % 2, 0:CR]))
                nc.vector.tensor_tensor(m["values"][:, t, CR:2 * CR], ck[:, t % 2, 0:CR],
                                        m["values"][:, t, 0:CR].bitcast(F32), ALU.subtract).then_inc(tok_ready, 1)
            for e in range(2):
                dve.wait_ge(kt_hi, e + 1)
                nc.vector.tensor_tensor(m["kt_lo"][e][:], kt32[:, e, :], m["kt_hi"][e][:].bitcast(F32), ALU.subtract)
            for n in range(NT * NCH):
                t, c = divmod(n, NCH)
                dve.wait_ge(pq_ready, n + 1)
                wait(dve, pe_ready, n - 1)
                rotate(rope_a[:, n % 2, :], rope_b[:, n % 2, :], pq[n % 2][:], HPC, t).then_inc(pq_used, 1)

        @block.gpsimd
        def _(pool):
            for n in range(NT * NCH):
                t, c = divmod(n, NCH)
                pool.wait_ge(pq_used, n + 1)
                wait(pool, pt_ready, n - 3)
                dst = q_pe[:, n % 4, :].rearrange("p (a two r) -> p a two r", two=2, r=ROPE)
                view = lambda ap: ap.rearrange("p (a two r) -> p a two r", two=2, r=ROPE)
                a, b = view(rope_a[:, n % 2, :]), view(rope_b[:, n % 2, :])
                nc.gpsimd.tensor_tensor(dst[:, :, 0, :], a[:, :, 1, :], b[:, :, 1, :], ALU.add)
                nc.gpsimd.tensor_tensor(dst[:, :, 1, :], a[:, :, 0, :], b[:, :, 0, :], ALU.add).then_inc(pe_ready, 1)


def mla_heads(nc, io, ident, m):
    with ExitStack() as ctx:
        sem = lambda n: ctx.enter_context(nc.semaphore(f"mh_{n}"))
        sb = lambda n, s, d=F32: ctx.enter_context(nc.sbuf_tensor(f"mh_{n}", s, d))
        w = sb("w", [P, PACK])
        w_q = w[:, 0:2 * QR].rearrange("p (e r) -> p e r", e=2)
        w_k = w[:, 2 * QR:2 * QR + 2 * CR].rearrange("p (e c) -> p e c", e=2)
        w_v = w[:, 2 * QR + 2 * CR:2 * QR + 4 * CR].rearrange("p (e c) -> p e c", e=2)
        w_o = w[:, 2 * QR + 4 * CR:PACK].rearrange("p (e n) -> p e n", e=2)
        absorbed1, absorbed2 = sb("absorbed1", [P, 2 * CR]), sb("absorbed2", [QR - P, 2 * CR])
        q32 = [sb(f"q32_{e}", [P, S]) for e in range(2)]
        q_hi = [sb(f"q_hi{e}", [P, S], F32R) for e in range(2)]
        q_lo = [sb(f"q_lo{e}", [P, S], F32R) for e in range(2)]
        minus_max = sb("minus_max", [P, 2, NT])
        probs = sb("probs", [P, 2, S])
        turned_hi = sb("turned_hi", [P, 2, NT, 2 * P], F32R)
        turned_lo = sb("turned_lo", [P, 2, NT, 2 * P], F32R)
        lower_mix = sb("lower_mix", [P, 2, 2 * P])
        mask, ident_bf, mask_f = sb("mask", [P, P], BF16), sb("ident_bf", [P, P], BF16), sb("mask_f", [P, P])
        score_ps = [ctx.enter_context(nc.psum_tensor(f"mh_score{i}", [P, S], F32)) for i in range(2)]
        turn_ps = [ctx.enter_context(nc.psum_tensor(f"mh_turn{i}", [P, 4, P], F32)) for i in range(2)]
        mix_ps = ctx.enter_context(nc.psum_tensor("mh_mix", [P, 2 * P], F32))
        prep_ps = ctx.enter_context(nc.psum_tensor("mh_prep", [P, BANK], F32))
        consts, mask_in = sem("consts"), sem("mask_in")
        w_in, pe_in = sem("w_in"), [sem(f"pe_in{e}") for e in range(2)]
        prep_ready, prep_used = sem("prep_ready"), sem("prep_used")
        hi_ready, lo_ready = sem("hi_ready"), sem("lo_ready")
        scores_ready, max_ready, probs_ready = sem("scores_ready"), sem("max_ready"), sem("probs_ready")
        turns_ready, turn_hi_ready, turn_lo_ready = sem("turns_ready"), sem("turn_hi_ready"), sem("turn_lo_ready")
        mix_ready, lower_ready, out_ready = sem("mix_ready"), sem("lower_ready"), sem("out_ready")
        block = ctx.enter_context(nc.Block())

        TURNS = [(t, range(j, min(j + 4, t + 1))) for t in range(NT) for j in range(0, t + 1, 4)]
        NTURN = len(TURNS)
        turns_of = lambda t: [g for g in range(NTURN) if TURNS[g][0] == t]
        turns_to = lambda t: sum(x[0] <= t for x in TURNS)

        def looped(engine, body, first=1, end=PAIRS - 1):
            for i in range(first):
                body(i)
            with engine.Fori(first, end) as i:
                body(i)
            for i in range(end, PAIRS):
                body(i)

        is_last = lambda i: isinstance(i, int) and i == PAIRS - 1
        head = lambda i, e: 2 * i + e
        follows = lambda i, e: None if is_last(i) and e == 1 else (i, 1) if e == 0 else (i + 1, 0)
        before = lambda i, e: (i, 0) if e == 1 else None if isinstance(i, int) and i == 0 else (i - 1, 1)

        def split_rows(e):
            return (slice(0, CR), slice(CR, P)) if e == 0 else (slice(CR, P), slice(0, CR))

        @block.sync
        def _(sp):
            sp.dma_start(mask_f[:], io["mask"]).then_inc(mask_in, 16)

            def load_weights(i):
                wait(sp, prep_ready, 4 * i - 2)
                sp.dma_start(w[:], io["w_pairs"][bass.ds(i * P, P), :]).then_inc(w_in, 16)

            def load_rotary(i, e):
                wait(sp, lo_ready, 2 * i + e - 1)
                rows = split_rows(e)[1]
                sp.dma_start(q32[e][rows, :], m["peT"][rows, i, :]).then_inc(pe_in[e], 16)

            def step(i, more_weights):
                load_rotary(i + 1, 0)
                load_rotary(i + 1, 1)
                if more_weights:
                    load_weights(i + 2)

            load_weights(0)
            load_rotary(0, 0)
            load_rotary(0, 1)
            load_weights(1)
            step(0, True)
            with sp.Fori(1, PAIRS - 2) as i:
                step(i, True)
            step(PAIRS - 2, False)

        @block.tensor
        def _(pe):
            def prep_absorb(i):
                wait(pe, w_in, 16 * (i + 1))
                wait(pe, prep_used, 4 * i)
                for e in range(2):
                    nc.tensor.matmul(prep_ps[:, e * CR:(e + 1) * CR], w_q[:, e, 0:P], w_k[:, e, :], start=True, stop=True)
                    last = nc.tensor.matmul(prep_ps[0:QR - P, P + e * CR:P + (e + 1) * CR], w_q[:, e, P:QR], w_k[:, e, :],
                                            start=True, stop=True)
                last.then_inc(prep_ready, 1)

            def prep_output(i):
                wait(pe, prep_used, 4 * i + 1)
                for e in range(2):
                    last = nc.tensor.matmul(prep_ps[e * CR:(e + 1) * CR, :], w_v[:, e, :], w_o[:, e, :], start=True, stop=True)
                last.then_inc(prep_ready, 1)

            def prep_queries(i, half):
                wait(pe, prep_used, 4 * i + 2 + half)
                h = slice(half * BANK, (half + 1) * BANK)
                nc.tensor.matmul(prep_ps[:], absorbed1[:], m["qnT1"][:, h], start=True, stop=False)
                nc.tensor.matmul(prep_ps[:], absorbed2[:], m["qnT2"][:, h], start=False, stop=True).then_inc(prep_ready, 1)

            def scores(i, e, t):
                if t == 0:
                    wait(pe, lo_ready, head(i, e) + 1)
                wait(pe, probs_ready, NT * head(i, e) + t - 1)
                q = slice(t * P, (t + 1) * P)
                for k0, k1, base in score_pieces(t):
                    out, k = score_ps[t % 2][:, base + k0:base + k1], slice(k0, k1)
                    diagonal = k1 == (t + 1) * P
                    nc.tensor.matmul(out, q_hi[e][:, q], m["kt_hi"][e][:, k], start=True, stop=False)
                    nc.tensor.matmul(out, q_hi[e][:, q], m["kt_lo"][e][:, k], start=False, stop=False)
                    last = nc.tensor.matmul(out, q_lo[e][:, q], m["kt_hi"][e][:, k], start=False, stop=not diagonal)
                    if diagonal:
                        last = nc.tensor.matmul(score_ps[t % 2][:, base + k1 - P:base + k1], ident_bf[:], mask[:],
                                                start=False, stop=True)
                last.then_inc(scores_ready, 1)

            def turn(i, e, t):
                wait(pe, probs_ready, NT * head(i, e) + t + 1)
                for g in turns_of(t):
                    wait(pe, turn_lo_ready, NTURN * head(i, e) + g - 1)
                    for n, j in enumerate(TURNS[g][1]):
                        last = nc.tensor.transpose(turn_ps[g % 2][:, n, :], probs[:, t % 2, j * P:(j + 1) * P], ident[:])
                    last.then_inc(turns_ready, 1)

            def mix(i, e, pair):
                wait(pe, turn_lo_ready, NTURN * head(i, e) + turns_to(2 * pair + 1))
                wait(pe, out_ready, 4 * head(i, e) + pair)
                for j in range(2 * pair + 2):
                    q0 = P if j == 2 * pair + 1 else 0
                    for part in (turned_hi, turned_lo):
                        last = nc.tensor.matmul(mix_ps[:, q0:2 * P], m["values"][:, j, :], part[:, pair % 2, j, q0:2 * P],
                                                start=j == 0 and part is turned_hi,
                                                stop=j == 2 * pair + 1 and part is turned_lo)
                last.then_inc(mix_ready, 1)

            def slot(i, e):
                for t in range(NT):
                    if t in (0, 2) and before(i, e):
                        mix(*before(i, e), 2 + t // 2)
                    if t in (4, 6):
                        mix(i, e, t // 2 - 2)
                    if not is_last(i):
                        if (e, t) == (0, 1):
                            prep_absorb(i + 1)
                        if (e, t) == (0, 3):
                            prep_output(i + 1)
                        if (e, t) == (0, 7):
                            prep_queries(i + 1, 0)
                        if (e, t) == (1, 1):
                            prep_queries(i + 1, 1)
                    if t + 2 < NT:
                        scores(i, e, t + 2)
                    elif follows(i, e):
                        scores(*follows(i, e), t + 2 - NT)
                    turn(i, e, t)

            pe.wait_ge(consts, 2)
            prep_absorb(0)
            prep_output(0)
            prep_queries(0, 0)
            prep_queries(0, 1)
            scores(0, 0, 0)
            scores(0, 0, 1)

            def body(i):
                slot(i, 0)
                slot(i, 1)
            looped(pe, body)
            mix(PAIRS - 1, 1, 2)
            mix(PAIRS - 1, 1, 3)

        @block.scalar
        def _(act):
            def take_absorbed(i):
                wait(act, prep_ready, 4 * i + 1)
                nc.scalar.copy(absorbed1[:], prep_ps[:, 0:P])
                nc.scalar.copy(absorbed2[:], prep_ps[0:QR - P, P:2 * P]).then_inc(prep_used, 1)

            def take_output(i):
                wait(act, prep_ready, 4 * i + 2)
                nc.scalar.mul(m["w_out"][:, bass.ds(i, 1), :].rearrange("p a n -> p (a n)"), prep_ps[:], m["kw2"][:, 0:1]
                              ).then_inc(prep_used, 1)

            def take_queries(i, half):
                wait(act, prep_ready, 4 * i + 3 + half)
                if half == 0:
                    wait(act, lo_ready, 2 * i)
                h = slice(half * BANK, (half + 1) * BANK)
                for e in range(2):
                    rows = split_rows(e)[0]
                    last = nc.scalar.copy(q32[e][rows, h], prep_ps[rows, :])
                last.then_inc(prep_used, 1)

            def upper(i, e):
                wait(act, scores_ready, NT * (head(i, e) - 1))
                if e == 0:
                    wait(act, prep_used, 4 * i + 4)
                wait(act, pe_in[e], 16 * (i + 1))
                nc.scalar.copy(q_hi[e][:], q32[e][:]).then_inc(hi_ready, 1)

            def exp(i, e, t):
                wait(act, max_ready, NT * head(i, e) + t + 1)
                wait(act, turns_ready, NTURN * (head(i, e) - 1) + turns_to(NT - 2 + t) if t < 2 else
                     NTURN * head(i, e) + turns_to(t - 2))
                base, width = score_pieces(t)[0][2], (t + 1) * P
                nc.scalar.activation(probs[:, t % 2, 0:width], score_ps[t % 2][:, base:base + width], ACT.Exp,
                                     bias=minus_max[:, e, t:t + 1],
                                     accum_out=m["sums"][:, bass.ds(head(i, e), 1), t:t + 1].rearrange("p a b -> p (a b)")
                                     ).then_inc(probs_ready, 1)

            def turned_upper(i, e, t):
                pair, half = t // 2 % 2, t % 2
                for g in turns_of(t):
                    wait(act, turns_ready, NTURN * head(i, e) + g + 1)
                    wait(act, mix_ready, 4 * head(i, e) + t // 2 - 1)
                    j = TURNS[g][1]
                    nc.scalar.copy(turned_hi[:, pair, j[0]:j[-1] + 1, half * P:(half + 1) * P], turn_ps[g % 2][:, 0:len(j), :]
                                   ).then_inc(turn_hi_ready, 1)

            def take_lower(i, e, pair):
                wait(act, mix_ready, 4 * head(i, e) + pair + 1)
                wait(act, out_ready, 4 * head(i, e) + pair - 1)
                nc.scalar.copy(lower_mix[CR:P, pair % 2, :], mix_ps[CR:P, :]).then_inc(lower_ready, 1)

            def slot(i, e):
                for t in range(NT):
                    exp(i, e, t)
                    if t:
                        turned_upper(i, e, t - 1)
                    elif before(i, e):
                        turned_upper(*before(i, e), NT - 1)
                    if t in (1, 3) and before(i, e):
                        take_lower(*before(i, e), 2 + t // 2)
                    if t in (5, 7):
                        take_lower(i, e, t // 2 - 2)
                    if not is_last(i):
                        if (e, t) == (0, 2):
                            take_absorbed(i + 1)
                        if (e, t) == (0, 4):
                            take_output(i + 1)
                        if (e, t) == (1, 0):
                            take_queries(i + 1, 0)
                        if (e, t) == (1, 2):
                            take_queries(i + 1, 1)
                    if t == 4 and follows(i, e):
                        upper(*follows(i, e))

            take_absorbed(0)
            take_output(0)
            take_queries(0, 0)
            take_queries(0, 1)
            upper(0, 0)

            def body(i):
                slot(i, 0)
                slot(i, 1)
            looped(act, body)
            turned_upper(PAIRS - 1, 1, NT - 1)
            take_lower(PAIRS - 1, 1, 2)
            take_lower(PAIRS - 1, 1, 3)

        @block.vector
        def _(dve):
            dve.wait_ge(mask_in, 16)
            nc.vector.tensor_copy(mask[:], mask_f[:]).then_inc(consts, 1)
            nc.vector.tensor_copy(ident_bf[:], ident[:]).then_inc(consts, 1)

            def lower(i, e):
                wait(dve, hi_ready, head(i, e) + 1)
                nc.vector.tensor_tensor(q_lo[e][:], q32[e][:], q_hi[e][:].bitcast(F32), ALU.subtract).then_inc(lo_ready, 1)

            def take_max(i, e, t):
                wait(dve, scores_ready, NT * head(i, e) + t + 1)
                base, width = score_pieces(t)[0][2], (t + 1) * P
                nc.vector.reduce_max(minus_max[:, e, t:t + 1], score_ps[t % 2][:, base:base + width], AX.X, negate=True
                                     ).then_inc(max_ready, 1)

            def turned_lower(i, e, t):
                pair, half = t // 2 % 2, t % 2
                for g in turns_of(t):
                    wait(dve, turn_hi_ready, NTURN * head(i, e) + g + 1)
                    j = TURNS[g][1]
                    place = (slice(None), pair, slice(j[0], j[-1] + 1), slice(half * P, (half + 1) * P))
                    nc.vector.tensor_tensor(turned_lo[place], turn_ps[g % 2][:, 0:len(j), :], turned_hi[place].bitcast(F32),
                                            ALU.subtract).then_inc(turn_lo_ready, 1)

            def join(i, e, pair):
                wait(dve, lower_ready, 4 * head(i, e) + pair + 1)
                rows = split_rows(e)[0]
                out = m["peT"][rows, bass.ds(i, 1), pair * 2 * P:(pair + 1) * 2 * P].rearrange("p a n -> p (a n)")
                nc.vector.tensor_tensor(out, mix_ps[0:CR, :], lower_mix[CR:P, pair % 2, :], ALU.add
                                        ).then_inc(out_ready, 1)

            def slot(i, e):
                for t in range(NT):
                    if t + 1 < NT:
                        take_max(i, e, t + 1)
                    elif follows(i, e):
                        take_max(*follows(i, e), 0)
                    if t:
                        turned_lower(i, e, t - 1)
                    elif before(i, e):
                        turned_lower(*before(i, e), NT - 1)
                    if t in (1, 3) and before(i, e):
                        join(*before(i, e), 2 + t // 2)
                    if t in (5, 7):
                        join(i, e, t // 2 - 2)
                    if t == 4 and follows(i, e):
                        lower(*follows(i, e))

            lower(0, 0)
            take_max(0, 0, 0)

            def body(i):
                slot(i, 0)
                slot(i, 1)
            looped(dve, body)
            turned_lower(PAIRS - 1, 1, NT - 1)
            join(PAIRS - 1, 1, 2)
            join(PAIRS - 1, 1, 3)


def score_pieces(t):
    n = (t + 1) * P
    if n <= BANK:
        return [(0, n, 0)]
    if n == BANK + P:
        return [(0, BANK - P, P), (BANK - P, n, P)]
    return [(0, BANK, 0), (BANK, n, 0)]


def mla_output(nc, io, load, ident, mixed, w_out, sums, x_dram_out, hT_dram, out_dram):
    with ExitStack() as ctx:
        sem = lambda n: ctx.enter_context(nc.semaphore(f"mo_{n}"))
        sb = lambda n, s, d=F32: ctx.enter_context(nc.sbuf_tensor(f"mo_{n}", s, d))
        w_hi, w_lo = sb("w_hi", [P, PAIRS, D], F32R), sb("w_lo", [P, PAIRS, D], F32R)
        with ExitStack() as part:
            inverse = part.enter_context(nc.sbuf_tensor("mo_inverse", [P, H, NT], F32))
            rows_hi = part.enter_context(nc.sbuf_tensor("mo_rows_hi", [H, S], F32R))
            rows_lo = part.enter_context(nc.sbuf_tensor("mo_rows_lo", [H, S], F32R))
            spread_f = part.enter_context(nc.sbuf_tensor("mo_spread_f", [H, PAIRS, P], F32))
            spread = part.enter_context(nc.sbuf_tensor("mo_spread", [H, PAIRS, P], F32R))
            rows_ps = part.enter_context(nc.psum_tensor("mo_rows_ps", [P, S], F32))
            ps = [part.enter_context(nc.psum_tensor(f"mo_ps{i}", [P, BANK], F32)) for i in range(4)]
            names = ("spread_in", "spread_set", "inverse_ready", "rows_ready", "hi_ready", "lo_ready", "spreads", "used",
                     "w_hi_ready")
            spread_in, spread_set, inverse_ready, rows_ready, hi_ready, lo_ready, spreads, used, w_hi_ready = (
                part.enter_context(nc.semaphore(f"mo_{n}")) for n in names)
            block = part.enter_context(nc.Block())
            QUARTER = PAIRS // 4

            @block.sync
            def _(sp):
                sp.dma_start(spread_f[:], io["spread_mla"]).then_inc(spread_in, 16)

            @block.tensor
            def _(pe):
                pe.wait_ge(inverse_ready, 1)
                for t in range(NT):
                    last = nc.tensor.transpose(rows_ps[0:H, t * P:(t + 1) * P], inverse[:, :, t], ident[:])
                last.then_inc(rows_ready, 1)
                pe.wait_ge(lo_ready, 1)
                pe.wait_ge(spread_set, 1)
                for n in range(PAIRS * NHALF):
                    i, half = n // NHALF, n % NHALF
                    h = slice(half * BANK, (half + 1) * BANK)
                    wait(pe, used, n - 3)
                    nc.tensor.matmul(ps[n % 4][:], spread[:, i, :], rows_hi[:, h], start=True, stop=False)
                    nc.tensor.matmul(ps[n % 4][:], spread[:, i, :], rows_lo[:, h], start=False, stop=True).then_inc(spreads, 1)

            @block.scalar
            def _(act):
                act.wait_ge(spread_in, 16)
                nc.scalar.copy(spread[:], spread_f[:]).then_inc(spread_set, 1)
                act.wait_ge(rows_ready, 1)
                nc.scalar.copy(rows_hi[:], rows_ps[0:H, :]).then_inc(hi_ready, 1)
                for n in range(4):
                    quarter = slice(n * QUARTER, (n + 1) * QUARTER)
                    nc.scalar.copy(w_hi[:, quarter, :], w_out[:, quarter, :]).then_inc(w_hi_ready, 1)

            @block.vector
            def _(dve):
                nc.vector.reciprocal(inverse[:], sums[:]).then_inc(inverse_ready, 1)
                dve.wait_ge(hi_ready, 1)
                nc.vector.tensor_tensor(rows_lo[:], rows_ps[0:H, :], rows_hi[:].bitcast(F32), ALU.subtract).then_inc(lo_ready, 1)
                for n in range(PAIRS * NHALF):
                    i, half = n // NHALF, n % NHALF
                    o = mixed[:, i, half * BANK:(half + 1) * BANK]
                    dve.wait_ge(spreads, n + 1)
                    nc.vector.tensor_tensor(o, o, ps[n % 4][:], ALU.mult).then_inc(used, 1)
                for n in range(4):
                    quarter = slice(n * QUARTER, (n + 1) * QUARTER)
                    dve.wait_ge(w_hi_ready, n + 1)
                    nc.vector.tensor_tensor(w_lo[:, quarter, :], w_out[:, quarter, :], w_hi[:, quarter, :].bitcast(F32),
                                            ALU.subtract)

        x = w_out[:, 0:NT, :]
        hT = w_out[:, NT:2 * NT, :].rearrange("p a n -> p (a n)").rearrange("p (k s) -> p k s", k=ND)
        a_hi, a_lo = sb("a_hi", [P, 2, PAIRS, P], F32R), sb("a_lo", [P, 2, PAIRS, P], F32R)
        a_hi_ready, a_lo_ready, used = sem("a_hi_ready"), sem("a_lo_ready"), sem("a_used")

        def scalar_work(act, t):
            wait(act, used, t - 1)
            nc.scalar.copy(a_hi[:, t % 2, :, :], mixed[:, :, t * P:(t + 1) * P]).then_inc(a_hi_ready, 1)

        def vector_work(dve, t):
            dve.wait_ge(a_hi_ready, t + 1)
            nc.vector.tensor_tensor(a_lo[:, t % 2, :, :], mixed[:, :, t * P:(t + 1) * P],
                                    a_hi[:, t % 2, :, :].bitcast(F32), ALU.subtract).then_inc(a_lo_ready, 1)

        def project(pe, t, out):
            pe.wait_ge(a_lo_ready, t + 1)
            products = [(a, w, i) for i in range(PAIRS) for a, w in ((a_hi, w_hi), (a_hi, w_lo), (a_lo, w_hi))]
            for n, (a, w, i) in enumerate(products):
                last = nc.tensor.matmul(out[:], a[:, t % 2, i, :], w[:, i, :], start=n == 0, stop=n == len(products) - 1)
            return last
        norm_block(nc, "n1", x, None if out_dram is not None else hT, ident, project=project, x_dram=io["x"],
                   scalar_work=scalar_work, vector_work=vector_work, out_dram=out_dram, projected=used)
        if out_dram is None:
            load((x_dram_out.rearrange("(t p) d -> p t d", p=P), x),
                 (hT_dram, w_out[:, NT:2 * NT, :].rearrange("p a n -> p (a n)")))


def normalise(nc, name, out, sums_src, sums_dram_waits, select, n, io_select):
    with ExitStack() as ctx:
        sem = lambda s: ctx.enter_context(nc.semaphore(f"{name}_{s}"))
        sums = ctx.enter_context(nc.sbuf_tensor(f"{name}_sums", [H, S], F32))
        inverse = ctx.enter_context(nc.sbuf_tensor(f"{name}_inverse", [H, S], F32))
        spread = ctx.enter_context(nc.sbuf_tensor(f"{name}_spread", [H, n, P], F32))
        ps = [ctx.enter_context(nc.psum_tensor(f"{name}_ps{i}", [P, BANK], F32)) for i in range(4)]
        loads, inverse_ready, spread_ready, used = sem("loads"), sem("inverse_ready"), sem("spread_ready"), sem("used")
        block = ctx.enter_context(nc.Block())
        n_loads = len(sums_src(sums)) + 1

        @block.sync
        def _(sp):
            sp.dma_start(spread[:], io_select).then_inc(loads, 16)
            for dst, src in sums_src(sums):
                sp.dma_start(dst, src).then_inc(loads, 16)

        @block.tensor
        def _(pe):
            pe.wait_ge(inverse_ready, 1)
            for i in range(n):
                for half in range(NHALF):
                    k = NHALF * i + half
                    wait(pe, used, k - 3)
                    nc.tensor.matmul(ps[k % 4][:], spread[:, i, :], inverse[:, half * BANK:(half + 1) * BANK],
                                     start=True, stop=True).then_inc(spread_ready, 1)

        @block.vector
        def _(dve):
            dve.wait_ge(loads, 16 * n_loads)
            nc.vector.reciprocal(inverse[:], sums[:]).then_inc(inverse_ready, 1)
            for i in range(n):
                for half in range(NHALF):
                    k = NHALF * i + half
                    o = out[:, i, half * BANK:(half + 1) * BANK]
                    dve.wait_ge(spread_ready, k + 1)
                    nc.vector.tensor_tensor(o, o, ps[k % 4][:], ALU.mult).then_inc(used, 1)


def ffn_inner(nc, io, hT_dram, x, d, down_hi, down_lo):
    with ExitStack() as ctx:
        sem = lambda s: ctx.enter_context(nc.semaphore(f"ff_{s}"))
        sb = lambda n, s, dt=F32: ctx.enter_context(nc.sbuf_tensor(f"ff_{n}", s, dt))
        hT_hi, hT_lo = sb("hT_hi", [P, ND, S], F32R), sb("hT_lo", [P, ND, S], F32R)
        w = x[:, 0:6, :].rearrange("p a n -> p (a n)").rearrange("p (a n) -> p a n", a=2)
        gated = x[:, 6:8, :]
        w_hi, w_lo = sb("w_hi", [P, 2, 2 * D], F32R), sb("w_lo", [P, 2, 2 * D], F32R)
        sides = sb("sides", [96, SIDES], F32R)
        sv_now = sb("sv_now", [96, 2, P], F32R)
        hT = d[:, NI - ND:NI, :]
        sides_f = d[0:96, 0:7, :].rearrange("p a n -> p (a n)")[:, 0:SIDES]
        su = [sides[:, n * INNER:(n + 1) * INNER] for n in range(2)]
        su_down = sides[:, 2 * INNER:RIGHT]
        sv = [sides[:, RIGHT + n * D:RIGHT + (n + 1) * D] for n in range(2)]
        sv_down = sides[:, RIGHT + 2 * D:SIDES]
        scale_ps = ctx.enter_context(nc.psum_tensor("ff_scale", [P, 3 * D], F32))
        gate_ps = [ctx.enter_context(nc.psum_tensor(f"ff_gate{i}", [P, BANK], F32)) for i in range(2)]
        up_ps = [ctx.enter_context(nc.psum_tensor(f"ff_up{i}", [P, BANK], F32)) for i in range(2)]
        cleared, sides_in, hT_in = sem("cleared"), sem("sides_in"), sem("hT_in")
        w_in = [sem(f"w_in{i}") for i in range(2)]
        sides_hi, sides_ready, hT_hi_ready, hT_ready = (sem(s) for s in ("sides_hi", "sides_ready", "hT_hi_ready", "hT_ready"))
        sv_ready, scale_ready, scaled, hi_ready, split = (sem(s) for s in ("sv_ready", "scale_ready", "scaled", "hi_ready", "split"))
        gate_ready, up_ready, gated_ready, d_ready = sem("gate_ready"), sem("up_ready"), sem("gated_ready"), sem("d_ready")
        block = ctx.enter_context(nc.Block())
        half_of = lambda h: slice(h * BANK, (h + 1) * BANK)
        last = NI // 2 - 1

        def looped(engine, body):
            body(0, 0)
            body(1, 1)
            with engine.Fori(1, last) as r:
                body(2 * r, 0)
                body(2 * r + 1, 1)
            body(2 * last, 0)
            body(2 * last + 1, 1)

        is_last = lambda it, back=1: isinstance(it, int) and it >= NI - back
        times = lambda it, a: it // 2 + 1 if isinstance(it, int) else (it - a) // 2 + 1

        @block.sync
        def _(sp):
            def load(it, a, count=None):
                wait(sp, split, it - 1)
                sp.dma_start(w[:, a, :], io["w_inner"][bass.ds(it * P, P), :]).then_inc(w_in[a], 16)

            sp.wait_ge(cleared, 1)
            for part in range(3):
                sp.dma_start(sides_f[32 * part:32 * part + RANK, :], io["sides"]).then_inc(sides_in, 16)
            load(0, 0)
            sp.dma_start(hT.rearrange("p k s -> p (k s)"), hT_dram).then_inc(hT_in, 16)
            load(1, 1)

            def body(it, a):
                if not is_last(it, 2):
                    load(it + 2, a)
            looped(sp, body)

        @block.tensor
        def _(pe):
            def scales(it, a):
                wait(pe, scaled, it)
                wait(pe, sv_ready, it + 1)
                for n in range(2):
                    for k in range(ND):
                        nc.tensor.matmul(scale_ps[:, n * D + k * P:n * D + (k + 1) * P], sv[n][:, k * P:(k + 1) * P],
                                         su[n][:, bass.ds(it * P, P)], start=True, stop=True)
                nc.tensor.matmul(scale_ps[:, 2 * D:3 * D], sv_now[:, a, :], su_down, start=True, stop=True
                                 ).then_inc(scale_ready, 1)

            def products(it, a):
                wait(pe, split, it + 1)
                for half in range(NHALF):
                    wait(pe, d_ready, 2 * it + half - 1)
                    for n, (out, ready) in enumerate(((gate_ps, gate_ready), (up_ps, up_ready))):
                        for k in range(ND):
                            cols = slice(n * D + k * P, n * D + (k + 1) * P)
                            for m, (weights, h) in enumerate(((w_hi, hT_hi), (w_hi, hT_lo), (w_lo, hT_hi))):
                                final = nc.tensor.matmul(out[half][:], weights[:, a, cols], h[:, k, half_of(half)],
                                                         start=k == 0 and m == 0, stop=k == ND - 1 and m == 2)
                        final.then_inc(ready, 1)

            pe.wait_ge(sides_ready, 2)
            scales(0, 0)
            pe.wait_ge(hT_ready, NHALF)

            def body(it, a):
                if not is_last(it):
                    scales(it + 1, 1 - a)
                products(it, a)
            looped(pe, body)

        @block.scalar
        def _(act):
            def take_sv(it, a):
                wait(act, scale_ready, it - 1)
                nc.scalar.copy(sv_now[:, a, :], sv_down[:, bass.ds(it * P, P)].bitcast(F32)).then_inc(sv_ready, 1)

            def upper(it, a):
                wait(act, scaled, it + 1)
                wait(act, up_ready, 2 * it - 2)
                nc.scalar.copy(w_hi[:, a, :], w[:, a, 0:2 * D])
                nc.scalar.copy(down_hi[:, bass.ds(it, 1), :].rearrange("p a n -> p (a n)"), w[:, a, 2 * D:3 * D]
                               ).then_inc(hi_ready, 1)

            def gate(it, half):
                wait(act, gate_ready, 2 * it + half + 1)
                wait(act, d_ready, 2 * it + half - 1)
                nc.scalar.activation(gated[:, half, :], gate_ps[half][:], ACT.Silu).then_inc(gated_ready, 1)

            act.wait_ge(sides_in, 48)
            nc.scalar.copy(sides[:, 0:RIGHT], sides_f[:, 0:RIGHT]).then_inc(sides_hi, 1)
            nc.scalar.copy(sides[:, RIGHT:SIDES], sides_f[:, RIGHT:SIDES]).then_inc(sides_hi, 1)
            act.wait_ge(hT_in, 16)
            for half in range(NHALF):
                nc.scalar.copy(hT_hi[:, :, half_of(half)], hT[:, :, half_of(half)]).then_inc(hT_hi_ready, 1)
            act.wait_ge(sides_ready, 2)
            take_sv(0, 0)
            take_sv(1, 1)
            upper(0, 0)

            def body(it, a):
                if not is_last(it, 2):
                    take_sv(it + 2, a)
                gate(it, 0)
                if not is_last(it):
                    upper(it + 1, 1 - a)
                gate(it, 1)
            looped(act, body)

        @block.vector
        def _(dve):
            def scale(it, a):
                dve.wait_ge(w_in[a], 16 * times(it, a))
                wait(dve, scale_ready, it + 1)
                nc.vector.tensor_tensor(w[:, a, :], w[:, a, :], scale_ps[:], ALU.mult).then_inc(scaled, 1)

            def lower(it, a):
                wait(dve, hi_ready, it + 1)
                wait(dve, up_ready, 2 * it - 2)
                nc.vector.tensor_tensor(w_lo[:, a, :], w[:, a, 0:2 * D], w_hi[:, a, :].bitcast(F32), ALU.subtract)
                one = lambda m: m[:, bass.ds(it, 1), :].rearrange("p a n -> p (a n)")
                nc.vector.tensor_tensor(one(down_lo), w[:, a, 2 * D:3 * D], one(down_hi).bitcast(F32), ALU.subtract
                                        ).then_inc(split, 1)

            def join(it, half):
                wait(dve, gated_ready, 2 * it + half + 1)
                wait(dve, up_ready, 2 * it + half + 1)
                nc.vector.tensor_tensor(d[:, bass.ds(it, 1), half_of(half)].rearrange("p a n -> p (a n)"),
                                        gated[:, half, :], up_ps[half][:], ALU.mult).then_inc(d_ready, 1)

            nc.vector.memset(sides_f, 0.0).then_inc(cleared, 1)
            for n, (rows, cols) in enumerate(((slice(64, 96), slice(0, RIGHT)), (slice(32, 64), slice(RIGHT, SIDES)))):
                dve.wait_ge(sides_hi, n + 1)
                nc.vector.tensor_tensor(sides[rows, cols], sides_f[rows, cols], sides[rows, cols].bitcast(F32), ALU.subtract
                                        ).then_inc(sides_ready, 1)
            for half in range(NHALF):
                dve.wait_ge(hT_hi_ready, half + 1)
                nc.vector.tensor_tensor(hT_lo[:, :, half_of(half)], hT[:, :, half_of(half)],
                                        hT_hi[:, :, half_of(half)].bitcast(F32), ALU.subtract).then_inc(hT_ready, 1)
            scale(0, 0)
            lower(0, 0)

            def body(it, a):
                if not is_last(it):
                    scale(it + 1, 1 - a)
                join(it, 0)
                if not is_last(it):
                    lower(it + 1, 1 - a)
                join(it, 1)
            looped(dve, body)


def mha_inputs(nc, io, h, spare, w_hi, w_lo, hi, lo, scratch):
    with ExitStack() as ctx:
        sem = lambda s: ctx.enter_context(nc.semaphore(f"ai_{s}"))
        sb = lambda n, s, dt=F32: ctx.enter_context(nc.sbuf_tensor(f"ai_{n}", s, dt))
        w = [spare[:, 2 * c:2 * c + 2, :].rearrange("p a n -> p (a n)").rearrange("p (k n) -> p k n", k=ND) for c in range(3)]
        values = [spare[:, 6 + i, :].rearrange("p (h r) -> p h r", h=H) for i in range(2)]
        full = spare[:, 8:10, :].rearrange("p a n -> p (a n)").rearrange("p (a n) -> p a n", n=BANK)
        bias_qk, bias_v = sb("bias_qk", [P, 2 * ND]), sb("bias_v", [P, D])
        ps = [ctx.enter_context(nc.psum_tensor(f"ai_ps{i}", [P, BANK], F32)) for i in range(4)]
        w_in, bias_in = [sem(f"w_in{c}") for c in range(3)], sem("bias_in")
        w_hi_ready, w_ready, ones_set, ready, full_ready, hi_ready, lo_ready = (sem(s) for s in (
            "w_hi_ready", "w_ready", "ones_set", "ready", "full_ready", "hi_ready", "lo_ready"))
        part_out, v_ready, v_out = [sem(f"part_out{i}") for i in range(3)], sem("v_ready"), [sem(f"v_out{i}") for i in range(2)]
        block = ctx.enter_context(nc.Block())
        NQK = 2 * ND * NHALF
        of = lambda part, c: part[:, ND * c:ND * (c + 1), :]

        @block.sync
        def _(sp):
            for c in range(3):
                sp.dma_start(w[c], io["qkv_w"][:, :, c * D:(c + 1) * D]).then_inc(w_in[c], 16)
                if c == 0:
                    for dst, src in ((bias_qk[:], io["bias_qk"]), (bias_v[:], io["bias_v"])):
                        sp.dma_start(dst, src).then_inc(bias_in, 16)
            for n in range(NQK):
                blk, half = divmod(n, NHALF)
                for part, buf, done in ((0, hi, hi_ready), (1, lo, lo_ready)):
                    sp.wait_ge(done, n + 1)
                    sp.dma_start(scratch["qk"][part, blk * P:(blk + 1) * P, half * BANK:(half + 1) * BANK],
                                 buf[:, n % 3, :].bitcast(F32)
                                 ).then_inc(part_out[n % 3], 16)
            for t in range(NT):
                sp.wait_ge(v_ready, t + 1)
                sp.dma_start(scratch["v"][t * P:(t + 1) * P, :], values[t % 2].rearrange("p h r -> p (h r)")
                             ).then_inc(v_out[t % 2], 16)
            for i in range(3):
                sp.wait_ge(part_out[i], 32 * len(range(i, NQK, 3)))
            for i in range(2):
                sp.wait_ge(v_out[i], 16 * NT // 2)

        @block.tensor
        def _(pe):
            for n in range(NQK + NT):
                wait(pe, full_ready, min(n - 3, NQK))
                wait(pe, v_ready, n - 3 - NQK)
                blk, half = divmod(n, NHALF)
                c = blk // ND if n < NQK else 2
                pe.wait_ge(w_ready, c + 1)
                for k in range(ND):
                    for m, (a, b) in enumerate(((0, 0), (0, 1), (1, 0))):
                        weights = of((w_hi, w_lo)[a], c)
                        if n < NQK:
                            left, right = weights[:, k, blk % ND * P:(blk % ND + 1) * P], h[b][:, k, half * BANK:(half + 1) * BANK]
                        else:
                            left, right = h[b][:, k, (n - NQK) * P:(n - NQK + 1) * P], weights[:, k, :]
                        last = nc.tensor.matmul(ps[n % 4][:], left, right, start=k == 0 and m == 0, stop=k == ND - 1 and m == 2)
                last.then_inc(ready, 1)

        @block.scalar
        def _(act):
            def upper(c):
                act.wait_ge(w_in[c], 16)
                nc.scalar.copy(of(w_hi, c), w[c]).then_inc(w_hi_ready, 1)

            upper(0)
            act.wait_ge(bias_in, 32)
            for n in range(NQK):
                blk = n // NHALF
                if n in (1, 3):
                    upper((n + 1) // 2)
                act.wait_ge(ready, n + 1)
                wait(act, lo_ready, n - 2)
                nc.scalar.activation(full[:, n % 3, :], ps[n % 4][:], ACT.Identity, bias=bias_qk[:, blk:blk + 1]
                                     ).then_inc(full_ready, 1)

        @block.vector
        def _(dve):
            def lower(c):
                dve.wait_ge(w_hi_ready, c + 1)
                nc.vector.tensor_tensor(of(w_lo, c), w[c], of(w_hi, c).bitcast(F32), ALU.subtract).then_inc(w_ready, 1)

            for v in values:
                nc.vector.memset(v[:, :, HD:2 * HD], 1.0).then_inc(ones_set, 1)
            lower(0)
            for n in range(NQK):
                if n in (1, 3):
                    lower((n + 1) // 2)
                dve.wait_ge(full_ready, n + 1)
                if n >= 3:
                    dve.wait_ge(part_out[n % 3], 32 * (n // 3))
                nc.vector.tensor_copy(hi[:, n % 3, :], full[:, n % 3, :]).then_inc(hi_ready, 1)
                dve.wait_ge(hi_ready, n + 1)
                nc.vector.tensor_tensor(lo[:, n % 3, :], full[:, n % 3, :], hi[:, n % 3, :].bitcast(F32), ALU.subtract
                                        ).then_inc(lo_ready, 1)
            dve.wait_ge(bias_in, 32)
            dve.wait_ge(ones_set, 2)
            for t in range(NT):
                dve.wait_ge(ready, NQK + t + 1)
                if t >= 2:
                    dve.wait_ge(v_out[t % 2], 16 * (t // 2))
                nc.vector.tensor_tensor(values[t % 2][:, :, 0:HD], ps[(NQK + t) % 4][:].rearrange("p (h r) -> p h r", h=H),
                                        bias_v[:].rearrange("p (h r) -> p h r", h=H), ALU.add).then_inc(v_ready, 1)


def mha_heads(nc, io, ident, scratch, out):
    with ExitStack() as ctx:
        sem = lambda s: ctx.enter_context(nc.semaphore(f"ah_{s}"))
        sb = lambda n, s, dt=F32: ctx.enter_context(nc.sbuf_tensor(f"ah_{n}", s, dt))
        MAX_ROW = 3 * HD
        q_stack = [sb(f"q_stack{i}", [P, 4, S], F32R) for i in range(2)]
        k_stack = [sb(f"k_stack{i}", [P, 4, S], F32R) for i in range(2)]
        v = [sb(f"v{i}", [P, NT, 4 * 2 * HD]) for i in range(2)]
        zero_one = sb("zero_one", [1, 2, 4 * S], F32R)
        half_max, row_max = sb("half_max", [P, 4, NT, 2]), sb("row_max", [P, 4 * NT])
        minus_max = sb("minus_max", [4 * NT, P], F32R)
        probs = sb("probs", [P, 4, 2 * BANK])
        ring = [ctx.enter_context(nc.psum_tensor(f"ah_ring{i}", [P, BANK], F32)) for i in range(3)]
        score_ps = [ctx.enter_context(nc.psum_tensor(f"ah_score{i}", [P, 2, BANK], F32)) for i in range(2)]
        mix_ps = ctx.enter_context(nc.psum_tensor("ah_mix", [P, BANK], F32))
        cleared, rows_set = sem("cleared"), sem("rows_set")
        stacks_in = [sem(f"stacks_in{i}") for i in range(2)]
        v_in = [sem(f"v_in{i}") for i in range(2)]
        max_ready, max_taken, row_max_ready, turned, minus_ready, max_row_in = (sem(s) for s in (
            "max_ready", "max_taken", "row_max_ready", "turned", "minus_ready", "max_row_in"))
        scores_ready, probs_ready, mixed, out_taken = (sem(s) for s in ("scores_ready", "probs_ready", "mixed", "out_taken"))
        dve_done = sem("dve_done")
        block = ctx.enter_context(nc.Block())
        NUNIT = NHALF * NT
        NMAX = 4 * NT * 2
        turn_ps = ring[NMAX % 3]
        qk_rows = scratch["qk"].rearrange("part (kind h d) s -> part kind d h s", kind=2, d=HD)
        v_rows = scratch["v"].rearrange("(t p) n -> p t n", p=P)

        def looped(engine, body):
            body(0)
            with engine.Fori(1, GROUPS // 2 - 1) as r:
                body(r)
            body(GROUPS // 2 - 1)

        more = lambda r, a: not (isinstance(r, int) and r == GROUPS // 2 - 1 and a == 1)

        @block.sync
        def _(sp):
            def load(r, a):
                g = 2 * r + a
                wait(sp, mixed, NUNIT * (g - 1))
                heads = bass.ds(4 * g, 4)
                for kind, stack, parts in ((0, q_stack[a], (0, 0, 1)), (1, k_stack[a], (0, 1, 0))):
                    for n, part in enumerate(parts):
                        sp.dma_start(stack[n * HD:(n + 1) * HD, :, :].bitcast(F32), qk_rows[part, kind, :, heads, :]).then_inc(stacks_in[a], 16)
                sp.dma_start(q_stack[a][MAX_ROW:MAX_ROW + 1, :, :].bitcast(F32), zero_f32r[0]).then_inc(stacks_in[a], 16)
                sp.dma_start(v[a][:], v_rows[:, :, bass.ds(4 * g * 2 * HD, 4 * 2 * HD)]).then_inc(v_in[a], 16)

            def put_max(r, a):
                g = 2 * r + a
                wait(sp, minus_ready, g + 1)
                sp.dma_start(q_stack[a][MAX_ROW:MAX_ROW + 1, :, :].rearrange("p h (t q) -> p (h t) q", q=P).bitcast(F32),
                             minus_max[:].bitcast(F32)).then_inc(max_row_in, 16)

            sp.wait_ge(cleared, 6)
            zero_f32r = [zero_one[:, i, :].rearrange("p (h s) -> p h s", h=4).bitcast(F32) for i in range(2)]
            for a in range(2):
                sp.dma_start(k_stack[a][MAX_ROW:MAX_ROW + 1, :, :].bitcast(F32), zero_f32r[1]).then_inc(rows_set, 16)
            load(0, 0)
            load(0, 1)
            put_max(0, 0)

            def body(r):
                for a in range(2):
                    if more(r, a):
                        put_max(*((r, 1) if a == 0 else (r + 1, 0)))
                    if not (isinstance(r, int) and r == GROUPS // 2 - 1):
                        load(r + 1, a)
            looped(sp, body)

        @block.tensor
        def _(pe):
            def maximum(r, a, n):
                g = 2 * r + a
                t, head, half = n // 8, n // 2 % 4, n % 2
                if n == 0:
                    wait(pe, stacks_in[a], 16 * 7 * (r + 1))
                if n == 1:
                    wait(pe, minus_ready, g)
                else:
                    wait(pe, max_taken, NMAX * g + max(n - 2, 0))
                nc.tensor.matmul(ring[n % 3][:], q_stack[a][:, head, t * P:(t + 1) * P],
                                 k_stack[a][:, head, half * BANK:(half + 1) * BANK], start=True, stop=True
                                 ).then_inc(max_ready, 1)

            def turn_max(r, a):
                g = 2 * r + a
                wait(pe, row_max_ready, g + 1)
                nc.tensor.transpose(turn_ps[0:4 * NT, 0:P], row_max[:], ident[:]).then_inc(turned, 1)

            def scores(r, a, u, pair):
                g = 2 * r + a
                half, j = divmod(u, NT)
                if u == 0 and pair == 0:
                    wait(pe, max_row_in, 16 * (g + 1))
                wait(pe, probs_ready, 2 * (NUNIT * g + u) + pair - 1)
                for e in range(2):
                    head = 2 * pair + e
                    last = nc.tensor.matmul(score_ps[pair][:, e, :], k_stack[a][:, head, j * P:(j + 1) * P],
                                            q_stack[a][:, head, half * BANK:(half + 1) * BANK], start=True, stop=True)
                last.then_inc(scores_ready, 1)

            def mix(r, a, u):
                g = 2 * r + a
                half, j = divmod(u, NT)
                if u == 0:
                    wait(pe, v_in[a], 16 * (r + 1))
                if j == 0:
                    wait(pe, out_taken, NHALF * g + half)
                wait(pe, probs_ready, 2 * (NUNIT * g + u + 1))
                for head in range(4):
                    rows = slice(32 * head, 32 * head + 32)
                    last = nc.tensor.matmul(mix_ps[rows, :], v[a][:, j, rows],
                                            probs[:, 2 * (u % 2) + head // 2, (head % 2) * BANK:(head % 2 + 1) * BANK],
                                            start=j == 0, stop=j == NT - 1)
                last.then_inc(mixed, 1)

            def slot(r, a):
                nxt = (r, 1) if a == 0 else (r + 1, 0)
                n = [0]

                def some_maxima(count):
                    for _ in range(min(count, NMAX - n[0]) if more(r, a) else 0):
                        maximum(*nxt, n[0])
                        n[0] += 1

                for u in range(NUNIT):
                    scores(r, a, u, 0)
                    some_maxima(1 if u else 0)
                    scores(r, a, u, 1)
                    some_maxima(1 if u else 0)
                    if u:
                        mix(r, a, u - 1)
                    some_maxima(3 if u % 4 == 1 else 2 if u else 0)
                mix(r, a, NUNIT - 1)
                if more(r, a):
                    turn_max(*nxt)

            pe.wait_ge(rows_set, 32)
            for n in range(NMAX):
                maximum(0, 0, n)
            turn_max(0, 0)

            def body(r):
                slot(r, 0)
                slot(r, 1)
            looped(pe, body)

        @block.scalar
        def _(act):
            def take_turned(r, a):
                g = 2 * r + a
                wait(act, turned, g + 1)
                wait(act, max_row_in, 16 * g)
                nc.scalar.mul(minus_max[:], turn_ps[0:4 * NT, 0:P], -1.0).then_inc(minus_ready, 1)

            def take_out(r, a, half):
                g = 2 * r + a
                wait(act, mixed, NUNIT * g + NT * (half + 1))
                nc.scalar.copy(out[:, bass.ds(g, 1), half * BANK:(half + 1) * BANK].rearrange("p a n -> p (a n)"), mix_ps[:]
                               ).then_inc(out_taken, 1)

            def exp(r, a, u, pair):
                g = 2 * r + a
                wait(act, scores_ready, 2 * (NUNIT * g + u) + pair + 1)
                wait(act, mixed, NUNIT * g + u - 1)
                nc.scalar.activation(probs[:, 2 * (u % 2) + pair, :], score_ps[pair][:].rearrange("p e n -> p (e n)"),
                                     ACT.Exp, scale=MHA_SCALE).then_inc(probs_ready, 1)

            def slot(r, a):
                for u in range(NUNIT):
                    exp(r, a, u, 0)
                    exp(r, a, u, 1)
                    if u == NT:
                        take_out(r, a, 0)
                take_out(r, a, 1)
                if more(r, a):
                    take_turned(*((r, 1) if a == 0 else (r + 1, 0)))

            take_turned(0, 0)

            def body(r):
                slot(r, 0)
                slot(r, 1)
            looped(act, body)

        @block.vector
        def _(dve):
            for stack in (*q_stack, *k_stack):
                nc.vector.memset(stack[:].bitcast(F32), 0.0).then_inc(cleared, 1)
            for i, value in enumerate((0.0, 1.0)):
                nc.vector.memset(zero_one[:, i, :].bitcast(F32), value).then_inc(cleared, 1)

            def take_max(r, a, n):
                g = 2 * r + a
                t, head, half = n // 8, n // 2 % 4, n % 2
                wait(dve, max_ready, NMAX * g + n + 1)
                nc.vector.reduce_max(half_max[:, head, t, half:half + 1], ring[n % 3][:], AX.X).then_inc(max_taken, 1)

            def join_max(r, a):
                g = 2 * r + a
                wait(dve, turned, g)
                wait(dve, max_taken, NMAX * (g + 1))
                flat = half_max[:].rearrange("p h t two -> p (h t) two")
                nc.vector.tensor_tensor(row_max[:], flat[:, :, 0], flat[:, :, 1], ALU.max).then_inc(row_max_ready, 1)

            def group(r, a):
                for n in range(NMAX):
                    take_max(r, a, n)
                join_max(r, a)

            group(0, 0)

            def body(r):
                group(r, 1)
                if more(r, 1):
                    group(r + 1, 0)
            looped(dve, body)


def dequantise(nc, io, w):
    with ExitStack() as ctx:
        sem = lambda s: ctx.enter_context(nc.semaphore(f"dq_{s}"))
        sb = lambda n, s, dt=F32: ctx.enter_context(nc.sbuf_tensor(f"dq_{n}", s, dt))
        q, zeros, scales = sb("q", [P, ND, D], I32), sb("zeros", [P, ND, D]), sb("scales", [P, ND, D])
        loads, done = sem("loads"), sem("done")
        block = ctx.enter_context(nc.Block())
        per_tile = P // QGROUP

        @block.sync
        def _(sp):
            sp.dma_start(q[:], io["qweight"].rearrange("(k p) o -> p k o", p=P)).then_inc(loads, 16)
            for dst, src in ((zeros, io["zeros"]), (scales, io["scales"])):
                grouped = src.rearrange("(k g) o -> g k o", g=per_tile)
                for g in range(per_tile):
                    sp.dma_start(dst[g * QGROUP:(g + 1) * QGROUP, :, :],
                                 grouped[g:g + 1, :, :].to_broadcast([QGROUP, ND, D])).then_inc(loads, 16)

        @block.vector
        def _(dve):
            dve.wait_ge(loads, 16 * (1 + 2 * per_tile))
            nc.vector.tensor_copy(w[:], q[:]).then_inc(done, 1)
            dve.wait_ge(done, 1)
            nc.vector.tensor_tensor(w[:], w[:], zeros[:], ALU.subtract).then_inc(done, 1)
            dve.wait_ge(done, 2)
            nc.vector.tensor_tensor(w[:], w[:], scales[:], ALU.mult).then_inc(done, 1)


class Loads:

    def __init__(self, nc, semaphore):
        self.nc, self.semaphore, self.count = nc, semaphore, 0

    def __call__(self, *pairs):
        with self.nc.Block() as block:
            @block.sync
            def _(sp):
                for dst, src in pairs:
                    sp.dma_start(dst, src).then_inc(self.semaphore, 16)
                    self.count += 16
                sp.wait_ge(self.semaphore, self.count)


def two_layers(nc, io, out_dram, upto=4):
    with ExitStack() as ctx:
        sb = lambda n, s, dt=F32: ctx.enter_context(nc.sbuf_tensor(n, s, dt))
        ident = sb("ident", [P, P])
        x_dram_out = nc.dram_tensor("x_scratch", (S, D), F32, kind="Internal").ap()
        hT_dram = nc.dram_tensor("hT_scratch", (P, ND * S), F32, kind="Internal").ap()
        scratch = {"qk": nc.dram_tensor("qk_scratch", (2, 2 * D, S), F32, kind="Internal").ap(),
                   "v": nc.dram_tensor("v_scratch", (S, H * 2 * HD), F32, kind="Internal").ap()}
        load = Loads(nc, ctx.enter_context(nc.semaphore("loads")))
        load((ident[:], io["ident"]))

        with ExitStack() as layer:
            sb = lambda n, s, dt=F32: layer.enter_context(nc.sbuf_tensor(n, s, dt))
            peT = sb("peT", [P, PAIRS, S])
            w_out = sb("w_out", [P, PAIRS, D])
            sums = sb("sums", [P, H, NT])
            with ExitStack() as part:
                sb = lambda n, s, dt=F32: part.enter_context(nc.sbuf_tensor(n, s, dt))
                m = {"peT": peT, "w_out": w_out, "sums": sums,
                     "qnT1": sb("qnT1", [P, S]), "qnT2": sb("qnT2", [QR - P, S]),
                     "kt_hi": [sb(f"kt_hi{e}", [P, S], F32R) for e in range(2)],
                     "kt_lo": [sb(f"kt_lo{e}", [P, S], F32R) for e in range(2)],
                     "values": sb("values", [P, NT, 2 * CR], F32R), "qw1": sb("qw1", [P, 1]), "qw2": sb("qw2", [QR - P, 1]),
                     "kw": sb("kw", [P, 2]), "kw2": sb("kw2", [P, 1])}
                load((m["kw2"][:], io["kw2"]))
                hT = w_out[:, 0:ND * S // D, :].rearrange("p a n -> p (a n)").rearrange("p (k s) -> p k s", k=ND)
                with nc.sbuf_tensor("x_first", [P, NT, D], F32) as x:
                    norm_block(nc, "n0", x, hT, ident, x_dram=io["x"])
                mla_inputs(nc, io, hT, ident, m)
                mla_heads(nc, io, ident, m)
            mla_output(nc, io, load, ident, peT, w_out, sums, x_dram_out, hT_dram, out_dram if upto == 1 else None)
            if upto == 1:
                return

        x = ctx.enter_context(nc.sbuf_tensor("x", [P, NT, D], F32))
        with ExitStack() as layer:
            sb = lambda n, s, dt=F32: layer.enter_context(nc.sbuf_tensor(n, s, dt))
            d = sb("d", [P, NI, S])
            down_hi, down_lo = sb("down_hi", [P, NI, D], F32R), sb("down_lo", [P, NI, D], F32R)
            ffn_inner(nc, io, hT_dram, x, d, down_hi, down_lo)

            h = (sb("h_hi", [P, ND, S], F32R), sb("h_lo", [P, ND, S], F32R))
            d_hi, d_lo = sb("d_hi", [P, 2, NI, P], F32R), sb("d_lo", [P, 2, NI, P], F32R)
            d_hi_ready, d_lo_ready, used = (layer.enter_context(nc.semaphore(f"fp_{n}")) for n in ("d_hi", "d_lo", "used"))

            def scalar_work(act, t):
                wait(act, used, t - 1)
                nc.scalar.copy(d_hi[:, t % 2, :, :], d[:, :, t * P:(t + 1) * P]).then_inc(d_hi_ready, 1)

            def vector_work(dve, t):
                dve.wait_ge(d_hi_ready, t + 1)
                nc.vector.tensor_tensor(d_lo[:, t % 2, :, :], d[:, :, t * P:(t + 1) * P],
                                        d_hi[:, t % 2, :, :].bitcast(F32), ALU.subtract).then_inc(d_lo_ready, 1)

            def project(pe, t, out):
                pe.wait_ge(d_lo_ready, t + 1)
                products = [(a, w, i) for i in range(NI) for a, w in ((d_hi, down_hi), (d_hi, down_lo), (d_lo, down_hi))]
                for n, (a, w, i) in enumerate(products):
                    last = nc.tensor.matmul(out[:], a[:, t % 2, i, :], w[:, i, :], start=n == 0, stop=n == len(products) - 1)
                return last
            works = dict(x_dram=x_dram_out, project=project, scalar_work=scalar_work, vector_work=vector_work, projected=used)
            if upto == 2:
                norm_block(nc, "n2", x, None, ident, out_dram=out_dram, **works)
                return
            norm_block(nc, "n2", x, h, ident, **works)
            ring = lambda part: part[:].rearrange("p a k n -> p (a k n)")[:, 0:3 * BANK].rearrange("p (a n) -> p a n", n=BANK)
            mha_inputs(nc, io, h, d, down_hi, down_lo, ring(d_hi), ring(d_lo), scratch)

        with ExitStack() as layer:
            sb = lambda n, s, dt=F32: layer.enter_context(nc.sbuf_tensor(n, s, dt))
            mixed, w_out = sb("mha_mixed", [P, GROUPS, S]), sb("w_out_mha", [P, GROUPS, D])
            load((w_out[:], io["o_w"]))
            mha_heads(nc, io, ident, scratch, mixed)
            normalise(nc, "an", mixed, lambda sums: [
                (sums[g * GROUPS:(g + 1) * GROUPS, :], mixed[32 * g + HD:32 * g + HD + 1, :, :]) for g in range(4)],
                None, io["spread_mha"], GROUPS, io["spread_mha"])

            def project(pe, t, out):
                for i in range(GROUPS):
                    last = nc.tensor.matmul(out[:], mixed[:, i, t * P:(t + 1) * P], w_out[:, i, :], start=i == 0,
                                            stop=i == GROUPS - 1)
                return last
            if upto == 3:
                norm_block(nc, "n3", x, None, ident, project=project, out_dram=out_dram)
                return
            hT, w, bias, ones = sb("hT3", [P, ND, S]), sb("w_lin", [P, ND, D]), sb("bias_lin", [1, D]), sb("ones_lin", [1, P])
            norm_block(nc, "n3", x, hT, ident, project=project)
            dequantise(nc, io, w)
            load((bias[:], io["lin_bias"]), (ones[:], io["ones"]))

            def project(pe, t, out):
                for k in range(ND):
                    nc.tensor.matmul(out[:], hT[:, k, t * P:(t + 1) * P], w[:, k, :], start=k == 0, stop=False)
                return nc.tensor.matmul(out[:], ones[:], bias[:], start=False, stop=True)
            norm_block(nc, "n4", x, None, ident, project=project, out_dram=out_dram)


def layouts(i):
    import numpy as np
    c = np.ascontiguousarray
    a = {k: np.asarray(v) for k, v in i.items()}
    wq = a["L0_attn_Wq_b"].reshape(QR, H, NOPE + ROPE)
    wkv = a["L0_attn_Wkv_b"].reshape(CR, H, NOPE + VD)
    wo = a["L0_attn_Wo"].reshape(H, VD, D)
    by_pair = lambda m: m.reshape(PAIRS, 2, P, -1).transpose(0, 2, 1, 3).reshape(PAIRS, P, -1)
    packed = [by_pair(m) for m in (wq[:, :, :NOPE].transpose(1, 2, 0), wkv[:, :, :NOPE].transpose(1, 2, 0),
                                   wkv[:, :, NOPE:].transpose(1, 2, 0), wo)]
    qw, kw = a["L0_attn_q_a_ln_w"], a["L0_attn_kv_a_ln_w"]
    one = np.ones((CR,), np.float32)
    w_a = np.concatenate([a["L0_attn_Wq_a"], a["L0_attn_Wkv_a"]], 1)
    angle_f = np.float32(1.0) / np.float32(10000.0) ** (np.arange(0, ROPE, 2, dtype=np.float32) / np.float32(ROPE))
    angle = np.outer(np.arange(S, dtype=np.float32), angle_f.astype(np.float32)).astype(np.float32)
    cos = np.repeat(np.cos(angle), 2, 1).astype(np.float32)
    sin = np.repeat(np.sin(angle), 2, 1).astype(np.float32) * np.tile(np.array([-1, 1], np.float32), ROPE // 2)
    by_tile = lambda m: c(m.reshape(-1, P, m.shape[1]).transpose(1, 0, 2))
    inner = lambda k: a[k].T.reshape(ND, P, NI, P).transpose(2, 1, 0, 3).reshape(NI, P, D)
    below = np.arange(P)[:, None] < np.arange(P)[None, :]
    mask = np.where(below, np.float32(-1e30), np.float32(0))
    rows = np.arange(P)
    spread_mla = np.zeros((H, PAIRS, P), np.float32)
    for n in range(PAIRS):
        spread_mla[2 * n + rows // CR, n, rows] = 1
    spread_mha = np.zeros((H, GROUPS, P), np.float32)
    for n in range(GROUPS):
        spread_mha[(rows // 32) * GROUPS + n, n, rows] = 1
    o_w = np.zeros((4, 32, GROUPS, D), np.float32)
    o_w[:, :HD] = a["L1_attn_attn_ow"].reshape(GROUPS, 4, HD, D).transpose(1, 2, 0, 3)
    o_w[0, HD, 0] = a["L1_attn_attn_ob"]
    qkv_b = a["L1_attn_attn_qkvb"]
    return {
        "x": c(a["L0_attn_hidden_states"].reshape(S, D)), "ident": np.eye(P, dtype=np.float32),
        "w_a": by_tile(w_a), "cos": by_tile(cos), "sin": by_tile(sin),
        "qw1": c(qw[:P, None]), "qw2": c(qw[P:, None]), "kw2": c(np.concatenate([kw, kw])[:, None]),
        "kw": c(np.stack([np.concatenate([kw, one]), np.concatenate([one, kw])], 1)),
        "w_pe": c(wq[:, :, NOPE:].reshape(QR, H * ROPE)),
        "w_pairs": c(np.concatenate(packed, 2).reshape(PAIRS * P, PACK)),
        "mask": mask, "spread_mla": spread_mla, "spread_mha": spread_mha,
        "w_inner": c(np.concatenate([inner("L0_ffn_gate_w"), inner("L0_ffn_up_w"),
                                     a["L0_ffn_down_w"].T.reshape(NI, P, D)], 2).reshape(NI * P, 3 * D)),
        "sides": c(np.concatenate([a["L0_ffn_gate_su"].T, a["L0_ffn_up_su"].T, a["L0_ffn_down_su"].T,
                                   a["L0_ffn_gate_sv"], a["L0_ffn_up_sv"], a["L0_ffn_down_sv"]], 1)),
        "qkv_w": by_tile(a["L1_attn_attn_qkvw"]), "bias_qk": c(qkv_b[:2 * D].reshape(2 * ND, P).T),
        "bias_v": c(np.broadcast_to(qkv_b[None, 2 * D:], (P, D))), "o_w": c(o_w.reshape(P, GROUPS, D)),
        "qweight": c(a["L1_ffn_qweight"].T),
        "zeros": c(a["L1_ffn_zeros"].reshape(D, -1).T), "scales": c(a["L1_ffn_scales"].reshape(D, -1).T),
        "lin_bias": c(a["L1_ffn_bias"][None, :]), "ones": np.ones((1, P), np.float32),
    }


def kernel(**inputs):
    import concourse.bacc as bacc
    import numpy as np
    from concourse.bass_utils import run_bass_kernel_spmd

    nc = bacc.Bacc("TRN2", target_bir_lowering=False, num_devices=1)
    arrays = {f"in_{k}": v for k, v in layouts(inputs).items()}
    io = {k[3:]: nc.dram_tensor(k, v.shape, mybir.dt.from_np(v.dtype), kind="ExternalInput").ap() for k, v in arrays.items()}
    out = nc.dram_tensor("out", (S, D), F32, kind="ExternalOutput").ap()
    two_layers(nc, io, out)
    r = run_bass_kernel_spmd(nc, [arrays], core_ids=[0])
    return r.results[0]["out"].reshape(1, S, D)
```

```python
import concourse.bass as bass
from concourse import mybir
from contextlib import ExitStack

F32 = mybir.dt.float32
F32R = mybir.dt.float32r
BF16 = mybir.dt.bfloat16
I32 = mybir.dt.int32
ALU = mybir.AluOpType
ACT = mybir.ActivationFunctionType
AX = mybir.AxisListType

P = 128
S = 1024
D = 512
NT = S // P
ND = D // P
BANK = 512
NHALF = S // BANK
LN_EPS = 1e-5

H = 32
QR, CR = 192, 64
NOPE, ROPE, VD = 128, 64, 128
PAIRS = H // 2
RMS_EPS = 1e-6
MLA_SCALE = float((NOPE + ROPE) ** -0.5)
PACK = 2 * (2 * P + CR + CR + D)

INNER = 1792
NI = INNER // P
RANK = 4
RIGHT = 2 * INNER + D
SIDES = RIGHT + 2 * D + INNER

HD = 16
GROUPS = H // 4
MHA_SCALE = float(HD ** -0.5)

QGROUP = 32


def wait(engine, semaphore, value):
    if isinstance(value, int) and value <= 0:
        return
    engine.wait_ge(semaphore, value)


def norm_block(nc, name, x, hT, ident, project=None, out_dram=None, x_dram=None, scalar_work=None, vector_work=None,
               projected=None, hT_dram=None):
    with ExitStack() as ctx:
        sem = lambda n: ctx.enter_context(nc.semaphore(f"{name}_{n}"))
        sb = lambda n, s, d=F32: ctx.enter_context(nc.sbuf_tensor(f"{name}_{n}", s, d))
        var_ready, std_ready, dve_done = sem("var_ready"), sem("std_ready"), sem("dve_done")
        if project is not None:
            y_ready, y_used = projected or sem("y_ready"), sem("y_used")
        if hT is not None:
            h_ready, ht_ready, ht_used = sem("h_ready"), sem("ht_ready"), sem("ht_used")
            parts = isinstance(hT, tuple)
            hT_hi_ready = sem("hT_hi_ready") if parts else None
        if out_dram is not None:
            x_ready, x_out = sem("x_ready"), sem("x_out")
        if x_dram is not None:
            x_tiles = ((0, NT),) if project is not None else ((0, 1), (1, NT))
            x_in = [sem(f"x_in{n}") for n in range(len(x_tiles))]
        py = [ctx.enter_context(nc.psum_tensor(f"{name}_py{i}", [P, D], F32)) for i in range(2)]
        pt = [ctx.enter_context(nc.psum_tensor(f"{name}_pt{i}", [P, ND, P], F32)) for i in range(2)]
        stats, mv = sb("stats", [P, 2, 6]), sb("mv", [P, 2, 2])
        std, rstd = sb("std", [P, 2]), sb("rstd", [P, 2])
        eps = sb("eps", [P, 1])
        yn, hn = sb("yn", [P, D]), sb("hn", [P, 2, D])
        block = ctx.enter_context(nc.Block())
        norms = (project is not None) + (hT is not None)
        ahead = int(hT is not None and scalar_work is None)

        if x_dram is not None:
            @block.sync
            def _(sp):
                for n, (first, end) in enumerate(x_tiles):
                    sp.dma_start(x[:, first:end, :], x_dram[first * P:end * P, :].rearrange("(t p) d -> p t d", p=P)
                                 ).then_inc(x_in[n], 16)

        @block.tensor
        def _(pe):
            def transposes(t):
                pe.wait_ge(h_ready, t + 1)
                wait(pe, ht_used, t - 1)
                for k in range(ND):
                    last = nc.tensor.transpose(pt[t % 2][:, k, :], hn[:, t % 2, k * P:(k + 1) * P], ident[:])
                last.then_inc(ht_ready, 1)

            for t in range(NT):
                if project is not None:
                    wait(pe, y_used, t - 1)
                    project(pe, t, py[t % 2]).then_inc(y_ready, 1)
                if hT is not None and t:
                    transposes(t - 1)
            if hT is not None:
                transposes(NT - 1)

        @block.scalar
        def _(act):
            n = 0
            if scalar_work is not None:
                scalar_work(act, 0)
                scalar_work(act, 1)
            for t in range(NT):
                while n < min(norms * (t + 1) + ahead, norms * NT):
                    act.wait_ge(var_ready, n + 1)
                    nc.scalar.activation(std[:, n % 2:n % 2 + 1], mv[:, n % 2, 1:2], ACT.Sqrt,
                                         bias=eps[:, 0:1]).then_inc(std_ready, 1)
                    n += 1
                if scalar_work is not None and t + 2 < NT:
                    scalar_work(act, t + 2)
                if hT is not None:
                    act.wait_ge(ht_ready, t + 1)
                    nc.scalar.copy((hT[0] if parts else hT)[:, :, t * P:(t + 1) * P], pt[t % 2][:]
                                   ).then_inc(hT_hi_ready if parts else ht_used, 1)

        @block.vector
        def _(dve):
            done = [0]

            def then(instruction):
                done[0] += 1
                instruction.then_inc(dve_done, 1)
                dve.wait_ge(dve_done, done[0])

            def moments(n, src):
                then(nc.vector.bn_stats(stats[:, n % 2, :], src))
                nc.vector.bn_aggr(mv[:, n % 2, :], stats[:, n % 2, :]).then_inc(var_ready, 1)

            def reciprocal(n):
                dve.wait_ge(std_ready, n + 1)
                then(nc.vector.reciprocal(rstd[:, n % 2:n % 2 + 1], std[:, n % 2:n % 2 + 1]))

            def take_y(t):
                if project is not None:
                    dve.wait_ge(y_ready, t + 1)
                    moments(norms * t, py[t % 2][:])

            def take_x(t):
                if x_dram is not None:
                    dve.wait_ge(x_in[sum(t >= end for _, end in x_tiles)], 16)
                if project is not None:
                    n = norms * t
                    reciprocal(n)
                    nc.vector.tensor_scalar(yn[:], py[t % 2][:], mv[:, n % 2, 0:1], rstd[:, n % 2:n % 2 + 1],
                                            ALU.subtract, ALU.mult).then_inc(y_used, 1)
                    dve.wait_ge(y_used, t + 1)
                    sum_x = nc.vector.tensor_tensor(x[:, t, :], x[:, t, :], yn[:], ALU.add)
                    if out_dram is not None:
                        sum_x.then_inc(x_ready, 1)
                        dve.wait_ge(x_ready, t + 1)
                    else:
                        then(sum_x)
                if hT is not None:
                    moments(norms * (t + 1) - 1, x[:, t, :])

            def put_h(t):
                if hT is not None:
                    n = norms * (t + 1) - 1
                    reciprocal(n)
                    wait(dve, ht_ready, t - 1)
                    nc.vector.tensor_scalar(hn[:, t % 2, :], x[:, t, :], mv[:, n % 2, 0:1], rstd[:, n % 2:n % 2 + 1],
                                            ALU.subtract, ALU.mult).then_inc(h_ready, 1)

            def lower(t):
                dve.wait_ge(hT_hi_ready, t + 1)
                tokens = slice(t * P, (t + 1) * P)
                nc.vector.tensor_tensor(hT[1][:, :, tokens], pt[t % 2][:], hT[0][:, :, tokens].bitcast(F32), ALU.subtract
                                        ).then_inc(ht_used, 1)

            nc.vector.memset(eps[:], LN_EPS)
            if vector_work is not None:
                vector_work(dve, 0)
                vector_work(dve, 1)
            if ahead:
                take_y(0)
                if project is None:
                    take_x(0)
            for t in range(NT):
                if not ahead:
                    take_y(t)
                if not ahead or project is not None:
                    take_x(t)
                if ahead and t + 1 < NT:
                    take_y(t + 1) if project is not None else take_x(t + 1)
                put_h(t)
                if vector_work is not None and t + 2 < NT:
                    vector_work(dve, t + 2)
                if hT is not None and parts and t:
                    lower(t - 1)
            if hT is not None and parts:
                lower(NT - 1)

        if out_dram is not None:
            def store_hT(sp, t):
                sp.wait_ge(ht_used, t + 1)
                tokens = slice(t * P, (t + 1) * P)
                sp.dma_start(hT_dram[:, :, tokens], hT[:, :, tokens]).then_inc(x_out, 16)

            @block.sync
            def _(sp):
                for t in range(NT):
                    sp.wait_ge(x_ready, t + 1)
                    sp.dma_start(out_dram[t * P:(t + 1) * P, :], x[:, t, :]).then_inc(x_out, 16)
                    if hT_dram is not None and t:
                        store_hT(sp, t - 1)
                if hT_dram is not None:
                    store_hT(sp, NT - 1)
                sp.wait_ge(x_out, 16 * NT * (1 if hT_dram is None else 2))


def mla_inputs(nc, io, hT, ident, m):
    with ExitStack() as ctx:
        sem = lambda n: ctx.enter_context(nc.semaphore(f"mi_{n}"))
        sb = lambda n, s, d=F32: ctx.enter_context(nc.sbuf_tensor(f"mi_{n}", s, d))
        w_a = sb("w_a", [P, ND, QR + CR + ROPE])
        w_pe = m["peT"][:, 0:4, :].rearrange("p a n -> p (a n)").rearrange("p (a n) -> p a n", a=2)
        w_pe_hi, w_pe_lo = sb("w_pe_hi", [P, 2, H * ROPE], F32R), sb("w_pe_lo", [P, 2, H * ROPE], F32R)
        cos, sin = sb("cos", [P, NT, ROPE]), sb("sin", [P, NT, ROPE])
        squares = sb("squares", [P, QR])
        ssq, std, rstd = sb("ssq", [P, 2, 2]), sb("std", [P, 2, 2]), sb("rstd", [P, 2, 2])
        eps = sb("eps", [P, 1])
        qn = sb("qn", [P, 2, QR])
        ck = sb("ck", [P, 2, 3 * CR])
        rope_k = sb("rope_k", [P, 2, ROPE])
        rope_a, rope_b = sb("rope_a", [P, 2, BANK]), sb("rope_b", [P, 2, BANK])
        q_pe = sb("q_pe", [P, 4, BANK])
        full = m["w_out"][:, ND * S // D:2 * ND * S // D, :].rearrange("p a n -> p (a n)").rearrange("p (a n) -> p a n", n=S)
        kt32, qn32 = full[:, 0:2, :], full[:, 2:4, :]
        down = [ctx.enter_context(nc.psum_tensor(f"mi_down{i}", [P, BANK], F32)) for i in range(2)]
        turned = [ctx.enter_context(nc.psum_tensor(f"mi_turned{i}", [P, 4, P], F32)) for i in range(2)]
        pq = [ctx.enter_context(nc.psum_tensor(f"mi_pq{i}", [P, BANK], F32)) for i in range(2)]
        loads = sem("loads")
        down_ready = sem("down_ready")
        ssq_ready, std_ready = sem("ssq_ready"), sem("std_ready")
        tok_ready, turned_ready, turned_used = sem("tok_ready"), sem("turned_ready"), sem("turned_used")
        dve_done, parts_hi, parts_ready = sem("dve_done"), sem("parts_hi"), sem("parts_ready")
        w_hi_ready, w_ready = sem("w_hi_ready"), sem("w_ready")
        eps_set = w_ready
        pq_ready, pq_used = sem("pq_ready"), sem("pq_used")
        pe_ready, pt_ready, pt_used = sem("pe_ready"), sem("pt_ready"), sem("pt_used")
        block = ctx.enter_context(nc.Block())
        n_loads = 11
        NCH = H * ROPE // BANK
        HPC = BANK // ROPE

        @block.sync
        def _(sp):
            for dst, src in ((w_a[:], io["w_a"]), (cos[:], io["cos"]), (sin[:], io["sin"]),
                             (m["qw1"][:], io["qw1"]), (m["qw2"][:], io["qw2"]),
                             (w_pe[:, 0, :], io["w_pe"][0:P, :]), (w_pe[0:QR - P, 1, :], io["w_pe"][P:QR, :]),
                             (w_pe[QR - P:P, 1, :], io["w_pe"][P:QR, :]),
                             (m["kw"][:], io["kw"]), (m["kw2"][:], io["kw2"]), (m["mask"][:], io["mask"])):
                sp.dma_start(dst, src).then_inc(loads, 16)

        @block.tensor
        def _(pe):
            pe.wait_ge(loads, 16 * n_loads)

            def project(t):
                wait(pe, tok_ready, t - 1)
                for k in range(ND):
                    last = nc.tensor.matmul(down[t % 2][:, 0:QR + CR + ROPE], hT[:, k, t * P:(t + 1) * P],
                                            w_a[:, k, :], start=k == 0, stop=k == ND - 1)
                last.then_inc(down_ready, 1)

            def turn(t):
                pe.wait_ge(tok_ready, t + 1)
                wait(pe, turned_used, t - 1)
                nc.tensor.transpose(turned[t % 2][:, 0, :], qn[:, t % 2, 0:P], ident[:])
                nc.tensor.transpose(turned[t % 2][0:QR - P, 1, :], qn[:, t % 2, P:QR], ident[:])
                nc.tensor.transpose(turned[t % 2][:, 2, :], ck[:, t % 2, 0:P], ident[:])
                nc.tensor.transpose(turned[t % 2][:, 3, :], ck[:, t % 2, CR:CR + P], ident[:]).then_inc(turned_ready, 1)

            project(0)
            for t in range(NT):
                if t + 1 < NT:
                    project(t + 1)
                turn(t)

            def rotary(n):
                t, c = divmod(n, NCH)
                wait(pe, pq_used, n - 1)
                tokens, cols = slice(t * P, (t + 1) * P), slice(c * BANK, (c + 1) * BANK)
                for k, (q, weights) in enumerate((
                        (m["q1_hi"][:, tokens], w_pe_hi[:, 0, cols]), (m["q1_hi"][:, tokens], w_pe_lo[:, 0, cols]),
                        (m["q1_lo"][:, tokens], w_pe_hi[:, 0, cols]), (m["q2"][:, tokens], w_pe_hi[:, 1, cols]),
                        (m["q2"][0:QR - P, tokens], w_pe_lo[0:QR - P, 1, cols]))):
                    last = nc.tensor.matmul(pq[n % 2][:], q, weights, start=k == 0, stop=k == 4)
                last.then_inc(pq_ready, 1)

            def turn_pe(n):
                t, c = divmod(n, NCH)
                pe.wait_ge(pe_ready, n + 1)
                wait(pe, pt_used, n - 1)
                for a in range(4):
                    last = nc.tensor.transpose(turned[n % 2][:, a, :], q_pe[:, n % 4, a * P:(a + 1) * P], ident[:])
                last.then_inc(pt_ready, 1)

            pe.wait_ge(w_ready, 2)
            pe.wait_ge(parts_ready, NT)
            for n in range(NT * NCH):
                rotary(n)
                if n >= 2:
                    turn_pe(n - 2)
            turn_pe(NT * NCH - 2)
            turn_pe(NT * NCH - 1)

        @block.scalar
        def _(act):
            act.wait_ge(loads, 16 * n_loads)
            act.wait_ge(eps_set, 1)

            def norms(t):
                act.wait_ge(down_ready, t + 1)
                nc.scalar.activation(squares[:], down[t % 2][:, 0:QR], ACT.Square,
                                     accum_out=ssq[:, t % 2, 0:1]).then_inc(ssq_ready, 1)
                act.wait_ge(ssq_ready, 2 * t + 1)
                nc.scalar.activation(squares[:, 0:CR], down[t % 2][:, QR:QR + CR], ACT.Square,
                                     accum_out=ssq[:, t % 2, 1:2]).then_inc(ssq_ready, 1)
                act.wait_ge(ssq_ready, 2 * t + 2)
                nc.scalar.activation(std[:, t % 2, 0:1], ssq[:, t % 2, 0:1], ACT.Sqrt, scale=1.0 / QR,
                                     bias=eps[:, 0:1])
                nc.scalar.activation(std[:, t % 2, 1:2], ssq[:, t % 2, 1:2], ACT.Sqrt, scale=1.0 / CR,
                                     bias=eps[:, 0:1]).then_inc(std_ready, 1)

            nc.scalar.copy(w_pe_hi[:], w_pe).then_inc(w_hi_ready, 1)
            norms(0)
            for t in range(NT):
                if t + 1 < NT:
                    norms(t + 1)
                act.wait_ge(turned_ready, t + 1)
                tt = slice(t * P, (t + 1) * P)
                nc.scalar.mul(qn32[:, 0, tt], turned[t % 2][:, 0, :], m["qw1"][:, 0:1])
                nc.scalar.mul(qn32[0:QR - P, 1, tt], turned[t % 2][0:QR - P, 1, :], m["qw2"][:, 0:1])
                nc.scalar.mul(kt32[:, 0, tt], turned[t % 2][:, 2, :], m["kw"][:, 0:1])
                nc.scalar.mul(kt32[:, 1, tt], turned[t % 2][:, 3, :], m["kw"][:, 1:2]).then_inc(turned_used, 1)
                act.wait_ge(turned_used, t + 1)
                nc.scalar.copy(m["q1_hi"][:, tt], qn32[:, 0, tt])
                nc.scalar.copy(m["q2"][0:QR - P, tt], qn32[0:QR - P, 1, tt])
                for e in range(2):
                    last = nc.scalar.copy(m["kt_hi"][e][:, tt], kt32[:, e, tt])
                last.then_inc(parts_hi, 1)
            for n in range(NT * NCH):
                t, c = divmod(n, NCH)
                act.wait_ge(pt_ready, n + 1)
                nc.scalar.copy(m["peT"][:, 4 * c:4 * c + 4, t * P:(t + 1) * P], turned[n % 2][:]).then_inc(pt_used, 1)

        @block.vector
        def _(dve):
            done = [0]

            def then(instruction):
                done[0] += 1
                instruction.then_inc(dve_done, 1)
                dve.wait_ge(dve_done, done[0])

            nc.vector.memset(eps[:], RMS_EPS).then_inc(eps_set, 1)
            dve.wait_ge(loads, 16 * n_loads)

            def rotate(dst_a, dst_b, src, heads, t):
                pairs = lambda ap: ap.rearrange("p (h i two) -> p h i two", h=heads, two=2)
                table = lambda tab: tab[:, t, :].unsqueeze(1).to_broadcast([P, heads, ROPE])
                s4 = lambda tab: table(tab).rearrange("p h (i two) -> p h i two", two=2)
                nc.vector.tensor_tensor(dst_a.rearrange("p (h r) -> p h r", h=heads), src.rearrange("p (h r) -> p h r", h=heads),
                                        table(cos), ALU.mult)
                nc.vector.tensor_tensor(pairs(dst_b)[:, :, :, 0], pairs(src)[:, :, :, 1], s4(sin)[:, :, :, 0], ALU.mult)
                return nc.vector.tensor_tensor(pairs(dst_b)[:, :, :, 1], pairs(src)[:, :, :, 0], s4(sin)[:, :, :, 1],
                                               ALU.mult)

            def lower(t):
                dve.wait_ge(parts_hi, t + 1)
                tt = slice(t * P, (t + 1) * P)
                for dst, src, upper in ((m["q1_lo"][:, tt], qn32[:, 0, tt], m["q1_hi"][:, tt]),
                                        (m["q2"][QR - P:P, tt], qn32[0:QR - P, 1, tt], m["q2"][0:QR - P, tt]),
                                        (m["kt_lo"][0][:, tt], kt32[:, 0, tt], m["kt_hi"][0][:, tt]),
                                        (m["kt_lo"][1][:, tt], kt32[:, 1, tt], m["kt_hi"][1][:, tt])):
                    last = nc.vector.tensor_tensor(dst, src, upper.bitcast(F32), ALU.subtract)
                last.then_inc(parts_ready, 1)

            dve.wait_ge(w_hi_ready, 1)
            nc.vector.tensor_tensor(w_pe_lo[:], w_pe, w_pe_hi[:].bitcast(F32), ALU.subtract).then_inc(w_ready, 1)
            for t in range(NT):
                dve.wait_ge(std_ready, t + 1)
                wait(dve, turned_ready, t - 1)
                then(nc.vector.reciprocal(rstd[:, t % 2, :], std[:, t % 2, :]))
                then(rotate(rope_k[:, 0, :], rope_k[:, 1, :], down[t % 2][:, QR + CR:QR + CR + ROPE], 1, t))
                nc.vector.tensor_tensor(ck[:, t % 2, CR:2 * CR], rope_k[:, 0, :], rope_k[:, 1, :], ALU.add)
                latent = down[t % 2][:, QR:QR + CR].unsqueeze(1).to_broadcast([P, 2, CR])
                outer = lambda ap: ap.rearrange("p (a c) -> p a c", c=CR)[:, 0:3:2, :]
                nc.vector.tensor_scalar(outer(ck[:, t % 2, :]), latent, rstd[:, t % 2, 1:2], None, ALU.mult)
                then(nc.vector.tensor_scalar(qn[:, t % 2, :], down[t % 2][:, 0:QR], rstd[:, t % 2, 0:1], MLA_SCALE,
                                             ALU.mult, ALU.mult))
                then(nc.vector.tensor_copy(m["values"][:, t, 0:CR], ck[:, t % 2, 0:CR]))
                nc.vector.tensor_tensor(m["values"][:, t, CR:2 * CR], ck[:, t % 2, 0:CR],
                                        m["values"][:, t, 0:CR].bitcast(F32), ALU.subtract).then_inc(tok_ready, 1)
                if t:
                    lower(t - 1)
            lower(NT - 1)
            for n in range(NT * NCH):
                t, c = divmod(n, NCH)
                dve.wait_ge(pq_ready, n + 1)
                wait(dve, pe_ready, n - 1)
                rotate(rope_a[:, n % 2, :], rope_b[:, n % 2, :], pq[n % 2][:], HPC, t).then_inc(pq_used, 1)

        @block.gpsimd
        def _(pool):
            for n in range(NT * NCH):
                t, c = divmod(n, NCH)
                pool.wait_ge(pq_used, n + 1)
                wait(pool, pt_ready, n - 3)
                dst = q_pe[:, n % 4, :].rearrange("p (a two r) -> p a two r", two=2, r=ROPE)
                view = lambda ap: ap.rearrange("p (a two r) -> p a two r", two=2, r=ROPE)
                a, b = view(rope_a[:, n % 2, :]), view(rope_b[:, n % 2, :])
                nc.gpsimd.tensor_tensor(dst[:, :, 0, :], a[:, :, 1, :], b[:, :, 1, :], ALU.add)
                nc.gpsimd.tensor_tensor(dst[:, :, 1, :], a[:, :, 0, :], b[:, :, 0, :], ALU.add).then_inc(pe_ready, 1)


def mla_heads(nc, io, ident, m):
    with ExitStack() as ctx:
        sem = lambda n: ctx.enter_context(nc.semaphore(f"mh_{n}"))
        sb = lambda n, s, d=F32: ctx.enter_context(nc.sbuf_tensor(f"mh_{n}", s, d))
        w = sb("w", [P, PACK])
        w_q = w[:, 0:4 * P].rearrange("p (e r) -> p e r", e=2)
        w_k = w[:, 4 * P:4 * P + 2 * CR].rearrange("p (e c) -> p e c", e=2)
        w_v = w[:, 4 * P + 2 * CR:4 * P + 4 * CR].rearrange("p (e c) -> p e c", e=2)
        w_o = w[:, 4 * P + 4 * CR:PACK].rearrange("p (e n) -> p e n", e=2)
        absorbed_hi, absorbed_lo = sb("absorbed_hi", [P, 2, 2 * CR], F32R), sb("absorbed_lo", [P, 2, 2 * CR], F32R)
        q32 = [sb(f"q32_{e}", [P, S]) for e in range(2)]
        q_hi = [sb(f"q_hi{e}", [P, S], F32R) for e in range(2)]
        q_lo = [sb(f"q_lo{e}", [P, S], F32R) for e in range(2)]
        minus_max = sb("minus_max", [P, 2, NT])
        probs = sb("probs", [P, 2, S])
        turned_hi = sb("turned_hi", [P, 2, NT, 2 * P], F32R)
        turned_lo = sb("turned_lo", [P, 2, NT, 2 * P], F32R)
        lower_mix = sb("lower_mix", [P, 2, 2 * P])
        mask, ident_bf = sb("mask", [P, P], BF16), sb("ident_bf", [P, P], BF16)
        score_ps = [ctx.enter_context(nc.psum_tensor(f"mh_score{i}", [P, S], F32)) for i in range(2)]
        turn_ps = [ctx.enter_context(nc.psum_tensor(f"mh_turn{i}", [P, 4, P], F32)) for i in range(2)]
        mix_ps = ctx.enter_context(nc.psum_tensor("mh_mix", [P, 2 * P], F32))
        prep_ps = ctx.enter_context(nc.psum_tensor("mh_prep", [P, BANK], F32))
        consts = sem("consts")
        w_in, pe_in = sem("w_in"), [sem(f"pe_in{e}") for e in range(2)]
        prep_ready, prep_used = sem("prep_ready"), sem("prep_used")
        absorbed_ready = sem("absorbed_ready")
        hi_ready, lo_ready = sem("hi_ready"), sem("lo_ready")
        scores_ready, max_ready, probs_ready = sem("scores_ready"), sem("max_ready"), sem("probs_ready")
        turns_ready, turn_hi_ready, turn_lo_ready = sem("turns_ready"), sem("turn_hi_ready"), sem("turn_lo_ready")
        mix_ready, lower_ready, out_ready = sem("mix_ready"), sem("lower_ready"), sem("out_ready")
        block = ctx.enter_context(nc.Block())

        TURNS = [(t, range(j, min(j + 4, t + 1))) for t in range(NT) for j in range(0, t + 1, 4)]
        NTURN = len(TURNS)
        turns_of = lambda t: [g for g in range(NTURN) if TURNS[g][0] == t]
        turns_to = lambda t: sum(x[0] <= t for x in TURNS)

        def looped(engine, body, first=1, end=PAIRS - 1):
            for i in range(first):
                body(i)
            with engine.Fori(first, end) as i:
                body(i)
            for i in range(end, PAIRS):
                body(i)

        is_last = lambda i: isinstance(i, int) and i == PAIRS - 1
        head = lambda i, e: 2 * i + e
        follows = lambda i, e: None if is_last(i) and e == 1 else (i, 1) if e == 0 else (i + 1, 0)
        before = lambda i, e: (i, 0) if e == 1 else None if isinstance(i, int) and i == 0 else (i - 1, 1)

        def split_rows(e):
            return (slice(0, CR), slice(CR, P)) if e == 0 else (slice(CR, P), slice(0, CR))

        @block.sync
        def _(sp):
            def load_weights(i):
                wait(sp, prep_ready, 4 * i - 2)
                sp.dma_start(w[:], io["w_pairs"][bass.ds(i * P, P), :]).then_inc(w_in, 16)

            def load_rotary(i, e):
                wait(sp, lo_ready, 2 * i + e - 1)
                rows = split_rows(e)[1]
                sp.dma_start(q32[e][rows, :], m["peT"][rows, i, :]).then_inc(pe_in[e], 16)

            def step(i, more_weights):
                load_rotary(i + 1, 0)
                load_rotary(i + 1, 1)
                if more_weights:
                    load_weights(i + 2)

            load_weights(0)
            load_rotary(0, 0)
            load_rotary(0, 1)
            load_weights(1)
            step(0, True)
            with sp.Fori(1, PAIRS - 2) as i:
                step(i, True)
            step(PAIRS - 2, False)

        @block.tensor
        def _(pe):
            def prep_absorb(i):
                wait(pe, w_in, 16 * (i + 1))
                wait(pe, prep_used, 4 * i)
                for e in range(2):
                    nc.tensor.matmul(prep_ps[:, e * CR:(e + 1) * CR], w_q[:, e, 0:P], w_k[:, e, :], start=True, stop=True)
                    last = nc.tensor.matmul(prep_ps[:, P + e * CR:P + (e + 1) * CR], w_q[:, e, P:2 * P], w_k[:, e, :],
                                            start=True, stop=True)
                last.then_inc(prep_ready, 1)

            def prep_output(i):
                wait(pe, prep_used, 4 * i + 1)
                for e in range(2):
                    last = nc.tensor.matmul(prep_ps[e * CR:(e + 1) * CR, :], w_v[:, e, :], w_o[:, e, :], start=True, stop=True)
                last.then_inc(prep_ready, 1)

            def prep_queries(i, half):
                wait(pe, prep_used, 4 * i + 2 + half)
                h = slice(half * BANK, (half + 1) * BANK)
                a = slice(0, QR - P)
                for n, (weights, ranks) in enumerate((
                        (absorbed_hi[:, 0, :], m["q1_hi"][:, h]), (absorbed_hi[:, 0, :], m["q1_lo"][:, h]),
                        (absorbed_lo[:, 0, :], m["q1_hi"][:, h]), (absorbed_hi[:, 1, :], m["q2"][:, h]),
                        (absorbed_lo[a, 1, :], m["q2"][a, h]))):
                    last = nc.tensor.matmul(prep_ps[:], weights, ranks, start=n == 0, stop=n == 4)
                last.then_inc(prep_ready, 1)

            def scores(i, e, t):
                if t == 0:
                    wait(pe, lo_ready, head(i, e) + 1)
                wait(pe, probs_ready, NT * head(i, e) + t - 1)
                q = slice(t * P, (t + 1) * P)
                for k0, k1, base in score_pieces(t):
                    out, k = score_ps[t % 2][:, base + k0:base + k1], slice(k0, k1)
                    diagonal = k1 == (t + 1) * P
                    nc.tensor.matmul(out, q_hi[e][:, q], m["kt_hi"][e][:, k], start=True, stop=False)
                    nc.tensor.matmul(out, q_hi[e][:, q], m["kt_lo"][e][:, k], start=False, stop=False)
                    last = nc.tensor.matmul(out, q_lo[e][:, q], m["kt_hi"][e][:, k], start=False, stop=not diagonal)
                    if diagonal:
                        last = nc.tensor.matmul(score_ps[t % 2][:, base + k1 - P:base + k1], ident_bf[:], mask[:],
                                                start=False, stop=True)
                last.then_inc(scores_ready, 1)

            def turn(i, e, t):
                wait(pe, probs_ready, NT * head(i, e) + t + 1)
                for g in turns_of(t):
                    wait(pe, turn_lo_ready, NTURN * head(i, e) + g - 1)
                    for n, j in enumerate(TURNS[g][1]):
                        last = nc.tensor.transpose(turn_ps[g % 2][:, n, :], probs[:, t % 2, j * P:(j + 1) * P], ident[:])
                    last.then_inc(turns_ready, 1)

            def mix(i, e, pair):
                wait(pe, turn_lo_ready, NTURN * head(i, e) + turns_to(2 * pair + 1))
                wait(pe, out_ready, 4 * head(i, e) + pair)
                for j in range(2 * pair + 2):
                    q0 = P if j == 2 * pair + 1 else 0
                    for part in (turned_hi, turned_lo):
                        last = nc.tensor.matmul(mix_ps[:, q0:2 * P], m["values"][:, j, :], part[:, pair % 2, j, q0:2 * P],
                                                start=j == 0 and part is turned_hi,
                                                stop=j == 2 * pair + 1 and part is turned_lo)
                last.then_inc(mix_ready, 1)

            def slot(i, e):
                for t in range(NT):
                    if t in (0, 2) and before(i, e):
                        mix(*before(i, e), 2 + t // 2)
                    if t in (4, 6):
                        mix(i, e, t // 2 - 2)
                    if not is_last(i):
                        if (e, t) == (0, 1):
                            prep_absorb(i + 1)
                        if (e, t) == (0, 3):
                            prep_output(i + 1)
                        if (e, t) == (0, 7):
                            prep_queries(i + 1, 0)
                        if (e, t) == (1, 1):
                            prep_queries(i + 1, 1)
                    if t + 2 < NT:
                        scores(i, e, t + 2)
                    elif follows(i, e):
                        scores(*follows(i, e), t + 2 - NT)
                    turn(i, e, t)

            pe.wait_ge(consts, 2)
            prep_absorb(0)
            prep_output(0)
            prep_queries(0, 0)
            prep_queries(0, 1)
            scores(0, 0, 0)
            scores(0, 0, 1)

            def body(i):
                slot(i, 0)
                slot(i, 1)
            looped(pe, body)
            mix(PAIRS - 1, 1, 2)
            mix(PAIRS - 1, 1, 3)

        @block.scalar
        def _(act):
            def take_absorbed(i):
                wait(act, prep_ready, 4 * i + 1)
                nc.scalar.copy(absorbed_hi[:].rearrange("p a n -> p (a n)"), prep_ps[:, 0:2 * P]).then_inc(absorbed_ready, 1)

            def take_output(i):
                wait(act, prep_ready, 4 * i + 2)
                nc.scalar.mul(m["w_out"][:, bass.ds(i, 1), :].rearrange("p a n -> p (a n)"), prep_ps[:], m["kw2"][:, 0:1]
                              ).then_inc(prep_used, 1)

            def take_queries(i, half):
                wait(act, prep_ready, 4 * i + 3 + half)
                if half == 0:
                    wait(act, lo_ready, 2 * i)
                h = slice(half * BANK, (half + 1) * BANK)
                for e in range(2):
                    rows = split_rows(e)[0]
                    last = nc.scalar.copy(q32[e][rows, h], prep_ps[rows, :])
                last.then_inc(prep_used, 1)

            def upper(i, e):
                wait(act, scores_ready, NT * (head(i, e) - 1))
                if e == 0:
                    wait(act, prep_used, 4 * i + 4)
                wait(act, pe_in[e], 16 * (i + 1))
                nc.scalar.copy(q_hi[e][:], q32[e][:]).then_inc(hi_ready, 1)

            def exp(i, e, t):
                wait(act, max_ready, NT * head(i, e) + t + 1)
                wait(act, turns_ready, NTURN * (head(i, e) - 1) + turns_to(NT - 2 + t) if t < 2 else
                     NTURN * head(i, e) + turns_to(t - 2))
                base, width = score_pieces(t)[0][2], (t + 1) * P
                nc.scalar.activation(probs[:, t % 2, 0:width], score_ps[t % 2][:, base:base + width], ACT.Exp,
                                     bias=minus_max[:, e, t:t + 1],
                                     accum_out=m["sums"][:, bass.ds(head(i, e), 1), t:t + 1].rearrange("p a b -> p (a b)")
                                     ).then_inc(probs_ready, 1)

            def turned_upper(i, e, t):
                pair, half = t // 2 % 2, t % 2
                for g in turns_of(t):
                    wait(act, turns_ready, NTURN * head(i, e) + g + 1)
                    wait(act, mix_ready, 4 * head(i, e) + t // 2 - 1)
                    j = TURNS[g][1]
                    nc.scalar.copy(turned_hi[:, pair, j[0]:j[-1] + 1, half * P:(half + 1) * P], turn_ps[g % 2][:, 0:len(j), :]
                                   ).then_inc(turn_hi_ready, 1)

            def take_lower(i, e, pair):
                wait(act, mix_ready, 4 * head(i, e) + pair + 1)
                wait(act, out_ready, 4 * head(i, e) + pair - 1)
                nc.scalar.copy(lower_mix[CR:P, pair % 2, :], mix_ps[CR:P, :]).then_inc(lower_ready, 1)

            def slot(i, e):
                for t in range(NT):
                    exp(i, e, t)
                    if t:
                        turned_upper(i, e, t - 1)
                    elif before(i, e):
                        turned_upper(*before(i, e), NT - 1)
                    if t in (1, 3) and before(i, e):
                        take_lower(*before(i, e), 2 + t // 2)
                    if t in (5, 7):
                        take_lower(i, e, t // 2 - 2)
                    if not is_last(i):
                        if (e, t) == (0, 2):
                            take_absorbed(i + 1)
                        if (e, t) == (0, 4):
                            take_output(i + 1)
                        if (e, t) == (1, 0):
                            take_queries(i + 1, 0)
                        if (e, t) == (1, 2):
                            take_queries(i + 1, 1)
                    if t == 4 and follows(i, e):
                        upper(*follows(i, e))

            take_absorbed(0)
            take_output(0)
            take_queries(0, 0)
            take_queries(0, 1)
            upper(0, 0)

            def body(i):
                slot(i, 0)
                slot(i, 1)
            looped(act, body)
            turned_upper(PAIRS - 1, 1, NT - 1)
            take_lower(PAIRS - 1, 1, 2)
            take_lower(PAIRS - 1, 1, 3)

        @block.vector
        def _(dve):
            nc.vector.tensor_copy(mask[:], m["mask"][:]).then_inc(consts, 1)
            nc.vector.tensor_copy(ident_bf[:], ident[:]).then_inc(consts, 1)

            def lower(i, e):
                wait(dve, hi_ready, head(i, e) + 1)
                nc.vector.tensor_tensor(q_lo[e][:], q32[e][:], q_hi[e][:].bitcast(F32), ALU.subtract).then_inc(lo_ready, 1)

            def absorbed_lower(i):
                wait(dve, absorbed_ready, i + 1)
                nc.vector.tensor_tensor(absorbed_lo[:].rearrange("p a n -> p (a n)"), prep_ps[:, 0:2 * P],
                                        absorbed_hi[:].rearrange("p a n -> p (a n)").bitcast(F32), ALU.subtract
                                        ).then_inc(prep_used, 1)

            def take_max(i, e, t):
                wait(dve, scores_ready, NT * head(i, e) + t + 1)
                base, width = score_pieces(t)[0][2], (t + 1) * P
                nc.vector.reduce_max(minus_max[:, e, t:t + 1], score_ps[t % 2][:, base:base + width], AX.X, negate=True
                                     ).then_inc(max_ready, 1)

            def turned_lower(i, e, t):
                pair, half = t // 2 % 2, t % 2
                for g in turns_of(t):
                    wait(dve, turn_hi_ready, NTURN * head(i, e) + g + 1)
                    j = TURNS[g][1]
                    place = (slice(None), pair, slice(j[0], j[-1] + 1), slice(half * P, (half + 1) * P))
                    nc.vector.tensor_tensor(turned_lo[place], turn_ps[g % 2][:, 0:len(j), :], turned_hi[place].bitcast(F32),
                                            ALU.subtract).then_inc(turn_lo_ready, 1)

            def join(i, e, pair):
                wait(dve, lower_ready, 4 * head(i, e) + pair + 1)
                rows = split_rows(e)[0]
                out = m["peT"][rows, bass.ds(i, 1), pair * 2 * P:(pair + 1) * 2 * P].rearrange("p a n -> p (a n)")
                nc.vector.tensor_tensor(out, mix_ps[0:CR, :], lower_mix[CR:P, pair % 2, :], ALU.add
                                        ).then_inc(out_ready, 1)

            def slot(i, e):
                for t in range(NT):
                    if t + 1 < NT:
                        take_max(i, e, t + 1)
                    elif follows(i, e):
                        take_max(*follows(i, e), 0)
                    if t:
                        turned_lower(i, e, t - 1)
                    elif before(i, e):
                        turned_lower(*before(i, e), NT - 1)
                    if t in (1, 3) and before(i, e):
                        join(*before(i, e), 2 + t // 2)
                    if t in (5, 7):
                        join(i, e, t // 2 - 2)
                    if (e, t) == (0, 2) and not is_last(i):
                        absorbed_lower(i + 1)
                    if t == 4 and follows(i, e):
                        lower(*follows(i, e))

            absorbed_lower(0)
            lower(0, 0)
            take_max(0, 0, 0)

            def body(i):
                slot(i, 0)
                slot(i, 1)
            looped(dve, body)
            turned_lower(PAIRS - 1, 1, NT - 1)
            join(PAIRS - 1, 1, 2)
            join(PAIRS - 1, 1, 3)


def score_pieces(t):
    n = (t + 1) * P
    if n <= BANK:
        return [(0, n, 0)]
    if n == BANK + P:
        return [(0, BANK - P, P), (BANK - P, n, P)]
    return [(0, BANK, 0), (BANK, n, 0)]


def mla_output(nc, io, ident, mixed, w_out, sums, x_dram_out, hT_dram, out_dram):
    with ExitStack() as ctx:
        sem = lambda n: ctx.enter_context(nc.semaphore(f"mo_{n}"))
        sb = lambda n, s, d=F32: ctx.enter_context(nc.sbuf_tensor(f"mo_{n}", s, d))
        w_hi, w_lo = sb("w_hi", [P, PAIRS, D], F32R), sb("w_lo", [P, PAIRS, D], F32R)
        with ExitStack() as part:
            inverse = part.enter_context(nc.sbuf_tensor("mo_inverse", [P, H, NT], F32))
            rows_hi = part.enter_context(nc.sbuf_tensor("mo_rows_hi", [H, S], F32R))
            rows_lo = part.enter_context(nc.sbuf_tensor("mo_rows_lo", [H, S], F32R))
            spread_f = part.enter_context(nc.sbuf_tensor("mo_spread_f", [H, PAIRS, P], F32))
            spread = part.enter_context(nc.sbuf_tensor("mo_spread", [H, PAIRS, P], F32R))
            rows_ps = part.enter_context(nc.psum_tensor("mo_rows_ps", [P, S], F32))
            ps = [part.enter_context(nc.psum_tensor(f"mo_ps{i}", [P, BANK], F32)) for i in range(4)]
            names = ("spread_in", "spread_set", "inverse_ready", "rows_ready", "hi_ready", "lo_ready", "spreads", "used",
                     "w_hi_ready")
            spread_in, spread_set, inverse_ready, rows_ready, hi_ready, lo_ready, spreads, used, w_hi_ready = (
                part.enter_context(nc.semaphore(f"mo_{n}")) for n in names)
            block = part.enter_context(nc.Block())
            QUARTER = PAIRS // 4

            @block.sync
            def _(sp):
                sp.dma_start(spread_f[:], io["spread_mla"]).then_inc(spread_in, 16)

            @block.tensor
            def _(pe):
                pe.wait_ge(inverse_ready, 1)
                for t in range(NT):
                    last = nc.tensor.transpose(rows_ps[0:H, t * P:(t + 1) * P], inverse[:, :, t], ident[:])
                last.then_inc(rows_ready, 1)
                pe.wait_ge(lo_ready, 1)
                pe.wait_ge(spread_set, 1)
                for n in range(PAIRS * NHALF):
                    i, half = n // NHALF, n % NHALF
                    h = slice(half * BANK, (half + 1) * BANK)
                    wait(pe, used, n - 3)
                    nc.tensor.matmul(ps[n % 4][:], spread[:, i, :], rows_hi[:, h], start=True, stop=False)
                    nc.tensor.matmul(ps[n % 4][:], spread[:, i, :], rows_lo[:, h], start=False, stop=True).then_inc(spreads, 1)

            @block.scalar
            def _(act):
                for n in range(4):
                    if n == 1:
                        act.wait_ge(spread_in, 16)
                        nc.scalar.copy(spread[:], spread_f[:]).then_inc(spread_set, 1)
                        act.wait_ge(rows_ready, 1)
                        nc.scalar.copy(rows_hi[:], rows_ps[0:H, :]).then_inc(hi_ready, 1)
                    quarter = slice(n * QUARTER, (n + 1) * QUARTER)
                    nc.scalar.copy(w_hi[:, quarter, :], w_out[:, quarter, :]).then_inc(w_hi_ready, 1)

            def lower(engine, ops, n):
                quarter = slice(n * QUARTER, (n + 1) * QUARTER)
                engine.wait_ge(w_hi_ready, n + 1)
                ops.tensor_tensor(w_lo[:, quarter, :], w_out[:, quarter, :], w_hi[:, quarter, :].bitcast(F32), ALU.subtract)

            @block.gpsimd
            def _(pool):
                lower(pool, nc.gpsimd, 0)
                lower(pool, nc.gpsimd, 1)

            @block.vector
            def _(dve):
                nc.vector.reciprocal(inverse[:], sums[:]).then_inc(inverse_ready, 1)
                dve.wait_ge(hi_ready, 1)
                nc.vector.tensor_tensor(rows_lo[:], rows_ps[0:H, :], rows_hi[:].bitcast(F32), ALU.subtract).then_inc(lo_ready, 1)
                for n in range(PAIRS * NHALF):
                    i, half = n // NHALF, n % NHALF
                    o = mixed[:, i, half * BANK:(half + 1) * BANK]
                    dve.wait_ge(spreads, n + 1)
                    nc.vector.tensor_tensor(o, o, ps[n % 4][:], ALU.mult).then_inc(used, 1)
                lower(dve, nc.vector, 2)
                lower(dve, nc.vector, 3)

        x = w_out[:, 0:NT, :]
        hT = w_out[:, NT:2 * NT, :].rearrange("p a n -> p (a n)").rearrange("p (k s) -> p k s", k=ND)
        a_hi, a_lo = sb("a_hi", [P, 2, PAIRS, P], F32R), sb("a_lo", [P, 2, PAIRS, P], F32R)
        a_hi_ready, a_lo_ready, used = sem("a_hi_ready"), sem("a_lo_ready"), sem("a_used")

        def scalar_work(act, t):
            wait(act, used, t - 1)
            nc.scalar.copy(a_hi[:, t % 2, :, :], mixed[:, :, t * P:(t + 1) * P]).then_inc(a_hi_ready, 1)

        def vector_work(dve, t):
            dve.wait_ge(a_hi_ready, t + 1)
            nc.vector.tensor_tensor(a_lo[:, t % 2, :, :], mixed[:, :, t * P:(t + 1) * P],
                                    a_hi[:, t % 2, :, :].bitcast(F32), ALU.subtract).then_inc(a_lo_ready, 1)

        def project(pe, t, out):
            pe.wait_ge(a_lo_ready, t + 1)
            products = [(a, w, i) for i in range(PAIRS) for a, w in ((a_hi, w_hi), (a_hi, w_lo), (a_lo, w_hi))]
            for n, (a, w, i) in enumerate(products):
                last = nc.tensor.matmul(out[:], a[:, t % 2, i, :], w[:, i, :], start=n == 0, stop=n == len(products) - 1)
            return last
        works = dict(project=project, x_dram=io["x"], scalar_work=scalar_work, vector_work=vector_work, projected=used)
        if out_dram is not None:
            norm_block(nc, "n1", x, None, ident, out_dram=out_dram, **works)
        else:
            norm_block(nc, "n1", x, hT, ident, out_dram=x_dram_out, hT_dram=hT_dram, **works)


def ffn_inner(nc, io, hT_dram, x, d, down_hi, down_lo):
    with ExitStack() as ctx:
        sem = lambda s: ctx.enter_context(nc.semaphore(f"ff_{s}"))
        sb = lambda n, s, dt=F32: ctx.enter_context(nc.sbuf_tensor(f"ff_{n}", s, dt))
        hT_hi, hT_lo = sb("hT_hi", [P, ND, S], F32R), sb("hT_lo", [P, ND, S], F32R)
        w = x[:, 0:6, :].rearrange("p a n -> p (a n)").rearrange("p (a n) -> p a n", a=2)
        gated = x[:, 6:8, :]
        w_hi, w_lo = sb("w_hi", [P, 2, 2 * D], F32R), sb("w_lo", [P, 2, 2 * D], F32R)
        sides = sb("sides", [96, SIDES], F32R)
        sv_now = sb("sv_now", [96, 2, P], F32R)
        hT = d[:, NI - ND:NI, :]
        sides_f = d[0:96, 0:7, :].rearrange("p a n -> p (a n)")[:, 0:SIDES]
        su = [sides[:, n * INNER:(n + 1) * INNER] for n in range(2)]
        su_down = sides[:, 2 * INNER:RIGHT]
        sv = [sides[:, RIGHT + n * D:RIGHT + (n + 1) * D] for n in range(2)]
        sv_down = sides[:, RIGHT + 2 * D:SIDES]
        scale_ps = ctx.enter_context(nc.psum_tensor("ff_scale", [P, 3 * D], F32))
        gate_ps = [ctx.enter_context(nc.psum_tensor(f"ff_gate{i}", [P, BANK], F32)) for i in range(2)]
        up_ps = [ctx.enter_context(nc.psum_tensor(f"ff_up{i}", [P, BANK], F32)) for i in range(2)]
        cleared, sides_in, hT_in = sem("cleared"), sem("sides_in"), [sem(f"hT_in{i}") for i in range(NHALF)]
        w_in = [sem(f"w_in{i}") for i in range(2)]
        sides_hi, sides_ready, hT_hi_ready, hT_ready = (sem(s) for s in ("sides_hi", "sides_ready", "hT_hi_ready", "hT_ready"))
        sv_ready, scale_ready, scaled, hi_ready, split = (sem(s) for s in ("sv_ready", "scale_ready", "scaled", "hi_ready", "split"))
        gate_ready, up_ready, gated_ready, d_ready = sem("gate_ready"), sem("up_ready"), sem("gated_ready"), sem("d_ready")
        block = ctx.enter_context(nc.Block())
        half_of = lambda h: slice(h * BANK, (h + 1) * BANK)
        last = NI // 2 - 1

        def looped(engine, body):
            body(0, 0)
            body(1, 1)
            with engine.Fori(1, last) as r:
                body(2 * r, 0)
                body(2 * r + 1, 1)
            body(2 * last, 0)
            body(2 * last + 1, 1)

        @block.gpsimd
        def _(pool):
            nc.gpsimd.memset(sides_f[:, RIGHT:SIDES], 0.0).then_inc(cleared, 1)

        is_last = lambda it, back=1: isinstance(it, int) and it >= NI - back
        times = lambda it, a: it // 2 + 1 if isinstance(it, int) else (it - a) // 2 + 1

        @block.sync
        def _(sp):
            def load(it, a):
                wait(sp, split, it - 1)
                sp.dma_start(w[:, a, :], io["w_inner"][bass.ds(it * P, P), :]).then_inc(w_in[a], 16)

            sp.wait_ge(cleared, 2)
            for part in range(3):
                sp.dma_start(sides_f[32 * part:32 * part + RANK, :], io["sides"]).then_inc(sides_in, 16)
            load(0, 0)
            for half in range(NHALF):
                sp.dma_start(hT[:, :, half_of(half)], hT_dram[:, :, half_of(half)]).then_inc(hT_in[half], 16)
            load(1, 1)

            def body(it, a):
                if not is_last(it, 2):
                    load(it + 2, a)
            looped(sp, body)

        @block.tensor
        def _(pe):
            def scales(it, a):
                wait(pe, scaled, it)
                wait(pe, sv_ready, it + 1)
                for n in range(2):
                    for k in range(ND):
                        nc.tensor.matmul(scale_ps[:, n * D + k * P:n * D + (k + 1) * P], sv[n][:, k * P:(k + 1) * P],
                                         su[n][:, bass.ds(it * P, P)], start=True, stop=True)
                nc.tensor.matmul(scale_ps[:, 2 * D:3 * D], sv_now[:, a, :], su_down, start=True, stop=True
                                 ).then_inc(scale_ready, 1)

            def products(it, a):
                wait(pe, split, it + 1)
                for half in range(NHALF):
                    wait(pe, d_ready, 2 * it + half - 1)
                    for n, (out, ready) in enumerate(((gate_ps, gate_ready), (up_ps, up_ready))):
                        for k in range(ND):
                            cols = slice(n * D + k * P, n * D + (k + 1) * P)
                            for m, (weights, h) in enumerate(((w_hi, hT_hi), (w_hi, hT_lo), (w_lo, hT_hi))):
                                final = nc.tensor.matmul(out[half][:], weights[:, a, cols], h[:, k, half_of(half)],
                                                         start=k == 0 and m == 0, stop=k == ND - 1 and m == 2)
                        final.then_inc(ready, 1)

            pe.wait_ge(sides_ready, 2)
            scales(0, 0)
            pe.wait_ge(hT_ready, NHALF)

            def body(it, a):
                if not is_last(it):
                    scales(it + 1, 1 - a)
                products(it, a)
            looped(pe, body)

        @block.scalar
        def _(act):
            def take_sv(it, a):
                wait(act, scale_ready, it - 1)
                nc.scalar.copy(sv_now[:, a, :], sv_down[:, bass.ds(it * P, P)].bitcast(F32)).then_inc(sv_ready, 1)

            def upper(it, a):
                wait(act, scaled, it + 1)
                wait(act, up_ready, 2 * it - 2)
                nc.scalar.copy(w_hi[:, a, :], w[:, a, 0:2 * D])
                nc.scalar.copy(down_hi[:, bass.ds(it, 1), :].rearrange("p a n -> p (a n)"), w[:, a, 2 * D:3 * D]
                               ).then_inc(hi_ready, 1)

            def gate(it, half):
                wait(act, gate_ready, 2 * it + half + 1)
                wait(act, d_ready, 2 * it + half - 1)
                nc.scalar.activation(gated[:, half, :], gate_ps[half][:], ACT.Silu).then_inc(gated_ready, 1)

            act.wait_ge(sides_in, 48)
            nc.scalar.copy(sides[:, 0:RIGHT], sides_f[:, 0:RIGHT]).then_inc(sides_hi, 1)
            nc.scalar.copy(sides[:, RIGHT:SIDES], sides_f[:, RIGHT:SIDES]).then_inc(sides_hi, 1)
            for half in range(NHALF):
                act.wait_ge(hT_in[half], 16)
                nc.scalar.copy(hT_hi[:, :, half_of(half)], hT[:, :, half_of(half)]).then_inc(hT_hi_ready, 1)
            act.wait_ge(sides_ready, 2)
            take_sv(0, 0)
            take_sv(1, 1)
            upper(0, 0)

            def body(it, a):
                if not is_last(it, 2):
                    take_sv(it + 2, a)
                gate(it, 0)
                if not is_last(it):
                    upper(it + 1, 1 - a)
                gate(it, 1)
            looped(act, body)

        @block.vector
        def _(dve):
            def scale(it, a):
                dve.wait_ge(w_in[a], 16 * times(it, a))
                wait(dve, scale_ready, it + 1)
                nc.vector.tensor_tensor(w[:, a, :], w[:, a, :], scale_ps[:], ALU.mult).then_inc(scaled, 1)

            def lower(it, a):
                wait(dve, hi_ready, it + 1)
                wait(dve, up_ready, 2 * it - 2)
                nc.vector.tensor_tensor(w_lo[:, a, :], w[:, a, 0:2 * D], w_hi[:, a, :].bitcast(F32), ALU.subtract)
                one = lambda m: m[:, bass.ds(it, 1), :].rearrange("p a n -> p (a n)")
                nc.vector.tensor_tensor(one(down_lo), w[:, a, 2 * D:3 * D], one(down_hi).bitcast(F32), ALU.subtract
                                        ).then_inc(split, 1)

            def join(it, half):
                wait(dve, gated_ready, 2 * it + half + 1)
                wait(dve, up_ready, 2 * it + half + 1)
                nc.vector.tensor_tensor(d[:, bass.ds(it, 1), half_of(half)].rearrange("p a n -> p (a n)"),
                                        gated[:, half, :], up_ps[half][:], ALU.mult).then_inc(d_ready, 1)

            nc.vector.memset(sides_f[:, 0:RIGHT], 0.0).then_inc(cleared, 1)
            for n, (rows, cols) in enumerate(((slice(64, 96), slice(0, RIGHT)), (slice(32, 64), slice(RIGHT, SIDES)))):
                dve.wait_ge(sides_hi, n + 1)
                nc.vector.tensor_tensor(sides[rows, cols], sides_f[rows, cols], sides[rows, cols].bitcast(F32), ALU.subtract
                                        ).then_inc(sides_ready, 1)
            for half in range(NHALF):
                dve.wait_ge(hT_hi_ready, half + 1)
                nc.vector.tensor_tensor(hT_lo[:, :, half_of(half)], hT[:, :, half_of(half)],
                                        hT_hi[:, :, half_of(half)].bitcast(F32), ALU.subtract).then_inc(hT_ready, 1)
            scale(0, 0)
            lower(0, 0)

            def body(it, a):
                if not is_last(it):
                    scale(it + 1, 1 - a)
                join(it, 0)
                if not is_last(it):
                    lower(it + 1, 1 - a)
                join(it, 1)
            looped(dve, body)


def mha_inputs(nc, io, h, spare, w_hi, w_lo, hi, lo, scratch):
    with ExitStack() as ctx:
        sem = lambda s: ctx.enter_context(nc.semaphore(f"ai_{s}"))
        sb = lambda n, s, dt=F32: ctx.enter_context(nc.sbuf_tensor(f"ai_{n}", s, dt))
        w = [spare[:, 2 * c:2 * c + 2, :].rearrange("p a n -> p (a n)").rearrange("p (k n) -> p k n", k=ND) for c in range(3)]
        values = [spare[:, 6 + i, :].rearrange("p (h r) -> p h r", h=H) for i in range(2)]
        full = spare[:, 8:10, :].rearrange("p a n -> p (a n)").rearrange("p (a n) -> p a n", n=BANK)
        bias_qk, bias_v = sb("bias_qk", [P, 2 * ND]), sb("bias_v", [P, D])
        ps = [ctx.enter_context(nc.psum_tensor(f"ai_ps{i}", [P, BANK], F32)) for i in range(4)]
        w_in, bias_in = [sem(f"w_in{c}") for c in range(3)], sem("bias_in")
        w_hi_ready, w_ready, ready, full_ready, hi_ready, lo_ready = (sem(s) for s in (
            "w_hi_ready", "w_ready", "ready", "full_ready", "hi_ready", "lo_ready"))
        part_out, v_ready, v_out = [sem(f"part_out{i}") for i in range(3)], sem("v_ready"), [sem(f"v_out{i}") for i in range(2)]
        block = ctx.enter_context(nc.Block())
        NQK = 2 * ND * NHALF
        of = lambda part, c: part[:, ND * c:ND * (c + 1), :]

        @block.sync
        def _(sp):
            for c in range(3):
                sp.dma_start(w[c], io["qkv_w"][:, :, c * D:(c + 1) * D]).then_inc(w_in[c], 16)
                if c == 0:
                    for dst, src in ((bias_qk[:], io["bias_qk"]), (bias_v[:], io["bias_v"])):
                        sp.dma_start(dst, src).then_inc(bias_in, 16)
            for n in range(NQK):
                blk, half = divmod(n, NHALF)
                for part, buf, done in ((0, hi, hi_ready), (1, lo, lo_ready)):
                    sp.wait_ge(done, n + 1)
                    sp.dma_start(scratch["qk"][part, blk * P:(blk + 1) * P, half * BANK:(half + 1) * BANK],
                                 buf[:, n % 3, :].bitcast(F32)
                                 ).then_inc(part_out[n % 3], 16)
            for t in range(NT):
                sp.wait_ge(v_ready, t + 1)
                sp.dma_start(scratch["v"][t * P:(t + 1) * P, :], values[t % 2].rearrange("p h r -> p (h r)")
                             ).then_inc(v_out[t % 2], 16)
            for i in range(3):
                sp.wait_ge(part_out[i], 32 * len(range(i, NQK, 3)))
            for i in range(2):
                sp.wait_ge(v_out[i], 16 * NT // 2)

        @block.tensor
        def _(pe):
            for n in range(NQK + NT):
                wait(pe, full_ready, min(n - 3, NQK))
                wait(pe, v_ready, n - 3 - NQK)
                blk, half = divmod(n, NHALF)
                c = blk // ND if n < NQK else 2
                pe.wait_ge(w_ready, c + 1)
                for k in range(ND):
                    for m, (a, b) in enumerate(((0, 0), (0, 1), (1, 0))):
                        weights = of((w_hi, w_lo)[a], c)
                        if n < NQK:
                            left, right = weights[:, k, blk % ND * P:(blk % ND + 1) * P], h[b][:, k, half * BANK:(half + 1) * BANK]
                        else:
                            left, right = h[b][:, k, (n - NQK) * P:(n - NQK + 1) * P], weights[:, k, :]
                        last = nc.tensor.matmul(ps[n % 4][:], left, right, start=k == 0 and m == 0, stop=k == ND - 1 and m == 2)
                last.then_inc(ready, 1)

        @block.scalar
        def _(act):
            def upper(c):
                act.wait_ge(w_in[c], 16)
                nc.scalar.copy(of(w_hi, c), w[c]).then_inc(w_hi_ready, 1)

            upper(0)
            act.wait_ge(bias_in, 32)
            for n in range(NQK):
                blk = n // NHALF
                if n in (1, 3):
                    upper((n + 1) // 2)
                act.wait_ge(ready, n + 1)
                wait(act, lo_ready, n - 2)
                nc.scalar.activation(full[:, n % 3, :], ps[n % 4][:], ACT.Identity, bias=bias_qk[:, blk:blk + 1]
                                     ).then_inc(full_ready, 1)

        @block.vector
        def _(dve):
            def lower(c):
                dve.wait_ge(w_hi_ready, c + 1)
                nc.vector.tensor_tensor(of(w_lo, c), w[c], of(w_hi, c).bitcast(F32), ALU.subtract).then_inc(w_ready, 1)

            for v in values:
                nc.vector.memset(v[:, :, HD:2 * HD], 1.0)
            lower(0)
            for n in range(NQK):
                if n in (1, 3):
                    lower((n + 1) // 2)
                dve.wait_ge(full_ready, n + 1)
                if n >= 3:
                    dve.wait_ge(part_out[n % 3], 32 * (n // 3))
                nc.vector.tensor_copy(hi[:, n % 3, :], full[:, n % 3, :]).then_inc(hi_ready, 1)
                dve.wait_ge(hi_ready, n + 1)
                nc.vector.tensor_tensor(lo[:, n % 3, :], full[:, n % 3, :], hi[:, n % 3, :].bitcast(F32), ALU.subtract
                                        ).then_inc(lo_ready, 1)
            dve.wait_ge(bias_in, 32)
            for t in range(NT):
                dve.wait_ge(ready, NQK + t + 1)
                if t >= 2:
                    dve.wait_ge(v_out[t % 2], 16 * (t // 2))
                nc.vector.tensor_tensor(values[t % 2][:, :, 0:HD], ps[(NQK + t) % 4][:].rearrange("p (h r) -> p h r", h=H),
                                        bias_v[:].rearrange("p (h r) -> p h r", h=H), ALU.add).then_inc(v_ready, 1)


def mha_heads(nc, io, ident, scratch, later):
    with ExitStack() as ctx:
        sem = lambda s: ctx.enter_context(nc.semaphore(f"ah_{s}"))
        sb = lambda n, s, dt=F32: ctx.enter_context(nc.sbuf_tensor(f"ah_{n}", s, dt))
        MAX_ROW = 3 * HD
        q_stack = [sb(f"q_stack{i}", [P, 4, S], F32R) for i in range(2)]
        k_stack = [sb(f"k_stack{i}", [P, 4, S], F32R) for i in range(2)]
        v = [sb(f"v{i}", [P, NT, 4 * 2 * HD]) for i in range(2)]
        out = sb("out", [P, 2, S])
        raw, codes = sb("raw", [P, ND, D]), sb("codes", [P, ND, D], I32)
        zeros, scales = sb("zeros", [P, ND, D]), sb("scales", [P, ND, D])
        bias_f, ones_f = sb("bias_f", [1, 2, D]), sb("ones_f", [1, P])
        half_max, row_max = sb("half_max", [P, 4, NT, 2]), sb("row_max", [P, 4 * NT])
        minus_max = sb("minus_max", [4 * NT, P], F32R)
        probs = sb("probs", [P, 4, 2 * BANK])
        ring = [ctx.enter_context(nc.psum_tensor(f"ah_ring{i}", [P, BANK], F32)) for i in range(3)]
        score_ps = [ctx.enter_context(nc.psum_tensor(f"ah_score{i}", [P, 2, BANK], F32)) for i in range(2)]
        mix_ps = ctx.enter_context(nc.psum_tensor("ah_mix", [P, BANK], F32))
        cleared = [sem(f"cleared{i}") for i in range(2)]
        ctx_out = [sem(f"ctx_out{i}") for i in range(2)]
        later_in, pool_done = sem("later_in"), sem("pool_done")
        stacks_in = [sem(f"stacks_in{i}") for i in range(2)]
        v_in = [sem(f"v_in{i}") for i in range(2)]
        max_ready, max_taken, row_max_ready, turned, minus_ready, max_row_in = (sem(s) for s in (
            "max_ready", "max_taken", "row_max_ready", "turned", "minus_ready", "max_row_in"))
        scores_ready, probs_ready, mixed, out_taken = (sem(s) for s in ("scores_ready", "probs_ready", "mixed", "out_taken"))
        block = ctx.enter_context(nc.Block())
        NUNIT = NHALF * NT
        MAX_FROM, MAX_BESIDE = 3, (1, 2, 3)
        NMAX = 4 * NT * 2
        turn_ps = ring[NMAX % 3]
        qk_rows = scratch["qk"].rearrange("part (kind h d) s -> part kind d h s", kind=2, d=HD)
        v_rows = scratch["v"].rearrange("(t p) n -> p t n", p=P)

        def looped(engine, body):
            body(0)
            with engine.Fori(1, GROUPS // 2 - 1) as r:
                body(r)
            body(GROUPS // 2 - 1)

        before = lambda r, a: (r, 0) if a == 1 else None if isinstance(r, int) and r == 0 else (r - 1, 1)
        more = lambda r, a: not (isinstance(r, int) and r == GROUPS // 2 - 1 and a == 1)

        @block.sync
        def _(sp):
            def load(r, a):
                g = 2 * r + a
                wait(sp, scores_ready, 2 * NUNIT * (g - 1))
                heads = bass.ds(4 * g, 4)
                for kind, stack, parts in ((0, q_stack[a], (0, 0, 1)), (1, k_stack[a], (0, 1, 0))):
                    for n, part in enumerate(parts):
                        sp.dma_start(stack[n * HD:(n + 1) * HD, :, :].bitcast(F32), qk_rows[part, kind, :, heads, :]).then_inc(stacks_in[a], 16)
                for n, stack in enumerate((q_stack[a], k_stack[a])):
                    sp.dma_start(stack[MAX_ROW:MAX_ROW + 1, :, :].bitcast(F32), rows_01[n:n + 1]).then_inc(stacks_in[a], 16)
                wait(sp, mixed, NUNIT * (g - 1))
                sp.dma_start(v[a][:], v_rows[:, :, bass.ds(4 * g * 2 * HD, 4 * 2 * HD)]).then_inc(v_in[a], 16)

            def put_max(r, a):
                g = 2 * r + a
                wait(sp, minus_ready, g + 1)
                sp.dma_start(q_stack[a][MAX_ROW:MAX_ROW + 1, :, :].rearrange("p h (t q) -> p (h t) q", q=P).bitcast(F32),
                             minus_max[:].bitcast(F32)).then_inc(max_row_in, 16)

            def store(r, a):
                g = 2 * r + a
                wait(sp, out_taken, NHALF * (g + 1))
                for n in range(4):
                    sp.dma_start(scratch["ctx"][bass.ds(4 * g + n, 1), :, :].rearrange("a r s -> (a r) s"),
                                 out[32 * n:32 * n + HD + 1, a, :]).then_inc(ctx_out[a], 16)

            rows_01 = scratch["rows_01"].rearrange("n (h s) -> n h s", h=4)
            for a in range(2):
                sp.wait_ge(cleared[a], 2)
                load(0, a)
            put_max(0, 0)
            for dst, src in ((raw, io["o_w"]), (codes, io["qweight"].rearrange("(k p) o -> p k o", p=P)),
                             (bias_f, io["biases"]), (ones_f, io["ones"])):
                sp.dma_start(dst[:], src).then_inc(later_in, 16)
            for dst, src in ((zeros, io["zeros"]), (scales, io["scales"])):
                grouped = src.rearrange("(k g) o -> g k o", g=P // QGROUP)
                for n in range(P // QGROUP):
                    sp.dma_start(dst[n * QGROUP:(n + 1) * QGROUP, :, :],
                                 grouped[n:n + 1, :, :].to_broadcast([QGROUP, ND, D])).then_inc(later_in, 16)

            def body(r):
                for a in range(2):
                    if more(r, a):
                        put_max(*((r, 1) if a == 0 else (r + 1, 0)))
                    if not (isinstance(r, int) and r == GROUPS // 2 - 1):
                        load(r + 1, a)
                    store(r, a)
            looped(sp, body)
            for a in range(2):
                sp.wait_ge(ctx_out[a], 64 * GROUPS // 2)

        @block.gpsimd
        def _(pool):
            n = [0]

            def then(instruction):
                n[0] += 1
                instruction.then_inc(pool_done, 1)
                pool.wait_ge(pool_done, n[0])

            for i in range(2):
                nc.gpsimd.memset(k_stack[i][:].bitcast(F32), 0.0).then_inc(cleared[i], 1)
            pool.wait_ge(later_in, 16 * (4 + 2 * P // QGROUP))
            nc.gpsimd.tensor_copy(later["ones"][:], ones_f[:])
            then(nc.gpsimd.tensor_copy(later["bias"][0][:], bias_f[:]))
            nc.gpsimd.tensor_tensor(later["bias"][1][:], bias_f[:], later["bias"][0][:].bitcast(F32), ALU.subtract)
            then(nc.gpsimd.tensor_copy(later["w_out"][0][:], raw[:]))
            then(nc.gpsimd.tensor_tensor(later["w_out"][1][:], raw[:], later["w_out"][0][:].bitcast(F32), ALU.subtract))
            then(nc.gpsimd.tensor_copy(raw[:], codes[:]))
            then(nc.gpsimd.tensor_tensor(raw[:], raw[:], zeros[:], ALU.subtract))
            then(nc.gpsimd.tensor_tensor(raw[:], raw[:], scales[:], ALU.mult))
            then(nc.gpsimd.tensor_copy(later["w_lin"][0][:], raw[:]))
            nc.gpsimd.tensor_tensor(later["w_lin"][1][:], raw[:], later["w_lin"][0][:].bitcast(F32), ALU.subtract)

        @block.tensor
        def _(pe):
            def maximum(r, a, n):
                g = 2 * r + a
                t, head, half = n // 8, n // 2 % 4, n % 2
                if n == 0:
                    wait(pe, stacks_in[a], 16 * 8 * (r + 1))
                if n == 1:
                    wait(pe, minus_ready, g)
                else:
                    wait(pe, max_taken, NMAX * g + max(n - 2, 0))
                nc.tensor.matmul(ring[n % 3][:], q_stack[a][:, head, t * P:(t + 1) * P],
                                 k_stack[a][:, head, half * BANK:(half + 1) * BANK], start=True, stop=True
                                 ).then_inc(max_ready, 1)

            def turn_max(r, a):
                g = 2 * r + a
                wait(pe, row_max_ready, g + 1)
                nc.tensor.transpose(turn_ps[0:4 * NT, 0:P], row_max[:], ident[:]).then_inc(turned, 1)

            def scores(r, a, u, pair):
                g = 2 * r + a
                half, j = divmod(u, NT)
                if u == 0 and pair == 0:
                    wait(pe, max_row_in, 16 * (g + 1))
                wait(pe, probs_ready, 2 * (NUNIT * g + u) + pair - 1)
                for e in range(2):
                    head = 2 * pair + e
                    last = nc.tensor.matmul(score_ps[pair][:, e, :], k_stack[a][:, head, j * P:(j + 1) * P],
                                            q_stack[a][:, head, half * BANK:(half + 1) * BANK], start=True, stop=True)
                last.then_inc(scores_ready, 1)

            def mix(r, a, u):
                g = 2 * r + a
                half, j = divmod(u, NT)
                if u == 0:
                    wait(pe, v_in[a], 16 * (r + 1))
                if j == 0:
                    wait(pe, out_taken, NHALF * g + half)
                wait(pe, probs_ready, 2 * (NUNIT * g + u + 1))
                for head in range(4):
                    rows = slice(32 * head, 32 * head + 32)
                    last = nc.tensor.matmul(mix_ps[rows, :], v[a][:, j, rows],
                                            probs[:, 2 * (u % 2) + head // 2, (head % 2) * BANK:(head % 2 + 1) * BANK],
                                            start=j == 0, stop=j == NT - 1)
                last.then_inc(mixed, 1)

            def slot(r, a):
                nxt = (r, 1) if a == 0 else (r + 1, 0)
                n = [0]

                def some_maxima(count):
                    for _ in range(min(count, NMAX - n[0]) if more(r, a) else 0):
                        maximum(*nxt, n[0])
                        n[0] += 1

                for u in range(NUNIT):
                    now = MAX_FROM <= u
                    scores(r, a, u, 0)
                    some_maxima(MAX_BESIDE[0] if now else 0)
                    scores(r, a, u, 1)
                    some_maxima(MAX_BESIDE[1] if now else 0)
                    if u:
                        mix(r, a, u - 1)
                    elif before(r, a):
                        mix(*before(r, a), NUNIT - 1)
                    some_maxima(MAX_BESIDE[2] if now else 0)
                    if u == NUNIT - 2 and more(r, a):
                        turn_max(*nxt)

            for n in range(NMAX):
                maximum(0, 0, n)
            turn_max(0, 0)

            def body(r):
                slot(r, 0)
                slot(r, 1)
            looped(pe, body)
            mix(GROUPS // 2 - 1, 1, NUNIT - 1)

        @block.scalar
        def _(act):
            def take_turned(r, a):
                g = 2 * r + a
                wait(act, turned, g + 1)
                wait(act, max_row_in, 16 * g)
                nc.scalar.mul(minus_max[:], turn_ps[0:4 * NT, 0:P], -1.0).then_inc(minus_ready, 1)

            def take_out(r, a, half):
                g = 2 * r + a
                wait(act, mixed, NUNIT * g + NT * (half + 1))
                wait(act, ctx_out[a], 64 * r)
                nc.scalar.copy(out[:, a, half * BANK:(half + 1) * BANK], mix_ps[:]).then_inc(out_taken, 1)

            def exp(r, a, u, pair):
                g = 2 * r + a
                wait(act, scores_ready, 2 * (NUNIT * g + u) + pair + 1)
                wait(act, mixed, NUNIT * g + u - 1)
                nc.scalar.activation(probs[:, 2 * (u % 2) + pair, :], score_ps[pair][:].rearrange("p e n -> p (e n)"),
                                     ACT.Exp, scale=MHA_SCALE).then_inc(probs_ready, 1)

            def slot(r, a):
                for u in range(NUNIT):
                    exp(r, a, u, 0)
                    exp(r, a, u, 1)
                    if u == 0 and before(r, a):
                        take_out(*before(r, a), 1)
                    if u == NT:
                        take_out(r, a, 0)
                    if u == NUNIT - 2 and more(r, a):
                        take_turned(*((r, 1) if a == 0 else (r + 1, 0)))

            take_turned(0, 0)

            def body(r):
                slot(r, 0)
                slot(r, 1)
            looped(act, body)
            take_out(GROUPS // 2 - 1, 1, 1)

        @block.vector
        def _(dve):
            nc.vector.memset(q_stack[0][:].bitcast(F32), 0.0).then_inc(cleared[0], 1)
            nc.vector.memset(q_stack[1][:].bitcast(F32), 0.0).then_inc(cleared[1], 1)

            def take_max(r, a, n):
                g = 2 * r + a
                t, head, half = n // 8, n // 2 % 4, n % 2
                wait(dve, max_ready, NMAX * g + n + 1)
                nc.vector.reduce_max(half_max[:, head, t, half:half + 1], ring[n % 3][:], AX.X).then_inc(max_taken, 1)

            def join_max(r, a):
                g = 2 * r + a
                wait(dve, turned, g)
                wait(dve, max_taken, NMAX * (g + 1))
                flat = half_max[:].rearrange("p h t two -> p (h t) two")
                nc.vector.tensor_tensor(row_max[:], flat[:, :, 0], flat[:, :, 1], ALU.max).then_inc(row_max_ready, 1)

            def group(r, a):
                for n in range(NMAX):
                    take_max(r, a, n)
                join_max(r, a)

            group(0, 0)

            def body(r):
                group(r, 1)
                if more(r, 1):
                    group(r + 1, 0)
            looped(dve, body)


def mha_ratios(nc, io, scratch, c_hi, c_lo):
    with ExitStack() as ctx:
        sem = lambda s: ctx.enter_context(nc.semaphore(f"ar_{s}"))
        sb = lambda n, s, dt=F32: ctx.enter_context(nc.sbuf_tensor(f"ar_{n}", s, dt))
        sums, inverse = sb("sums", [H, S]), sb("inverse", [H, S])
        rows_hi, rows_lo = sb("rows_hi", [H, S], F32R), sb("rows_lo", [H, S], F32R)
        select_f, select = sb("select_f", [H, ND, P]), sb("select", [H, ND, P], F32R)
        c = sb("c", [P, ND, S])
        ps = [ctx.enter_context(nc.psum_tensor(f"ar_ps{i}", [P, BANK], F32)) for i in range(4)]
        loads, c_in = sem("loads"), sem("c_in")
        ready, spreads, c_ready, c_hi_ready = (sem(s) for s in ("ready", "spreads", "c_ready", "c_hi_ready"))
        block = ctx.enter_context(nc.Block())
        pieces = [(k, slice(half * BANK, (half + 1) * BANK)) for k in range(ND) for half in range(NHALF)]

        @block.sync
        def _(sp):
            sp.dma_start(sums[:], scratch["ctx"][:, HD, :]).then_inc(loads, 16)
            sp.dma_start(select_f[:], io["select_mha"]).then_inc(loads, 16)
            heads = P // HD
            for k in range(ND):
                for h in range(heads):
                    sp.dma_start(c[h * HD:(h + 1) * HD, k, :], scratch["ctx"][heads * k + h, 0:HD, :]).then_inc(c_in, 16)

        @block.tensor
        def _(pe):
            pe.wait_ge(ready, 4)
            for n, (k, cols) in enumerate(pieces):
                wait(pe, c_ready, n - 3)
                nc.tensor.matmul(ps[n % 4][:], select[:, k, :], rows_hi[:, cols], start=True, stop=False)
                nc.tensor.matmul(ps[n % 4][:], select[:, k, :], rows_lo[:, cols], start=False, stop=True).then_inc(spreads, 1)

        @block.scalar
        def _(act):
            act.wait_ge(loads, 32)
            nc.scalar.copy(select[:], select_f[:]).then_inc(ready, 1)
            act.wait_ge(ready, 2)
            nc.scalar.copy(rows_hi[:], inverse[:]).then_inc(ready, 1)
            for n, (k, cols) in enumerate(pieces):
                act.wait_ge(c_ready, n + 1)
                nc.scalar.copy(c_hi[:, k, cols], c[:, k, cols]).then_inc(c_hi_ready, 1)

        @block.vector
        def _(dve):
            dve.wait_ge(loads, 32)
            nc.vector.reciprocal(inverse[:], sums[:]).then_inc(ready, 1)
            dve.wait_ge(ready, 3)
            nc.vector.tensor_tensor(rows_lo[:], inverse[:], rows_hi[:].bitcast(F32), ALU.subtract).then_inc(ready, 1)
            dve.wait_ge(c_in, 16 * H)

            def lower(n):
                k, cols = pieces[n]
                dve.wait_ge(c_hi_ready, n + 1)
                nc.vector.tensor_tensor(c_lo[:, k, cols], c[:, k, cols], c_hi[:, k, cols].bitcast(F32), ALU.subtract)

            for n, (k, cols) in enumerate(pieces):
                dve.wait_ge(spreads, n + 1)
                nc.vector.tensor_tensor(c[:, k, cols], c[:, k, cols], ps[n % 4][:], ALU.mult).then_inc(c_ready, 1)
                if n:
                    lower(n - 1)
            lower(len(pieces) - 1)


class Loads:

    def __init__(self, nc, semaphore):
        self.nc, self.semaphore, self.count = nc, semaphore, 0

    def __call__(self, *pairs):
        with self.nc.Block() as block:
            @block.sync
            def _(sp):
                for dst, src in pairs:
                    sp.dma_start(dst, src).then_inc(self.semaphore, 16)
                    self.count += 16
                sp.wait_ge(self.semaphore, self.count)


def two_layers(nc, io, out_dram, upto=4):
    with ExitStack() as ctx:
        sb = lambda n, s, dt=F32: ctx.enter_context(nc.sbuf_tensor(n, s, dt))
        ident = sb("ident", [P, P])
        x_dram_out = nc.dram_tensor("x_scratch", (S, D), F32, kind="Internal").ap()
        hT_dram = nc.dram_tensor("hT_scratch", (P, ND, S), F32, kind="Internal").ap()
        scratch = {"qk": nc.dram_tensor("qk_scratch", (2, 2 * D, S), F32, kind="Internal").ap(),
                   "rows_01": nc.dram_tensor("rows_01_scratch", (2, 4 * S), F32, kind="Internal").ap(),
                   "ctx": nc.dram_tensor("ctx_scratch", (H, HD + 1, S), F32, kind="Internal").ap(),
                   "v": nc.dram_tensor("v_scratch", (S, H * 2 * HD), F32, kind="Internal").ap()}
        load = Loads(nc, ctx.enter_context(nc.semaphore("loads")))
        load((ident[:], io["ident"]), (scratch["rows_01"], io["rows_01"]))

        with ExitStack() as layer:
            sb = lambda n, s, dt=F32: layer.enter_context(nc.sbuf_tensor(n, s, dt))
            peT = sb("peT", [P, PAIRS, S])
            w_out = sb("w_out", [P, PAIRS, D])
            sums = sb("sums", [P, H, NT])
            with ExitStack() as part:
                sb = lambda n, s, dt=F32: part.enter_context(nc.sbuf_tensor(n, s, dt))
                m = {"peT": peT, "w_out": w_out, "sums": sums,
                     "q1_hi": sb("q1_hi", [P, S], F32R), "q1_lo": sb("q1_lo", [P, S], F32R), "q2": sb("q2", [P, S], F32R),
                     "kt_hi": [sb(f"kt_hi{e}", [P, S], F32R) for e in range(2)],
                     "kt_lo": [sb(f"kt_lo{e}", [P, S], F32R) for e in range(2)],
                     "values": sb("values", [P, NT, 2 * CR], F32R), "qw1": sb("qw1", [P, 1]), "qw2": sb("qw2", [QR - P, 1]),
                     "kw": sb("kw", [P, 2]), "kw2": sb("kw2", [P, 1]), "mask": sb("mask", [P, P])}
                hT = w_out[:, 0:ND * S // D, :].rearrange("p a n -> p (a n)").rearrange("p (k s) -> p k s", k=ND)
                with nc.sbuf_tensor("x_first", [P, NT, D], F32) as x:
                    norm_block(nc, "n0", x, hT, ident, x_dram=io["x"])
                mla_inputs(nc, io, hT, ident, m)
                mla_heads(nc, io, ident, m)
            mla_output(nc, io, ident, peT, w_out, sums, x_dram_out, hT_dram, out_dram if upto == 1 else None)
            if upto == 1:
                return

        x = ctx.enter_context(nc.sbuf_tensor("x", [P, NT, D], F32))
        with ExitStack() as layer:
            sb = lambda n, s, dt=F32: layer.enter_context(nc.sbuf_tensor(n, s, dt))
            d = sb("d", [P, NI, S])
            down_hi, down_lo = sb("down_hi", [P, NI, D], F32R), sb("down_lo", [P, NI, D], F32R)
            ffn_inner(nc, io, hT_dram, x, d, down_hi, down_lo)

            h = (sb("h_hi", [P, ND, S], F32R), sb("h_lo", [P, ND, S], F32R))
            d_hi, d_lo = sb("d_hi", [P, 2, NI, P], F32R), sb("d_lo", [P, 2, NI, P], F32R)
            d_hi_ready, d_lo_ready, used = (layer.enter_context(nc.semaphore(f"fp_{n}")) for n in ("d_hi", "d_lo", "used"))

            def scalar_work(act, t):
                wait(act, used, t - 1)
                nc.scalar.copy(d_hi[:, t % 2, :, :], d[:, :, t * P:(t + 1) * P]).then_inc(d_hi_ready, 1)

            def vector_work(dve, t):
                dve.wait_ge(d_hi_ready, t + 1)
                nc.vector.tensor_tensor(d_lo[:, t % 2, :, :], d[:, :, t * P:(t + 1) * P],
                                        d_hi[:, t % 2, :, :].bitcast(F32), ALU.subtract).then_inc(d_lo_ready, 1)

            def project(pe, t, out):
                pe.wait_ge(d_lo_ready, t + 1)
                products = [(a, w, i) for i in range(NI) for a, w in ((d_hi, down_hi), (d_hi, down_lo), (d_lo, down_hi))]
                for n, (a, w, i) in enumerate(products):
                    last = nc.tensor.matmul(out[:], a[:, t % 2, i, :], w[:, i, :], start=n == 0, stop=n == len(products) - 1)
                return last
            works = dict(x_dram=x_dram_out, project=project, scalar_work=scalar_work, vector_work=vector_work, projected=used)
            if upto == 2:
                norm_block(nc, "n2", x, None, ident, out_dram=out_dram, **works)
                return
            norm_block(nc, "n2", x, h, ident, **works)
            ring = lambda part: part[:].rearrange("p a k n -> p (a k n)")[:, 0:3 * BANK].rearrange("p (a n) -> p a n", n=BANK)
            mha_inputs(nc, io, h, d, down_hi, down_lo, ring(d_hi), ring(d_lo), scratch)

        with ExitStack() as layer:
            sb = lambda n, s, dt=F32: layer.enter_context(nc.sbuf_tensor(n, s, dt))
            parts = lambda n, shape: [sb(f"{n}_{part}", shape, F32R) for part in ("hi", "lo")]
            later = {"w_out": parts("w_out", [P, ND, D]), "w_lin": parts("w_lin", [P, ND, D]),
                     "bias": parts("bias", [1, 2, D]), "ones": sb("ones", [1, P], F32R)}
            mha_heads(nc, io, ident, scratch, later)
            c = parts("c", [P, ND, S])
            mha_ratios(nc, io, scratch, *c)

            def linear(source, weights, bias):
                def project(pe, t, out):
                    nc.tensor.matmul(out[:], later["ones"][:], later["bias"][0][:, bias, :], start=True, stop=False)
                    nc.tensor.matmul(out[:], later["ones"][:], later["bias"][1][:, bias, :], start=False, stop=False)
                    for k in range(ND):
                        for a, b in ((0, 0), (0, 1), (1, 0)):
                            last = nc.tensor.matmul(out[:], source[a][:, k, t * P:(t + 1) * P], weights[b][:, k, :],
                                                    start=False, stop=(k, a) == (ND - 1, 1))
                    return last
                return project

            if upto == 3:
                norm_block(nc, "n3", x, None, ident, project=linear(c, later["w_out"], 0), out_dram=out_dram)
                return
            h = tuple(parts("h3", [P, ND, S]))
            norm_block(nc, "n3", x, h, ident, project=linear(c, later["w_out"], 0))
            norm_block(nc, "n4", x, None, ident, project=linear(h, later["w_lin"], 1), out_dram=out_dram)


def layouts(i):
    import numpy as np
    c = np.ascontiguousarray
    a = {k: np.asarray(v) for k, v in i.items()}
    wq = a["L0_attn_Wq_b"].reshape(QR, H, NOPE + ROPE)
    wkv = a["L0_attn_Wkv_b"].reshape(CR, H, NOPE + VD)
    wo = a["L0_attn_Wo"].reshape(H, VD, D)
    by_pair = lambda m: m.reshape(PAIRS, 2, P, -1).transpose(0, 2, 1, 3).reshape(PAIRS, P, -1)
    w_nope = wq[:, :, :NOPE].transpose(1, 2, 0)
    w_nope = np.concatenate([w_nope, w_nope[:, :, P:]], 2)
    packed = [by_pair(m) for m in (w_nope, wkv[:, :, :NOPE].transpose(1, 2, 0),
                                   wkv[:, :, NOPE:].transpose(1, 2, 0), wo)]
    qw, kw = a["L0_attn_q_a_ln_w"], a["L0_attn_kv_a_ln_w"]
    one = np.ones((CR,), np.float32)
    w_a = np.concatenate([a["L0_attn_Wq_a"], a["L0_attn_Wkv_a"]], 1)
    angle_f = np.float32(1.0) / np.float32(10000.0) ** (np.arange(0, ROPE, 2, dtype=np.float32) / np.float32(ROPE))
    angle = np.outer(np.arange(S, dtype=np.float32), angle_f.astype(np.float32)).astype(np.float32)
    cos = np.repeat(np.cos(angle), 2, 1).astype(np.float32)
    sin = np.repeat(np.sin(angle), 2, 1).astype(np.float32) * np.tile(np.array([-1, 1], np.float32), ROPE // 2)
    by_tile = lambda m: c(m.reshape(-1, P, m.shape[1]).transpose(1, 0, 2))
    inner = lambda k: a[k].T.reshape(ND, P, NI, P).transpose(2, 1, 0, 3).reshape(NI, P, D)
    below = np.arange(P)[:, None] < np.arange(P)[None, :]
    mask = np.where(below, np.float32(-1e30), np.float32(0))
    rows = np.arange(P)
    spread_mla = np.zeros((H, PAIRS, P), np.float32)
    for n in range(PAIRS):
        spread_mla[2 * n + rows // CR, n, rows] = 1
    select_mha = np.zeros((H, ND, P), np.float32)
    for k in range(ND):
        select_mha[k * (P // HD) + rows // HD, k, rows] = 1
    qkv_b = a["L1_attn_attn_qkvb"]
    return {
        "x": c(a["L0_attn_hidden_states"].reshape(S, D)), "ident": np.eye(P, dtype=np.float32),
        "w_a": by_tile(w_a), "cos": by_tile(cos), "sin": by_tile(sin),
        "qw1": c(qw[:P, None]), "qw2": c(qw[P:, None]), "kw2": c(np.concatenate([kw, kw])[:, None]),
        "kw": c(np.stack([np.concatenate([kw, one]), np.concatenate([one, kw])], 1)),
        "w_pe": c(wq[:, :, NOPE:].reshape(QR, H * ROPE)),
        "w_pairs": c(np.concatenate(packed, 2).reshape(PAIRS * P, PACK)),
        "mask": mask, "spread_mla": spread_mla, "select_mha": select_mha,
        "w_inner": c(np.concatenate([inner("L0_ffn_gate_w"), inner("L0_ffn_up_w"),
                                     a["L0_ffn_down_w"].T.reshape(NI, P, D)], 2).reshape(NI * P, 3 * D)),
        "sides": c(np.concatenate([a["L0_ffn_gate_su"].T, a["L0_ffn_up_su"].T, a["L0_ffn_down_su"].T,
                                   a["L0_ffn_gate_sv"], a["L0_ffn_up_sv"], a["L0_ffn_down_sv"]], 1)),
        "qkv_w": by_tile(a["L1_attn_attn_qkvw"]), "bias_qk": c(qkv_b[:2 * D].reshape(2 * ND, P).T),
        "bias_v": c(np.broadcast_to(qkv_b[None, 2 * D:], (P, D))), "o_w": by_tile(a["L1_attn_attn_ow"]),
        "rows_01": np.stack([np.zeros(4 * S, np.float32), np.ones(4 * S, np.float32)]),
        "qweight": c(a["L1_ffn_qweight"].T),
        "zeros": c(a["L1_ffn_zeros"].reshape(D, -1).T), "scales": c(a["L1_ffn_scales"].reshape(D, -1).T),
        "biases": c(np.stack([a["L1_attn_attn_ob"], a["L1_ffn_bias"]])[None]), "ones": np.ones((1, P), np.float32),
    }


def kernel(**inputs):
    import concourse.bacc as bacc
    import numpy as np
    from concourse.bass_utils import run_bass_kernel_spmd

    nc = bacc.Bacc("TRN2", target_bir_lowering=False, num_devices=1)
    arrays = {f"in_{k}": v for k, v in layouts(inputs).items()}
    io = {k[3:]: nc.dram_tensor(k, v.shape, mybir.dt.from_np(v.dtype), kind="ExternalInput").ap() for k, v in arrays.items()}
    out = nc.dram_tensor("out", (S, D), F32, kind="ExternalOutput").ap()
    two_layers(nc, io, out)
    r = run_bass_kernel_spmd(nc, [arrays], core_ids=[0])
    return r.results[0]["out"].reshape(1, S, D)
```
